# Optimizing a Trainium2 kernel written in Bass

```python
import numpy as np
import jax
import jax.numpy as jnp

def _softmax(x, axis=-1):
    return jax.nn.softmax(x, axis=axis)

def _gelu(x):
    return jax.nn.gelu(x, approximate=True)

def _silu(x):
    return jax.nn.silu(x)

def _sigmoid(x):
    return jax.nn.sigmoid(x)

def _layernorm(x, axis=-1, eps=1e-05):
    m = jnp.mean(x, axis=axis, keepdims=True)
    v = jnp.var(x, axis=axis, keepdims=True)
    return (x - m) / jnp.sqrt(v + eps)

def _scatter_add(tgt, idx, src, axis=0):
    return tgt.at[idx].add(src)

def _segment_sum(src, seg, n):
    return jax.ops.segment_sum(src, seg, n)
kernel_name = 'mk_flamingo_gated_d2_seqx_r4_e92132'

def setup_inputs(seed: int=0):
    np.random.seed(seed)
    _w = jnp.asarray

    def _rec_inputs():
        import jax
        import jax.numpy as jnp
        _rk = jax.random.key(seed)
        x = -0.0002928 + 1 * jax.random.normal(jax.random.fold_in(_rk, 1), (8, 256, 256), jnp.float32)
        _lenS = 256 - jax.random.randint(jax.random.fold_in(_rk, 7), (8,), 0, max(1, 256 // 4) + 1, jnp.int32)
        _lenS2 = 256 - jax.random.randint(jax.random.fold_in(_rk, 8), (8,), 0, max(1, 256 // 4) + 1, jnp.int32)
        _ctx_1024P = jax.random.normal(jax.random.fold_in(_rk, 11), (8, 16, 256), jnp.float32)
        _ctx_1024c = jax.random.dirichlet(jax.random.fold_in(_rk, 511), 0.3 * jnp.ones((16,), jnp.float32), (8, 256))
        _ctx_1024t = jnp.einsum('bsk,bkd->bsd', _ctx_1024c, _ctx_1024P)
        _ctx_1024t = _ctx_1024t * jax.lax.rsqrt(jnp.mean(jnp.square(_ctx_1024t)) + 1e-12) * 0.953939
        ctx_1024 = -1.39393e-06 + 0.999914 * (_ctx_1024t + 0.3 * jax.random.normal(jax.random.fold_in(_rk, 611), (8, 256, 256), jnp.float32))
        _validS = jnp.arange(256)[None, :] < _lenS[:, None]
        _validS2 = jnp.arange(256)[None, :] < _lenS2[:, None]
        _causal = jnp.tril(jnp.ones((256, 256), dtype=bool))
        mask_BxS2_bk0 = jnp.logical_not(jnp.broadcast_to(_validS2[:, :], (8, 256)))
        _g = jax.random.normal(jax.random.fold_in(_rk, 9001), (2, 2), jnp.float32)
        _g = jnp.sign(_g) * jnp.maximum(jnp.abs(_g), 1.0) + (_g == 0) * 1.0
        g_xattn = _g[0]
        g_ffn = _g[1]
        return (x, ctx_1024, mask_BxS2_bk0, g_xattn, g_ffn)
    x, ctx_1024, mask_BxS2_bk0, g_xattn, g_ffn = _rec_inputs()

    def _L0_xattn_setup():
        import jax, jax.numpy as jnp
        import numpy as np
        N_HEADS = 16
        EMBED = 256
        HEAD_DIM = EMBED // N_HEADS
        key = jax.random.key(seed)
        ks = jax.random.split(key, 11)
        B, S, E = (2, 512, EMBED)
        s = 1.0 / np.sqrt(E)
        return {'q': jax.random.normal(ks[0], (B, S, E), jnp.float32), 'k': jax.random.normal(ks[1], (B, S, E), jnp.float32), 'v': jax.random.normal(ks[2], (B, S, E), jnp.float32), 'Wq': jax.random.normal(ks[3], (E, E), jnp.float32) * s, 'bq': jax.random.normal(ks[4], (E,), jnp.float32) * s, 'Wk': jax.random.normal(ks[5], (E, E), jnp.float32) * s, 'bk': jax.random.normal(ks[6], (E,), jnp.float32) * s, 'Wv': jax.random.normal(ks[7], (E, E), jnp.float32) * s, 'bv': jax.random.normal(ks[8], (E,), jnp.float32) * s, 'Wp': jax.random.normal(ks[9], (E, E), jnp.float32) * s, 'bp': jax.random.normal(ks[10], (E,), jnp.float32) * s}
    _L0_xattn_all = _L0_xattn_setup()
    _L0_xattn_in = {k: v for k, v in _L0_xattn_all.items() if k in ('Wq', 'bq', 'Wk', 'bk', 'Wv', 'bv', 'Wp', 'bp')}
    del _L0_xattn_all

    def _L0_ffn_setup():
        import jax, jax.numpy as jnp
        import numpy as np
        B, T = (2, 512)
        D_MODEL, D_HIDDEN = (256, 512)
        N_EXPERTS, TOP_K = (8, 2)
        N_TOKENS = B * T
        CAPACITY = 2 * N_TOKENS * TOP_K // N_EXPERTS
        key = jax.random.key(seed)
        k_x, k_rw, k_w, k_v, k_o = jax.random.split(key, 5)
        x = jax.random.normal(k_x, (B, T, D_MODEL), jnp.float32)
        router_w = jax.random.normal(k_rw, (N_EXPERTS, D_MODEL), jnp.float32) * D_MODEL ** (-0.5)
        router_b = jnp.zeros((N_EXPERTS,), jnp.float32)
        W = jax.random.normal(k_w, (N_EXPERTS, D_MODEL, D_HIDDEN), jnp.float32) * D_MODEL ** (-0.5)
        V = jax.random.normal(k_v, (N_EXPERTS, D_MODEL, D_HIDDEN), jnp.float32) * D_MODEL ** (-0.5)
        W_out = jax.random.normal(k_o, (N_EXPERTS, D_HIDDEN, D_MODEL), jnp.float32) * D_HIDDEN ** (-0.5)
        return {'x': x, 'router_w': router_w, 'router_b': router_b, 'W': W, 'V': V, 'W_out': W_out}
    _L0_ffn_all = _L0_ffn_setup()
    _L0_ffn_in = {k: v for k, v in _L0_ffn_all.items() if k in ('router_w', 'router_b', 'W', 'V', 'W_out')}
    del _L0_ffn_all

    def _L1_xattn_setup():
        import jax, jax.numpy as jnp
        import numpy as np
        D_MODEL = 256
        N_HEAD = 16
        D_H = D_MODEL // N_HEAD
        key = jax.random.key(seed)
        ks = jax.random.split(key, 12)
        B, LQ, LK = (4, 256, 512)
        s = 1.0 / np.sqrt(D_MODEL)
        inp = {'q_input': jax.random.normal(ks[0], (B, LQ, D_MODEL), jnp.float32), 'kv_input': jax.random.normal(ks[1], (B, LK, D_MODEL), jnp.float32), 'key_padding_mask': jax.random.randint(ks[2], (B, LK), 0, 2) > 0, 'W_Q': jax.random.normal(ks[3], (D_MODEL, D_MODEL), jnp.float32) * s, 'b_Q': jnp.zeros((D_MODEL,), jnp.float32), 'W_K': jax.random.normal(ks[4], (D_MODEL, D_MODEL), jnp.float32) * s, 'b_K': jnp.zeros((D_MODEL,), jnp.float32), 'W_V': jax.random.normal(ks[5], (D_MODEL, D_MODEL), jnp.float32) * s, 'b_V': jnp.zeros((D_MODEL,), jnp.float32), 'W_O': jax.random.normal(ks[6], (D_MODEL, D_MODEL), jnp.float32) * s, 'b_O': jnp.zeros((D_MODEL,), jnp.float32)}
        return inp
    _L1_xattn_all = _L1_xattn_setup()
    _L1_xattn_in = {k: v for k, v in _L1_xattn_all.items() if k in ('W_Q', 'b_Q', 'W_K', 'b_K', 'W_V', 'b_V', 'W_O', 'b_O')}
    del _L1_xattn_all

    def _L1_ffn_setup():
        import jax, jax.numpy as jnp
        import numpy as np
        E = 16
        F_C = 2.0
        D = 256
        I = 4 * D
        IS = 2 * D
        B, S = (4, 256)
        key = jax.random.key(seed)
        ks = jax.random.split(key, 8)
        w = 0.02
        return {'hidden_states': jax.random.normal(ks[0], (B, S, D), dtype=jnp.float32), 'gate_w': jax.random.normal(ks[1], (E, D), dtype=jnp.float32) * w, 'Wg': jax.random.normal(ks[2], (E, I, D), dtype=jnp.float32) * w, 'Wu': jax.random.normal(ks[3], (E, I, D), dtype=jnp.float32) * w, 'Wd': jax.random.normal(ks[4], (E, D, I), dtype=jnp.float32) * w, 'Sg': jax.random.normal(ks[5], (IS, D), dtype=jnp.float32) * w, 'Su': jax.random.normal(ks[6], (IS, D), dtype=jnp.float32) * w, 'Sd': jax.random.normal(ks[7], (D, IS), dtype=jnp.float32) * w}
    _L1_ffn_all = _L1_ffn_setup()
    _L1_ffn_in = {k: v for k, v in _L1_ffn_all.items() if k in ('gate_w', 'Wg', 'Wu', 'Wd', 'Sg', 'Su', 'Sd')}
    del _L1_ffn_all
    return {'x': x, 'ctx_1024': ctx_1024, 'mask_BxS2_bk0': mask_BxS2_bk0, 'g_xattn': g_xattn, 'g_ffn': g_ffn, 'L0_xattn_Wq': _L0_xattn_in['Wq'], 'L0_xattn_bq': _L0_xattn_in['bq'], 'L0_xattn_Wk': _L0_xattn_in['Wk'], 'L0_xattn_bk': _L0_xattn_in['bk'], 'L0_xattn_Wv': _L0_xattn_in['Wv'], 'L0_xattn_bv': _L0_xattn_in['bv'], 'L0_xattn_Wp': _L0_xattn_in['Wp'], 'L0_xattn_bp': _L0_xattn_in['bp'], 'L0_ffn_router_w': _L0_ffn_in['router_w'], 'L0_ffn_router_b': _L0_ffn_in['router_b'], 'L0_ffn_W': _L0_ffn_in['W'], 'L0_ffn_V': _L0_ffn_in['V'], 'L0_ffn_W_out': _L0_ffn_in['W_out'], 'L1_xattn_W_Q': _L1_xattn_in['W_Q'], 'L1_xattn_b_Q': _L1_xattn_in['b_Q'], 'L1_xattn_W_K': _L1_xattn_in['W_K'], 'L1_xattn_b_K': _L1_xattn_in['b_K'], 'L1_xattn_W_V': _L1_xattn_in['W_V'], 'L1_xattn_b_V': _L1_xattn_in['b_V'], 'L1_xattn_W_O': _L1_xattn_in['W_O'], 'L1_xattn_b_O': _L1_xattn_in['b_O'], 'L1_ffn_gate_w': _L1_ffn_in['gate_w'], 'L1_ffn_Wg': _L1_ffn_in['Wg'], 'L1_ffn_Wu': _L1_ffn_in['Wu'], 'L1_ffn_Wd': _L1_ffn_in['Wd'], 'L1_ffn_Sg': _L1_ffn_in['Sg'], 'L1_ffn_Su': _L1_ffn_in['Su'], 'L1_ffn_Sd': _L1_ffn_in['Sd']}

def reference(x, ctx_1024, mask_BxS2_bk0, g_xattn, g_ffn, L0_xattn_Wq, L0_xattn_bq, L0_xattn_Wk, L0_xattn_bk, L0_xattn_Wv, L0_xattn_bv, L0_xattn_Wp, L0_xattn_bp, L0_ffn_router_w, L0_ffn_router_b, L0_ffn_W, L0_ffn_V, L0_ffn_W_out, L1_xattn_W_Q, L1_xattn_b_Q, L1_xattn_W_K, L1_xattn_b_K, L1_xattn_W_V, L1_xattn_b_V, L1_xattn_W_O, L1_xattn_b_O, L1_ffn_gate_w, L1_ffn_Wg, L1_ffn_Wu, L1_ffn_Wd, L1_ffn_Sg, L1_ffn_Su, L1_ffn_Sd):
    import jax
    import jax.numpy as jnp

    def _L0_xattn_ref(q, k, v, Wq, bq, Wk, bk, Wv, bv, Wp, bp):
        import jax, jax.numpy as jnp
        import numpy as np
        N_HEADS = 16
        EMBED = 256
        HEAD_DIM = EMBED // N_HEADS
        B, Sq, E = q.shape
        Skv = k.shape[1]
        qh = q @ Wq.T + bq
        kh = k @ Wk.T + bk
        vh = v @ Wv.T + bv
        qh = qh.reshape(B, N_HEADS, Sq, HEAD_DIM)
        kh = kh.reshape(B, N_HEADS, Skv, HEAD_DIM)
        vh = vh.reshape(B, N_HEADS, Skv, HEAD_DIM)
        scale = 1.0 / jnp.sqrt(jnp.float32(HEAD_DIM))
        scores = jnp.einsum('bhqd,bhkd->bhqk', qh, kh) * scale
        causal = jnp.triu(jnp.ones((Sq, Sq), bool), k=1)
        scores = jnp.where(causal, -jnp.inf, scores)
        attn = jax.nn.softmax(scores, axis=-1)
        out = jnp.einsum('bhqk,bhkd->bhqd', attn, vh)
        out = out.reshape(B, Sq, E)
        return out @ Wp.T + bp

    def _L0_ffn_ref(x, router_w, router_b, W, V, W_out):
        import jax, jax.numpy as jnp
        import numpy as np
        B, T = (2, 512)
        D_MODEL, D_HIDDEN = (256, 512)
        N_EXPERTS, TOP_K = (8, 2)
        N_TOKENS = B * T
        CAPACITY = 2 * N_TOKENS * TOP_K // N_EXPERTS
        Bq, Tq, D = x.shape
        N = Bq * Tq
        x_flat = x.reshape(N, D)
        router_logits = x_flat @ router_w.T + router_b
        top_vals, top_ids = jax.lax.top_k(router_logits, TOP_K)
        top_probs = jax.nn.softmax(top_vals, axis=-1)
        x_pad = jnp.concatenate([x_flat, jnp.zeros((1, D), x_flat.dtype)], axis=0)
        probs_pad = jnp.concatenate([top_probs, jnp.zeros((1, TOP_K), top_probs.dtype)], axis=0)
        out = jnp.zeros((N + 1, D), x_flat.dtype)
        for e in range(N_EXPERTS):
            tok, slot = jnp.nonzero(top_ids == e, size=CAPACITY, fill_value=(N, 0))
            w = probs_pad[tok, slot][:, None]
            xin = x_pad[tok]
            a = xin @ W[e]
            b = xin @ V[e]
            y = a * (b * jax.nn.sigmoid(b)) @ W_out[e]
            out = out.at[tok].add(y * w)
        return out[:N].reshape(Bq, Tq, D)

    def _L1_xattn_ref(q_input, kv_input, key_padding_mask, W_Q, b_Q, W_K, b_K, W_V, b_V, W_O, b_O):
        import jax, jax.numpy as jnp
        import numpy as np
        D_MODEL = 256
        N_HEAD = 16
        D_H = D_MODEL // N_HEAD
        B, LQ, _ = q_input.shape
        LK = kv_input.shape[1]
        q = q_input @ W_Q + b_Q
        k = kv_input @ W_K + b_K
        v = kv_input @ W_V + b_V
        q = q.reshape(B, LQ, N_HEAD, D_H).transpose(0, 2, 1, 3)
        k = k.reshape(B, LK, N_HEAD, D_H).transpose(0, 2, 1, 3)
        v = v.reshape(B, LK, N_HEAD, D_H).transpose(0, 2, 1, 3)
        sim = jnp.einsum('bhqd,bhkd->bhqk', q, k) / jnp.sqrt(jnp.float32(D_H))
        neg_inf = jnp.finfo(sim.dtype).min
        mask = key_padding_mask[:, None, None, :]
        sim = jnp.where(mask, neg_inf, sim)
        attn = jax.nn.softmax(sim, axis=-1)
        out = jnp.einsum('bhqk,bhkd->bhqd', attn, v)
        out = out.transpose(0, 2, 1, 3).reshape(B, LQ, D_MODEL)
        return out @ W_O + b_O

    def _L1_ffn_ref(hidden_states, gate_w, Wg, Wu, Wd, Sg, Su, Sd):
        import jax, jax.numpy as jnp
        import numpy as np
        E = 16
        F_C = 2.0
        D = 256
        I = 4 * D
        IS = 2 * D
        B, S = (4, 256)
        b, s, d = hidden_states.shape
        T = b * s
        C = int(T * F_C / E)
        flat_x = hidden_states.reshape(T, d)
        logits = flat_x @ gate_w.T
        scores = jax.nn.softmax(logits, axis=-1).T
        topk_weight, topk_idx = jax.lax.top_k(scores, C)
        xg = flat_x[topk_idx]
        g = jnp.einsum('ecd,eid->eci', xg, Wg)
        u = jnp.einsum('ecd,eid->eci', xg, Wu)
        h = jax.nn.gelu(g, approximate=False) * u
        eo = jnp.einsum('eci,edi->ecd', h, Wd)
        eo = eo * topk_weight[..., None]
        flat_out = jnp.zeros_like(flat_x).at[topk_idx.reshape(-1)].add(eo.reshape(-1, d))
        out = flat_out.reshape(b, s, d)
        sg = hidden_states @ Sg.T
        su = hidden_states @ Su.T
        shared = jax.nn.gelu(sg, approximate=False) * su @ Sd.T
        return out + shared
    x = x + jnp.tanh(g_xattn[0]) * _L0_xattn_ref(_layernorm(x, axis=-1), ctx_1024, ctx_1024, L0_xattn_Wq, L0_xattn_bq, L0_xattn_Wk, L0_xattn_bk, L0_xattn_Wv, L0_xattn_bv, L0_xattn_Wp, L0_xattn_bp)
    x = x + jnp.tanh(g_ffn[0]) * _L0_ffn_ref(_layernorm(x, axis=-1), L0_ffn_router_w, L0_ffn_router_b, L0_ffn_W, L0_ffn_V, L0_ffn_W_out)
    x = x + jnp.tanh(g_xattn[1]) * _L1_xattn_ref(_layernorm(x, axis=-1), ctx_1024, mask_BxS2_bk0, L1_xattn_W_Q, L1_xattn_b_Q, L1_xattn_W_K, L1_xattn_b_K, L1_xattn_W_V, L1_xattn_b_V, L1_xattn_W_O, L1_xattn_b_O)
    x = x + jnp.tanh(g_ffn[1]) * _L1_ffn_ref(_layernorm(x, axis=-1), L1_ffn_gate_w, L1_ffn_Wg, L1_ffn_Wu, L1_ffn_Wd, L1_ffn_Sg, L1_ffn_Su, L1_ffn_Sd)
    return x

_drawn_inputs = setup_inputs


def setup_inputs(seed=0):
    import zlib

    import numpy as np

    out = dict(_drawn_inputs(seed))
    spreads = {'g_ffn': (-1.0, 0.6),
     'L0_ffn_router_b': (0.0, 0.1),
     'L1_xattn_b_Q': (0.0, 0.448),
     'L1_xattn_b_K': (0.0, 0.8),
     'L1_xattn_b_V': (0.0, 0.1),
     'L1_xattn_b_O': (0.0, 0.1)}
    factors = {'L0_xattn_bq': 2.785,
     'L1_ffn_gate_w': 8.0,
     'L1_ffn_Wg': 8.0,
     'L1_ffn_Wu': 8.0,
     'L1_ffn_Wd': 8.0,
     'L1_ffn_Sg': 3.213,
     'L1_ffn_Su': 3.224,
     'L1_ffn_Sd': 3.17}
    for name, (base, spread) in spreads.items():
        noise = np.random.default_rng([zlib.crc32(name.encode()), seed]).standard_normal(out[name].shape)
        drawn = base * np.exp(spread * noise) if base else spread * noise
        out[name] = jnp.asarray(drawn.astype(out[name].dtype))
    for name, factor in factors.items():
        out[name] = (out[name] * factor).astype(out[name].dtype)
    return out
```

```python
from contextlib import ExitStack

import concourse.bass as bass
import concourse.mybir as mybir

ACT = mybir.ActivationFunctionType
ALU = mybir.AluOpType
AX = mybir.AxisListType
F32 = mybir.dt.float32
F32R = mybir.dt.float32r
BF16 = mybir.dt.bfloat16
U8 = mybir.dt.uint8
I32 = mybir.dt.int32
U32 = mybir.dt.uint32

P = 128
D = 256
KT = D // P
B = 8
S = 256
ST = S // P
N = B * S
NT = N // P
H = 16
HD = D // H
HB = H // 2
NEG = -float(2 ** 100)
EPS = 1e-5
SLOTS = 4096
SLOT_TILES = SLOTS // P
SPARE = 512


def wait(eng, sem, value):
    if isinstance(value, int) and value <= 0:
        return
    eng.wait_ge(sem, value)


class Steps:

    def __init__(self, eng, sem):
        self.eng, self.sem, self.base, self.n = eng, sem, 0, 0

    def at(self, base):
        self.base, self.n = base, 0

    def mark(self, instruction):
        instruction.then_inc(self.sem, 1)
        self.n += 1

    def wait(self):
        self.eng.wait_ge(self.sem, self.base + self.n)


class Semaphores(dict):

    def __init__(self, take):
        super().__init__()
        self.take = take

    def __missing__(self, name):
        self[name] = self.take(name)
        return self[name]


def split_matmul(pe, out, lhs, rhs, first=True, last=True):
    (lh, ll), (rh, rl) = lhs, rhs
    pe.matmul(out, lh, rh, start=first, stop=False)
    pe.matmul(out, lh, rl, start=False, stop=False)
    return pe.matmul(out, ll, rh, start=False, stop=last)


def bcast(row, n):
    return row.to_broadcast([n, row.shape[-1]])


def constants(nc, c):
    with nc.Block() as block:

        @block.sync
        def _(sp):
            sp.dma_start(c.gates[:, 0:2], bcast(c.g_xattn, P)).then_inc(c.gates_loaded, 16)
            sp.dma_start(c.gates[:, 2:4], bcast(c.g_ffn, P)).then_inc(c.gates_loaded, 16)
            sp.wait_ge(c.zeros_set, 1)
            for x in c.with_spare:
                sp.dma_start(x[N:N + SPARE, :].rearrange("(t p) f -> p t f", p=P),
                             c.zeros[:].rearrange("p (t f) -> p t f", f=D)).then_inc(c.spare_zeroed, 16)
            sp.wait_ge(c.spare_zeroed, 16 * len(c.with_spare))

        @block.scalar
        def _(act):
            act.wait_ge(c.gates_loaded, 32)
            act.activation(c.tgate[:], c.gates[:], ACT.Tanh).then_inc(c.gates_ready, 1)
            act.wait_ge(c.gates_ready, 1)

        @block.gpsimd
        def _(pool):
            pool.memset(c.zeros[:], 0.0).then_inc(c.zeros_set, 1)
            pool.memset(c.ident[:], 0.0).then_inc(c.const_set, 1)
            pool.memset(c.mask_q[:], 0.0).then_inc(c.const_set, 1)
            pool.memset(c.mask_k[:], 0.0).then_inc(c.const_set, 1)
            pool.memset(c.minus_half[:], -0.5).then_inc(c.const_set, 1)
            pool.wait_ge(c.const_set, 4)
            pool.affine_select(out=c.ident[:], in_=c.ident[:], compare_op=ALU.not_equal, fill=1.0,
                               base=0, pattern=[[-1, P]], channel_multiplier=1).then_inc(c.const_set, 1)
            pool.affine_select(out=c.mask_q[:], in_=c.mask_q[:], compare_op=ALU.is_ge, fill=NEG,
                               base=0, pattern=[[-1, P]], channel_multiplier=1).then_inc(c.const_set, 1)
            pool.affine_select(out=c.mask_k[:], in_=c.mask_k[:], compare_op=ALU.is_ge, fill=NEG,
                               base=0, pattern=[[1, P]], channel_multiplier=-1).then_inc(c.const_set, 1)
            pool.wait_ge(c.const_set, 7)

        @block.vector
        def _(dve):
            dve.wait_ge(c.const_set, 7)
            dve.tensor_copy(c.ident_b[:], c.ident[:]).then_inc(c.ident_b_ready, 1)
            dve.wait_ge(c.ident_b_ready, 1)


def attention(nc, c, layer, x_src, weights, biases, mask, router, logits, experts, x_dst, xn_dst):
    causal = layer == 0
    with ExitStack() as ctx:
        def sb(name, shape, dt=F32):
            return ctx.enter_context(nc.sbuf_tensor(f"{name}_{layer}", shape, dt))

        def sem(name):
            return nc.alloc_semaphore(name=f"{name}_{layer}")

        w_raw = sb("w_raw", [P, 4, KT, D])
        w_hi = sb("w_hi", [P, 4, KT, D], F32R)
        w_lo = sb("w_lo", [P, 4, KT, D], F32R)
        bias = sb("bias", [P, 4, D])
        rw = sb("rw", [P, KT, experts])
        xb = [sb(f"xb{i}", [P, ST, D]) for i in range(2)]
        ctxf = [sb(f"ctxf{i}", [P, KT, S]) for i in range(2)]
        stats = sb("stats", [P, ST, 6])
        moments = sb("moments", [P, ST, 2])
        rstd = sb("rstd", [P, ST])
        xn = sb("xn", [P, ST, D])
        xt_hi, xt_lo = sb("xt_hi", [P, KT, S], F32R), sb("xt_lo", [P, KT, S], F32R)
        ct_hi, ct_lo = sb("ct_hi", [P, KT, S], F32R), sb("ct_lo", [P, KT, S], F32R)
        qkv_f = [sb(f"{n}_f", [P, ST, D]) for n in ("q", "k", "v")] if causal else None
        qk_pos = [sb(f"{n}_pos", [P, H, ST, HD]) for n in ("q", "k")]
        cols = [sb(f"{n}_cols", [P, HB, ST, 2, 4, HD], F32R) for n in ("q", "k")]
        q_st = [sb(f"q_st{i}", [P, HB * S], F32R) for i in range(2)]
        k_st = [sb(f"k_st{i}", [P, HB * S], F32R) for i in range(2)]
        v_st = [sb(f"v_st{i}", [P, H, ST, 32]) for i in range(2)]
        blocks = 3 if causal else 2
        mx_raw = sb("mx_raw", [P, 2, 2, 4, blocks])
        mx = sb("mx", [P, 2, 2, 4, ST])
        m_rows = [sb(f"m_rows{g}", [16, P], F32R) for g in range(2)]
        probs = [sb(f"probs{i}", [P, ST * S]) for i in range(8)]
        o_t = sb("o_t", [P, 4, S])
        rsum = sb("rsum", [P, ST, H])
        ao = sb("ao", [P, ST * D])
        ao_tok = sb("ao_tok", [P, ST, D]) if causal else None
        at_hi, at_lo = sb("at_hi", [P, KT, S], F32R), sb("at_lo", [P, KT, S], F32R)
        xr = sb("xr", [P, ST, D])
        proj = sb("proj", [P, ST, D])
        x_new = sb("x_new", [P, ST, D])
        stats2 = sb("stats2", [P, ST, 6])
        moments2 = sb("moments2", [P, ST, 2])
        rstd2 = sb("rstd2", [P, ST])
        xn2 = sb("xn2", [P, ST, D])
        xn2_t = sb("xn2_t", [P, KT, S])
        if not causal:
            mask_b = sb("mask_b", [P, B, ST], U8)
            mask_neg = sb("mask_neg", [P, B, ST])
            mask_keep = sb("mask_keep", [P, B, ST])

        pa, ps, pt, po = c.banks[0:2], c.banks[2:4], c.banks[4:6], c.banks[6:8]

        s = Semaphores(sem)

        def run(eng, step):
            step(0, 0, has_a=True, has_c=False)
            with eng.Fori(0, (B - 2) // 2) as i:
                step(2 * i + 1, 1, has_a=True, has_c=True)
                step(2 * i + 2, 0, has_a=True, has_c=True)
            step(B - 1, 1, has_a=False, has_c=True)

        with nc.Block() as block:

            @block.sync
            def _(sp):
                sp.dma_start(xb[0][:], c.rows(x_src, 0)).then_inc(s["x_loaded"], 16)
                sp.dma_start(ctxf[0][:], c.ctx_rows(0)).then_inc(s["ctx_loaded"], 16)
                for n, w in enumerate(weights):
                    sp.dma_start(w_raw[:, n], w).then_inc(s["w_loaded"], 16)
                for n, b in enumerate(biases):
                    sp.dma_start(bias[:, n], bcast(b, P)).then_inc(s["consts_loaded"], 16)
                sp.dma_start(rw[:], router).then_inc(s["consts_loaded"], 16)
                if not causal:
                    sp.dma_start(mask_b[:], mask).then_inc(s["consts_loaded"], 16)

                def bounce_a(b, par):
                    for n in range(3):
                        sp.wait_ge(s["qkv_ready"], 3 * b + n + 1)
                        c.settle(sp)
                        wait(sp, s["bounced_in"], 48 * b)
                        sp.dma_start(c.tokens(c.qkv_dram[n]), qkv_f[n][:]).then_inc(s["bounced_out"], 16)
                    for n in range(3):
                        sp.wait_ge(s["bounced_out"], 48 * (b + 1))
                        c.settle(sp)
                        if n < 2:
                            wait(sp, s["parts_lo"], 2 * b)
                            to = qk_pos[n][:]
                        else:
                            wait(sp, s["pv_done"], 4 * b - 4)
                            to = v_st[par][:, :, :, 0:HD]
                        sp.dma_start(to.rearrange("p h b d -> p (h b) d"), c.by_position(c.qkv_dram[n])
                                     ).then_inc(s["bounced_in"], 16)

                def bounce_c(b):
                    sp.wait_ge(s["ao_ready"], 2 * b + 2)
                    sp.dma_start(c.by_position(c.ao_dram),
                                 ao[:].rearrange("p (h d) -> p h d", d=HD)).then_inc(s["ao_out"], 16)
                    sp.wait_ge(s["ao_out"], 16 * (b + 2))
                    sp.wait_ge(s["at_filled"], b + 1)
                    sp.dma_start(ao_tok[:], c.tokens(c.ao_dram)).then_inc(s["ao_in"], 16)

                def store_c(b):
                    sp.wait_ge(s["out_ready"], b + 2)
                    c.settle(sp)
                    sp.dma_start(c.rows(x_dst, b), x_new[:]).then_inc(s["x_stored"], 16)
                    sp.wait_ge(s["xn2_ready"], b + 1)
                    c.settle(sp)
                    sp.dma_start(c.rows(xn_dst, b), xn2[:]).then_inc(s["xn_stored"], 16)

                def load_residual(b):
                    sp.wait_ge(s["out_ready"], b + 1)
                    c.settle(sp)
                    sp.dma_start(xr[:], c.rows(x_src, b)).then_inc(s["xr_loaded"], 16)

                def step(t, par, has_a, has_c):
                    if has_c:
                        load_residual(t - 1)
                        if causal:
                            bounce_c(t - 1)
                    if has_a:
                        if causal:
                            bounce_a(t + 1, 1 - par)
                        nxt = (t + 2) % B
                        sp.wait_ge(s["xn_ready"], t + 1)
                        c.settle(sp)
                        sp.wait_ge(s["x_loaded"], 16 * (t + 2))
                        c.settle(sp)
                        sp.dma_start(xb[par][:], c.rows(x_src, nxt)).then_inc(s["x_loaded"], 16)
                        sp.wait_ge(s["ctx_lo"], t + 1)
                        c.settle(sp)
                        sp.wait_ge(s["ctx_loaded"], 16 * (t + 2))
                        c.settle(sp)
                        sp.dma_start(ctxf[par][:], c.ctx_rows(nxt)).then_inc(s["ctx_loaded"], 16)
                    if has_c:
                        store_c(t - 1)

                sp.wait_ge(s["x_loaded"], 16)
                sp.dma_start(xb[1][:], c.rows(x_src, 1)).then_inc(s["x_loaded"], 16)
                sp.wait_ge(s["ctx_loaded"], 16)
                sp.dma_start(ctxf[1][:], c.ctx_rows(1)).then_inc(s["ctx_loaded"], 16)
                sp.sem_inc(s["x_stored"], 16)
                sp.sem_inc(s["xn_stored"], 16)
                sp.sem_inc(s["ao_out"], 16)
                if causal:
                    bounce_a(0, 0)
                run(sp, step)
                load_residual(B - 1)
                if causal:
                    bounce_c(B - 1)
                store_c(B - 1)
                sp.wait_ge(s["x_stored"], 16 * (B + 1))
                sp.wait_ge(s["xn_stored"], 16 * (B + 1))
                sp.wait_ge(s["x_loaded"], 16 * (B + 1))
                sp.wait_ge(s["ctx_loaded"], 16 * (B + 1))

            @block.gpsimd
            def _(pool):
                for v in v_st:
                    pool.memset(v[:], 1.0).then_inc(s["presets"], 1)
                for n in range(2):
                    pool.memset(cols[n][:].bitcast(F32), 0.0).then_inc(s["presets"], 1)
                pool.wait_ge(s["presets"], 4)
                pool.memset(cols[0][:, :, :, :, 3, 0:1].bitcast(F32).rearrange("p a b h o -> p (a b h) o"), 1.0
                            ).then_inc(s["presets"], 1)
                pool.memset(cols[1][:, :, :, :, 3, 1:2].bitcast(F32).rearrange("p a b h o -> p (a b h) o"), 1.0
                            ).then_inc(s["presets"], 1)
                pool.wait_ge(s["presets"], 6)
                if not causal:
                    pool.wait_ge(s["mask_ready"], 1)

                def part_a(b, par):
                    pool.wait_ge(s["moments_ready"], b + 1)
                    pool.tensor_tensor(rstd[:], rstd[:], c.minus_half[:], ALU.pow).then_inc(s["rstd_ready"], 1)
                    pool.wait_ge(s["ctx_hi"], b + 1)
                    pool.tensor_tensor(ct_lo[:], ctxf[par][:], ct_hi[:].bitcast(F32), ALU.subtract
                                       ).then_inc(s["ctx_lo"], 1)

                def parts_lo(b):
                    for n, (hi, lo) in enumerate(((0, 2), (0, 1))):
                        pool.wait_ge(s["parts_hi"], 2 * b + n + 1)
                        if n == 1 and not causal:
                            pool.tensor_copy(
                                cols[1][:, :, :, :, 3, 0],
                                mask_neg[:, bass.ds(b, 1), :].to_broadcast([P, HB, ST]).unsqueeze(3)
                                .to_broadcast([P, HB, ST, 2])).then_inc(s["mask_placed"], 1)
                        for half in range(2):
                            last = pool.tensor_tensor(
                                cols[n][:, :, :, half, lo, :],
                                qk_pos[n][:, half * HB:(half + 1) * HB, :, :],
                                cols[n][:, :, :, half, hi, :].bitcast(F32), ALU.subtract)
                        last.then_inc(s["parts_lo"], 1)

                def part_c(b):
                    pool.wait_ge(s["moments2_ready"], b + 1)
                    pool.tensor_tensor(rstd2[:], rstd2[:], c.minus_half[:], ALU.pow).then_inc(s["rstd2_ready"], 1)

                def step(t, par, has_a, has_c):
                    if has_a:
                        part_a(t + 1, 1 - par)
                        parts_lo(t + 1)
                    if has_c:
                        part_c(t - 1)

                part_a(0, 0)
                parts_lo(0)
                run(pool, step)
                part_c(B - 1)

            @block.scalar
            def _(act):
                for n in range(4):
                    act.wait_ge(s["w_loaded"], 64)
                    act.copy(w_hi[:, n], w_raw[:, n]).then_inc(s["w_hi_ready"], 1)

                def part_a(b, par):
                    act.wait_ge(s["ctx_loaded"], 16 * (b + 1))
                    wait(act, s["proj_filled"], 3 * b)
                    act.copy(ct_hi[:], ctxf[par][:]).then_inc(s["ctx_hi"], 1)
                    act.wait_ge(s["xt_filled"], b + 1)
                    act.copy(xt_hi[:].rearrange("p k t -> p (k t)"), pa[0][:]).then_inc(s["xt_hi"], 1)

                def parts_hi(b):
                    act.wait_ge(s["presets"], 6)
                    for n, slots in enumerate(((0, 1), (0, 2))):
                        if causal:
                            act.wait_ge(s["bounced_in"], 48 * (b + 1))
                        else:
                            act.wait_ge(s["k_masked"] if n else s["qkv_ready"], b + 1 if n else 3 * b + 1)
                        wait(act, s["cols_filled"], 8 * b)
                        for slot in slots:
                            for half in range(2):
                                last = act.copy(cols[n][:, :, :, half, slot, :],
                                                qk_pos[n][:, half * HB:(half + 1) * HB, :, :])
                        last.then_inc(s["parts_hi"], 1)

                def maxima(b, par, g):
                    act.wait_ge(s["m_filled"], 2 * b + g + 1)
                    wait(act, s[f"m_placed{g}"], 32 * b)
                    act.mul(m_rows[g][:], pa[0][0:16, 0:P], -1.0).then_inc(s["m_copied"], 1)
                    act.wait_ge(s["m_copied"], 2 * b + g + 1)
                    for half in range(2):
                        r = 64 * half + 49
                        act.dma_start(q_st[par][r:r + 1, g * 1024:(g + 1) * 1024].bitcast(F32),
                                      m_rows[g][half * 8:half * 8 + 8, :].bitcast(F32)
                                      ).then_inc(s[f"m_placed{g}"], 16)

                def stacks(b, par):
                    for j in range(4):
                        act.wait_ge(s["cols_filled"], 8 * b + 2 * j + 1)
                        st, u = (q_st, k_st)[j // 2][par], 2 * (j % 2)
                        act.copy(st[:, u * 512:(u + 1) * 512], pa[0][:]).then_inc(s["stacks_act"], 1)

                def exps(b, quads):
                    for g in quads:
                        wait(act, s["pv_done"], 4 * b + g - 1)
                        for j in range(4):
                            i = 4 * g + j
                            act.wait_ge(s["scores_t_filled"], 16 * b + i + 1)
                            w = 384 if causal else 512
                            act.activation(probs[i % 8][:, 0:w], pt[i % 2][:, 0:w], ACT.Exp,
                                           scale=float(HD) ** -0.5).then_inc(s["exp_done"], 1)

                def at_part(b):
                    act.wait_ge(s["at_filled"], b + 2)
                    act.copy(at_hi[:].rearrange("p k t -> p (k t)"), pa[1][:]).then_inc(s["at_hi"], 1)

                def xn2_turned(b):
                    act.wait_ge(s["xn2_t_filled"], b + 1)
                    act.copy(xn2_t[:].rearrange("p k t -> p (k t)"), pa[0][:]).then_inc(s["xn2_t_ready"], 1)

                def step(t, par, has_a, has_c):
                    if has_a:
                        part_a(t + 1, 1 - par)
                    maxima(t, par, 0)
                    if has_c:
                        at_part(t - 1)
                    maxima(t, par, 1)
                    if has_a:
                        parts_hi(t + 1)
                        stacks(t + 1, 1 - par)
                    exps(t, (0, 1))
                    if has_c:
                        xn2_turned(t - 1)
                    exps(t, (2, 3))

                part_a(0, 0)
                parts_hi(0)
                stacks(0, 0)
                run(act, step)
                at_part(B - 1)
                xn2_turned(B - 1)

            @block.vector
            def _(dve):
                dve.sem_inc(s["out_ready"], 1)
                dve.sem_inc(s["logits_ready"], 1)
                chain_a, chain_c = Steps(dve, s["dve_a"]), Steps(dve, s["dve_c"])
                for n in range(4):
                    dve.wait_ge(s["w_hi_ready"], n + 1)
                    dve.tensor_tensor(w_lo[:, n], w_raw[:, n], w_hi[:, n].bitcast(F32), ALU.subtract
                                      ).then_inc(s["w_ready"], 1)
                dve.wait_ge(s["consts_loaded"], 16 * (5 if causal else 6))
                if not causal:
                    dve.tensor_copy(mask_neg[:], mask_b[:]).then_inc(s["dve_w"], 1)
                    dve.wait_ge(s["dve_w"], 1)
                    dve.tensor_scalar(mask_keep[:], mask_neg[:], -1.0, 1.0, ALU.mult, ALU.add
                                      ).then_inc(s["dve_w"], 1)
                    dve.wait_ge(s["dve_w"], 2)
                    dve.tensor_scalar(mask_neg[:], mask_neg[:], NEG, None, ALU.mult).then_inc(s["mask_ready"], 1)
                    dve.wait_ge(s["mask_ready"], 1)

                def moments_of(chain, x, st, mo, to, ready):
                    for i in range(ST):
                        chain.mark(dve.bn_stats(st[:, i, :], x[:, i, :]))
                    chain.wait()
                    c.settle(dve)
                    for i in range(ST):
                        chain.mark(dve.bn_aggr(mo[:, i, :], st[:, i, :]))
                    chain.wait()
                    dve.tensor_scalar(to[:], mo[:, :, 1], EPS, None, ALU.add).then_inc(ready, 1)

                def norm_stats(b, par):
                    chain_a.at(4 * b)
                    dve.wait_ge(s["x_loaded"], 16 * (b + 1))
                    moments_of(chain_a, xb[par], stats, moments, rstd, s["moments_ready"])

                def norm_apply(b, par):
                    dve.wait_ge(s["rstd_ready"], b + 1)
                    wait(dve, s["xt_filled"], b)
                    for i in range(ST):
                        last = dve.tensor_scalar(xn[:, i, :], xb[par][:, i, :], moments[:, i, 0:1],
                                                 rstd[:, i:i + 1], ALU.subtract, ALU.mult)
                    last.then_inc(s["xn_ready"], 1)

                def projections(b, par):
                    dve.wait_ge(s["xt_hi"], b + 1)
                    dve.tensor_tensor(xt_lo[:].rearrange("p k t -> p (k t)"), pa[0][:],
                                      xt_hi[:].bitcast(F32).rearrange("p k t -> p (k t)"), ALU.subtract
                                      ).then_inc(s["xt_lo"], 1)
                    for n in range(3):
                        dve.wait_ge(s["proj_filled"], 3 * b + n + 1)
                        bank = pa[(n + 1) % 2][:]
                        if causal:
                            wait(dve, s["bounced_out"], 48 * b)
                            to, row = qkv_f[n][:], bias[:, n].unsqueeze(1).to_broadcast([P, ST, D])
                            bank = bank.rearrange("p (t f) -> p t f", t=ST)
                        else:
                            if n < 2:
                                wait(dve, s["parts_lo"], 2 * b)
                                to = qk_pos[n][:].rearrange("p h b d -> p b h d")
                            else:
                                wait(dve, s["pv_done"], 4 * b - 4)
                                dve.wait_ge(s["presets"], 6)
                                to = v_st[par][:, :, :, 0:HD].rearrange("p h b d -> p b h d")
                            row = (bias[:, n].rearrange("p (h d) -> p h d", d=HD).unsqueeze(1)
                                   .to_broadcast([P, ST, H, HD]))
                            bank = bank.rearrange("p (t h d) -> p t h d", t=ST, d=HD)
                        dve.tensor_tensor(to, bank, row, ALU.add).then_inc(s["qkv_ready"], 1)
                        if n == 1 and not causal:
                            dve.wait_ge(s["qkv_ready"], 3 * b + 2)
                            for t in range(ST):
                                last = dve.tensor_scalar(qk_pos[1][:, :, t, :], qk_pos[1][:, :, t, :],
                                                         mask_keep[:, bass.ds(b, 1), t], None, ALU.mult)
                            last.then_inc(s["k_masked"], 1)

                def maxes(b, g):
                    for k in range(4):
                        for half in range(2):
                            i = 8 * g + 2 * k + half
                            dve.wait_ge(s["scores_filled"], 16 * b + i + 1)
                            to = (mx_raw if causal else mx)[:, g, half, k, :]
                            w = 384 if causal else 512
                            dve.tensor_reduce(to, ps[i % 2][:, 0:w].rearrange("p (a k) -> p a k", a=blocks),
                                              AX.X, ALU.max).then_inc(s["maxes"], 1)
                    if causal:
                        dve.wait_ge(s["maxes"], 16 * b + 8 * (g + 1))
                        raw = mx_raw[:, g].rearrange("p h k a -> p (h k) a")
                        out = mx[:, g].rearrange("p h k a -> p (h k) a")
                        dve.tensor_copy(out[:, :, 0], raw[:, :, 0])
                        dve.tensor_tensor(out[:, :, 1], raw[:, :, 1], raw[:, :, 2], ALU.max
                                          ).then_inc(s["mx_ready"], 1)

                def stacks(b, par):
                    for j in range(4):
                        dve.wait_ge(s["cols_filled"], 8 * b + 2 * j + 2)
                        st, u = (q_st, k_st)[j // 2][par], 2 * (j % 2) + 1
                        dve.tensor_copy(st[:, u * 512:(u + 1) * 512], pa[1][:]).then_inc(s["stacks_dve"], 1)

                def normalise(b):
                    chain_c.at(6 * b)
                    for t in range(ST):
                        dve.wait_ge(s["o_filled"], 2 * b + t + 1)
                        sums = pa[t][:].rearrange("p (g h e) -> p g h e", h=2, e=32)
                        inv = rsum[:, t, :].rearrange("p (g h) -> p g h", h=2)
                        chain_c.mark(dve.reciprocal(inv, sums[:, :, :, HD]))
                        chain_c.wait()
                        if causal:
                            dve.wait_ge(s["ao_out"], 16 * (b + 1))
                            to = ao[:].rearrange("p (h g b d) -> p b g h d", h=2, b=ST, d=HD)[:, t]
                        else:
                            dve.wait_ge(s["at_filled"], b + 1)
                            to = ao[:].rearrange("p (b h g d) -> p b g h d", b=ST, h=2, d=HD)[:, t]
                        dve.tensor_tensor(to, sums[:, :, :, 0:HD],
                                          inv.unsqueeze(3).to_broadcast([P, HB, 2, HD]), ALU.mult
                                          ).then_inc(s["ao_ready"], 1)

                def at_part(b):
                    dve.wait_ge(s["at_hi"], b + 1)
                    dve.tensor_tensor(at_lo[:].rearrange("p k t -> p (k t)"), pa[1][:],
                                      at_hi[:].bitcast(F32).rearrange("p k t -> p (k t)"), ALU.subtract
                                      ).then_inc(s["at_lo"], 1)

                def residual(b):
                    dve.wait_ge(s["out_filled"], b + 1)
                    dve.tensor_tensor(proj[:], pa[1][:].rearrange("p (t f) -> p t f", t=ST),
                                      bias[:, 3].unsqueeze(1).to_broadcast([P, ST, D]), ALU.add
                                      ).then_inc(s["proj_copied"], 1)
                    dve.wait_ge(s["proj_copied"], b + 1)
                    dve.wait_ge(s["xr_loaded"], 16 * (b + 1))
                    dve.wait_ge(s["x_stored"], 16 * (b + 1))
                    dve.scalar_tensor_tensor(x_new[:], proj[:], c.tgate[:, layer:layer + 1], xr[:],
                                             ALU.mult, ALU.add).then_inc(s["out_ready"], 1)
                    dve.wait_ge(s["out_ready"], b + 2)
                    chain_c.at(6 * b + 2)
                    moments_of(chain_c, x_new, stats2, moments2, rstd2, s["moments2_ready"])

                def norm2_apply(b):
                    dve.wait_ge(s["rstd2_ready"], b + 1)
                    dve.wait_ge(s["xn_stored"], 16 * (b + 1))
                    for i in range(ST):
                        last = dve.tensor_scalar(xn2[:, i, :], x_new[:, i, :], moments2[:, i, 0:1],
                                                 rstd2[:, i:i + 1], ALU.subtract, ALU.mult)
                    last.then_inc(s["xn2_ready"], 1)

                def outputs(b, quads):
                    for g in quads:
                        dve.wait_ge(s["pv_done"], 4 * b + g + 1)
                        dve.tensor_copy(o_t[:, g, :], po[g % 2][:, 0:S]).then_inc(s["o_copied"], 1)

                def take_logits(b):
                    dve.wait_ge(s["logits_filled"], b + 1)
                    at = bass.ds(ST * b, ST)
                    dve.tensor_copy(logits[:, at, :], pa[1][:, 0:ST * experts].rearrange(
                        "p (t e) -> p t e", t=ST)).then_inc(s["logits_ready"], 1)

                def step(t, par, has_a, has_c):
                    if has_a:
                        norm_stats(t + 1, 1 - par)
                    if has_c:
                        normalise(t - 1)
                    if has_a:
                        norm_apply(t + 1, 1 - par)
                    maxes(t, 0)
                    if has_a:
                        projections(t + 1, 1 - par)
                    maxes(t, 1)
                    if has_c:
                        at_part(t - 1)
                        residual(t - 1)
                    if has_a:
                        stacks(t + 1, 1 - par)
                    if has_c:
                        norm2_apply(t - 1)
                    outputs(t, (0, 1))
                    if has_c:
                        take_logits(t - 1)
                    outputs(t, (2, 3))

                norm_stats(0, 0)
                norm_apply(0, 0)
                projections(0, 0)
                stacks(0, 0)
                run(dve, step)
                normalise(B - 1)
                at_part(B - 1)
                residual(B - 1)
                norm2_apply(B - 1)
                take_logits(B - 1)

            @block.tensor
            def _(pe):
                pe.sem_inc(s["at_filled"], 1)

                def turn(bank, x):
                    for k in range(KT):
                        for i in range(ST):
                            last = pe.transpose(bank[:, k * S + i * P:k * S + (i + 1) * P],
                                                x[:, i, k * P:(k + 1) * P], c.ident[:])
                    return last

                def project(bank, hi, lo, n):
                    for i in range(ST):
                        for k in range(KT):
                            at = slice(i * P, (i + 1) * P)
                            last = split_matmul(pe, bank[:, i * D:(i + 1) * D], (hi[:, k, at], lo[:, k, at]),
                                                (w_hi[:, n, k, :], w_lo[:, n, k, :]),
                                                first=k == 0, last=k == KT - 1)
                    return last

                def a1(b, z):
                    pe.wait_ge(s["xn_ready"], b + 1)
                    if z is not None:
                        pe.wait_ge(s["ao_ready"], 2 * z + 2)
                    turn(pa[0], xn).then_inc(s["xt_filled"], 1)
                    pe.wait_ge(s["w_ready"], 4)
                    pe.wait_ge(s["xt_lo"], b + 1)
                    project(pa[1], xt_hi, xt_lo, 0).then_inc(s["proj_filled"], 1)
                    pe.wait_ge(s["ctx_lo"], b + 1)
                    project(pa[0], ct_hi, ct_lo, 1).then_inc(s["proj_filled"], 1)
                    pe.wait_ge(s["qkv_ready"], 3 * b + 1)
                    project(pa[1], ct_hi, ct_lo, 2).then_inc(s["proj_filled"], 1)

                def a2(b, t, has_c):
                    for n in range(2):
                        pe.wait_ge(s["parts_lo"], 2 * b + n + 1)
                        if n == 1 and not causal:
                            pe.wait_ge(s["mask_placed"], b + 1)
                        for u in range(4):
                            j = 2 * n + u // 2
                            if j == 0:
                                if t is None or (u == 1 and not has_c):
                                    pe.wait_ge(s["qkv_ready"], 3 * b + 3)
                                elif u == 0:
                                    pe.wait_ge(s["m_copied"], 2 * t + 2)
                                else:
                                    pe.wait_ge(s["proj_copied"], t)
                            else:
                                pe.wait_ge(s["stacks_dve"] if u % 2 else s["stacks_act"], 4 * b + j)
                            for v in range(4):
                                hb = 4 * u + v
                                last = pe.transpose(
                                    pa[u % 2][:, v * P:(v + 1) * P],
                                    cols[n][:, hb // 2, hb % 2].bitcast(F32).rearrange("p h a d -> p (h a d)"),
                                    c.ident[:])
                            last.then_inc(s["cols_filled"], 1)

                def scores(b, par, g):
                    q, k = q_st[par], k_st[par]
                    for n in range(4):
                        for half in range(2):
                            i = 8 * g + 2 * n + half
                            rows = slice(64 * half, 64 * half + 49)
                            at = (4 * g + n) * S
                            wait(pe, s["maxes"], 16 * b + i - 1)
                            bank = ps[i % 2]
                            if causal:
                                pe.matmul(bank[:, 0:P], q[rows, at:at + P], k[rows, at:at + P],
                                          start=True, stop=False)
                                pe.matmul(bank[:, 0:P], c.ident_b[:], c.mask_q[:], start=False, stop=True)
                                pe.matmul(bank[:, P:3 * P], q[rows, at + P:at + S], k[rows, at:at + S],
                                          start=True, stop=False)
                                last = pe.matmul(bank[:, S:3 * P], c.ident_b[:], c.mask_q[:],
                                                 start=False, stop=True)
                            else:
                                for t in range(ST):
                                    last = pe.matmul(bank[:, t * S:(t + 1) * S],
                                                     q[rows, at + t * P:at + (t + 1) * P],
                                                     k[rows, at:at + S], start=True, stop=True)
                            last.then_inc(s["scores_filled"], 1)

                def turn_maxes(b, g, a):
                    if causal:
                        pe.wait_ge(s["mx_ready"], 2 * b + g + 1)
                    else:
                        pe.wait_ge(s["maxes"], 16 * b + 8 * (g + 1))
                    if g:
                        pe.wait_ge(s["m_copied"], 2 * b + 1)
                    elif a is not None:
                        pe.wait_ge(s["qkv_ready"], 3 * a + 2)
                    pe.transpose(pa[0][0:16, 0:P], mx[:, g].rearrange("p h k t -> p (h k t)"), c.ident[:]
                                 ).then_inc(s["m_filled"], 1)

                def scores_t(b, par, g):
                    q, k = q_st[par], k_st[par]
                    for j in range(4):
                        half, h8, i = j % 2, 2 * g + j // 2, 4 * g + j
                        rows = slice(64 * half, 64 * half + 50)
                        at = h8 * S
                        wait(pe, s["exp_done"], 16 * b + i - 1)
                        bank = pt[i % 2]
                        if causal:
                            pe.matmul(bank[:, 0:S], k[rows, at:at + P], q[rows, at:at + S],
                                      start=True, stop=False)
                            pe.matmul(bank[:, 0:P], c.ident_b[:], c.mask_k[:], start=False, stop=True)
                            pe.matmul(bank[:, S:3 * P], k[rows, at + P:at + S], q[rows, at + P:at + S],
                                      start=True, stop=False)
                            last = pe.matmul(bank[:, S:3 * P], c.ident_b[:], c.mask_k[:],
                                             start=False, stop=True)
                        else:
                            for t in range(ST):
                                last = pe.matmul(bank[:, t * S:(t + 1) * S],
                                                 k[rows, at + t * P:at + (t + 1) * P],
                                                 q[rows, at:at + S], start=True, stop=True)
                        last.then_inc(s["scores_t_filled"], 1)

                def values(b, par, g):
                    pe.wait_ge(s["exp_done"], 16 * b + 4 * g + 4)
                    wait(pe, s["o_copied"], 4 * b + g - 1)
                    for t in range(ST):
                        for j in range(4):
                            h = (j % 2) * HB + 2 * g + j // 2
                            q0, w = (P, P) if causal and t else (0, S)
                            last = pe.matmul(po[g % 2][32 * j:32 * j + 32, q0:q0 + w], v_st[par][:, h, t, :],
                                             probs[(4 * g + j) % 8][:, t * S:t * S + w],
                                             start=t == 0, stop=t == ST - 1)
                    last.then_inc(s["pv_done"], 1)

                def c0(b, t):
                    pe.wait_ge(s["o_copied"], 4 * b + 4)
                    pe.wait_ge(s["stacks_act"], 4 * t + 4)
                    pe.wait_ge(s["stacks_dve"], 4 * t + 4)
                    pe.wait_ge(s["logits_ready"], b + 1)
                    for n in range(ST):
                        for g in range(4):
                            last = pe.transpose(pa[n][:, g * P:(g + 1) * P], o_t[:, g, n * P:(n + 1) * P],
                                                c.ident[:])
                        last.then_inc(s["o_filled"], 1)

                def c1a(b, a):
                    if causal:
                        pe.wait_ge(s["ao_in"], 16 * (b + 1))
                    pe.wait_ge(s["ao_ready"], 2 * b + 2)
                    if a is not None:
                        pe.wait_ge(s["qkv_ready"], 3 * a + 3)
                    x = ao_tok if causal else ao[:].rearrange("p (t f) -> p t f", t=ST)
                    turn(pa[1], x).then_inc(s["at_filled"], 1)

                def c1b(b):
                    pe.wait_ge(s["at_lo"], b + 1)
                    project(pa[1], at_hi, at_lo, 3).then_inc(s["out_filled"], 1)

                def c2(b, a, t):
                    pe.wait_ge(s["xn2_ready"], b + 1)
                    if a is not None:
                        pe.wait_ge(s["stacks_act"], 4 * a + 4)
                        pe.wait_ge(s["stacks_dve"], 4 * a + 4)
                    elif t is not None:
                        pe.wait_ge(s["m_copied"], 2 * t + 2)
                    turn(pa[0], xn2).then_inc(s["xn2_t_filled"], 1)
                    pe.wait_ge(s["xn2_t_ready"], b + 1)
                    for i in range(ST):
                        for k in range(KT):
                            last = pe.matmul(pa[1][:, i * experts:(i + 1) * experts],
                                             xn2_t[:, k, i * P:(i + 1) * P], rw[:, k, :],
                                             start=k == 0, stop=k == KT - 1)
                    last.then_inc(s["logits_filled"], 1)

                def step(t, par, has_a, has_c):
                    a = t + 1 if has_a else None
                    if has_c:
                        c0(t - 1, t)
                    pe.wait_ge(s["stacks_act"], 4 * t + 4)
                    pe.wait_ge(s["stacks_dve"], 4 * t + 4)
                    scores(t, par, 0)
                    if has_a:
                        a1(t + 1, t - 1 if has_c else None)
                    scores(t, par, 1)
                    if has_a is False:
                        pe.wait_ge(s["ao_ready"], 2 * t)
                    turn_maxes(t, 0, a)
                    if has_c:
                        c1a(t - 1, a)
                    turn_maxes(t, 1, a)
                    if has_c:
                        c1b(t - 1)
                    if has_a:
                        a2(t + 1, t, has_c)
                    if causal:
                        pe.wait_ge(s["bounced_in"], 48 * (t + 1))
                    else:
                        pe.wait_ge(s["qkv_ready"], 3 * t + 3)
                    pe.wait_ge(s["m_placed0"], 32 * (t + 1))
                    scores_t(t, par, 0)
                    scores_t(t, par, 1)
                    values(t, par, 0)
                    if has_c:
                        c2(t - 1, a, t)
                    pe.wait_ge(s["m_placed1"], 32 * (t + 1))
                    scores_t(t, par, 2)
                    values(t, par, 1)
                    scores_t(t, par, 3)
                    values(t, par, 2)
                    values(t, par, 3)

                a1(0, None)
                a2(0, None, False)
                run(pe, step)
                c0(B - 1, B - 1)
                c1a(B - 1, None)
                c1b(B - 1)
                c2(B - 1, None, None)


def route(nc, c, layer, logits, experts):
    top2 = layer == 0
    E, cap = experts, SLOTS // experts
    HI = cap // 16
    GE = P // HI
    CT = 4
    BITS = 30
    with ExitStack() as ctx:
        def sb(name, shape, dt=F32):
            return ctx.enter_context(nc.sbuf_tensor(f"{name}_r{layer}", shape, dt))

        def sem(name):
            return nc.alloc_semaphore(name=f"{name}_r{layer}")

        iota_hi_i, iota_hi = sb("iota_hi_i", [P, HI], I32), sb("iota_hi", [P, HI])
        ids_i, ids = sb("ids_i", [P, NT], I32), sb("ids", [P, NT])
        spare_p, spare_i, spare = sb("spare_p", [P, 16], I32), sb("spare_i", [P, 16], I32), sb("spare", [P, 16])
        before, ones = sb("before", [P, P]), sb("ones", [P, P])
        diag = sb("diag", [P, GE])
        rank_e = sb("rank_e", [P, E])
        not_first = sb("not_first", [P, E, NT])
        rb = sb("rb", [P, E])
        lg, tmp, tmp2 = sb("lg", [P, NT, E]), sb("tmp", [P, NT, E]), sb("tmp2", [P, NT, E])
        best, best2, pick = sb("best", [P, NT]), sb("best2", [P, NT]), sb("pick", [P, NT])
        ratio, p1, p2 = sb("ratio", [P, NT]), sb("p1", [P, NT]), sb("p2", [P, NT])
        one1, one2 = sb("one1", [P, NT, E]), sb("one2", [P, NT, E])
        sel, wt = sb("sel", [P, NT, E]), sb("wt", [P, NT, E])
        totals, through = sb("totals", [P, E, NT]), sb("through", [P, E, NT])
        pos, pos_i = sb("pos", [P, NT, E]), sb("pos_i", [P, NT, E], I32)
        hi_i, lo_i = sb("hi_i", [P, NT, E], I32), sb("lo_i", [P, NT, E], I32)
        hi_f, lo_f = sb("hi_f", [P, NT, E]), sb("lo_f", [P, NT, E])
        one_hi = [sb(f"one_hi{i}", [P, CT, E, HI]) for i in range(2)]
        one_lo = [sb(f"one_lo{i}", [P, CT, E, 3, 16]) for i in range(2)]
        spread, lists = sb("spread", [P, GE, 48]), sb("lists", [P, 2, 48])
        idx_f, idx_i = sb("idx_f", [P, 2, 16]), sb("idx_i", [P, 2, 16], I32)
        if not top2:
            thr, cand = sb("thr", [P, E], I32), sb("cand", [P, E], I32)
            part, add = sb("part", [P, E]), sb("add", [P, E], I32)
            need = sb("need", [P, E])

        tables, loaded = sem("tables"), sem("loaded")
        step_done, exp_ready = sem("step_done"), sem("exp_ready")
        counted, count_in = sem("counted"), sem("count_in")
        rows_ready, rows_used = sem("rows_ready"), sem("rows_used")
        lists_out, lists_in = sem("lists_out"), sem("lists_in")
        lists_ready = sem("lists_ready")
        sums, lists_bank = c.banks[0], c.banks[1:3]
        counts = {"n": 0}

        with nc.Block() as block:

            @block.sync
            def _(sp):
                if top2:
                    sp.dma_start(rb[:], bcast(c.router_b, P)).then_inc(loaded, 16)
                sp.wait_ge(lists_ready, 1)
                sp.dma_start(c.idx_dram.rearrange("(g p l) -> p g l", g=2, l=16), idx_i[:]).then_inc(lists_out, 16)
                sp.dma_start(c.wt_dram.rearrange("(g p l) -> p g l", g=2, l=16), lists[:, :, 16:32]
                             ).then_inc(lists_out, 16)
                sp.wait_ge(lists_out, 32)
                with nc.allow_non_contiguous_dma(reason="4096 words of lists, once"):
                    sp.dma_start(c.idx[:], c.idx_dram.rearrange("(t p) -> p t", p=P)).then_inc(lists_in, 16)
                    sp.dma_start(c.wt[:], c.wt_dram.rearrange("(t p) -> p t", p=P)).then_inc(lists_in, 16)
                sp.wait_ge(lists_in, 32)

            @block.gpsimd
            def _(pool):
                pool.iota(iota_hi_i[:], [[1, HI]], base=0, channel_multiplier=0).then_inc(tables, 1)
                pool.iota(ids_i[:], [[P, NT]], base=0, channel_multiplier=1).then_inc(tables, 1)
                pool.iota(spare_p[:], [[1, 16]], base=0, channel_multiplier=16).then_inc(tables, 1)
                pool.memset(before[:], 1.0).then_inc(tables, 1)
                pool.memset(ones[:], 1.0).then_inc(tables, 1)
                pool.memset(diag[:], 1.0).then_inc(tables, 1)
                for e in range(E):
                    pool.memset(rank_e[:, e:e + 1], float(E - e)).then_inc(tables, 1)
                pool.memset(not_first[:], 1.0).then_inc(tables, 1)
                pool.wait_ge(tables, 7 + E)
                pool.memset(not_first[:, :, 0:1], 0.0).then_inc(tables, 1)
                pool.affine_select(out=before[:], in_=before[:], compare_op=ALU.is_gt, fill=0.0, base=0,
                                   pattern=[[1, P]], channel_multiplier=-1).then_inc(tables, 1)
                pool.affine_select(out=diag[:], in_=diag[:], compare_op=ALU.is_ge, fill=0.0, base=0,
                                   pattern=[[-HI, GE]], channel_multiplier=1).then_inc(tables, 1)
                pool.wait_ge(tables, 10 + E)
                pool.affine_select(out=diag[:], in_=diag[:], compare_op=ALU.is_ge, fill=0.0, base=HI - 1,
                                   pattern=[[HI, GE]], channel_multiplier=-1).then_inc(tables, 1)
                pool.wait_ge(tables, 11 + E)

            @block.scalar
            def _(act):
                act.wait_ge(exp_ready, 1)
                if top2:
                    act.activation(ratio[:], ratio[:], ACT.Exp).then_inc(exp_ready, 1)
                else:
                    act.activation(lg[:], lg[:], ACT.Exp).then_inc(exp_ready, 1)

            @block.tensor
            def _(pe):
                pe.wait_ge(tables, 11 + E)
                flat = "p a b -> p (a b)"
                if not top2:
                    for n in range(BITS + 1):
                        pe.wait_ge(count_in, n + 1)
                        pe.matmul(sums[:, 0:E], ones[:], part[:], start=True, stop=True).then_inc(counted, 1)
                for n in range(1 if top2 else 2):
                    pe.wait_ge(count_in, n + 1 + (0 if top2 else BITS + 1))
                    x = (sel if n or top2 else tmp)[:].rearrange(flat)
                    pe.matmul(c.banks[3][:, 0:NT * E], before[:], x, start=True, stop=True)
                    pe.matmul(c.banks[4][:, 0:NT * E], ones[:], x, start=True, stop=True).then_inc(counted, 1)
                for q in range(NT // CT):
                    pe.wait_ge(rows_ready, q + 1)
                    for g in range(2):
                        for t in range(CT):
                            last = pe.matmul(lists_bank[g][:, 0:GE * 48],
                                             one_hi[q % 2][:, t, g * GE:(g + 1) * GE].rearrange(flat),
                                             one_lo[q % 2][:, t, g * GE:(g + 1) * GE].rearrange(
                                                 "p e v l -> p (e v l)"),
                                             start=q == 0 and t == 0, stop=q == NT // CT - 1 and t == CT - 1)
                    last.then_inc(rows_used, 1)

            @block.vector
            def _(dve):
                def link(instruction):
                    counts["n"] += 1
                    instruction.then_inc(step_done, 1)
                    dve.wait_ge(step_done, counts["n"])

                def over_e(x):
                    return x.unsqueeze(2).to_broadcast([P, NT, E])

                def over_t(x):
                    return x.unsqueeze(1).to_broadcast([P, NT, E])

                dve.wait_ge(tables, 11 + E)
                dve.tensor_copy(iota_hi[:], iota_hi_i[:])
                dve.tensor_copy(ids[:], ids_i[:])
                link(dve.tensor_scalar(spare_i[:], spare_p[:], cap - 1, None, ALU.bitwise_and))
                link(dve.tensor_scalar(spare[:], spare_i[:], float(N), None, ALU.add))
                gate = c.tgate[:, 2 + layer:3 + layer]
                if top2:
                    dve.wait_ge(loaded, 16)
                    link(dve.tensor_tensor(lg[:], logits, over_t(rb[:]), ALU.add))

                    def first_best(x, top, one):
                        link(dve.tensor_reduce(top[:], x[:], AX.X, ALU.max))
                        link(dve.tensor_tensor(tmp[:], x[:], over_e(top[:]), ALU.is_equal))
                        link(dve.tensor_tensor(tmp[:], tmp[:], over_t(rank_e[:]), ALU.mult))
                        link(dve.tensor_reduce(pick[:], tmp[:], AX.X, ALU.max))
                        link(dve.tensor_tensor(one[:], tmp[:], over_e(pick[:]), ALU.is_equal))

                    first_best(lg, best, one1)
                    link(dve.scalar_tensor_tensor(tmp2[:], one1[:], -3e38, lg[:], ALU.mult, ALU.add))
                    first_best(tmp2, best2, one2)
                    dve.tensor_tensor(ratio[:], best2[:], best[:], ALU.subtract).then_inc(exp_ready, 1)
                    dve.wait_ge(exp_ready, 2)
                    link(dve.tensor_scalar(p1[:], ratio[:], 1.0, None, ALU.add))
                    link(dve.reciprocal(p1[:], p1[:]))
                    link(dve.tensor_tensor(p2[:], ratio[:], p1[:], ALU.mult))
                    link(dve.tensor_tensor(wt[:], one1[:], over_e(p1[:]), ALU.mult))
                    link(dve.tensor_tensor(tmp[:], one2[:], over_e(p2[:]), ALU.mult))
                    link(dve.tensor_tensor(wt[:], wt[:], tmp[:], ALU.add))
                    link(dve.tensor_scalar(wt[:], wt[:], gate, None, ALU.mult))
                    counts["n"] += 0
                    dve.tensor_tensor(sel[:], one1[:], one2[:], ALU.add).then_inc(count_in, 1)
                else:
                    link(dve.tensor_reduce(best[:], logits, AX.X, ALU.max))
                    dve.tensor_tensor(lg[:], logits, over_e(best[:]), ALU.subtract).then_inc(exp_ready, 1)
                    dve.wait_ge(exp_ready, 2)
                    link(dve.tensor_reduce(best2[:], lg[:], AX.X, ALU.add))
                    link(dve.reciprocal(best2[:], best2[:]))
                    link(dve.tensor_tensor(lg[:], lg[:], over_e(best2[:]), ALU.mult))
                    link(dve.memset(thr[:], 0))
                    for n in range(BITS + 1):
                        last = n == BITS
                        if not last:
                            link(dve.tensor_scalar(cand[:], thr[:], 1 << (BITS - 1 - n), None, ALU.bitwise_or))
                        link(dve.tensor_tensor(tmp[:], lg[:], over_t((thr if last else cand)[:].bitcast(F32)),
                                               ALU.is_gt if last else ALU.is_ge))
                        dve.tensor_reduce(part[:], tmp[:].rearrange("p t e -> p e t"), AX.X, ALU.add
                                          ).then_inc(count_in, 1)
                        dve.wait_ge(counted, n + 1)
                        if not last:
                            link(dve.tensor_scalar(add[:], sums[:, 0:E], float(cap), float(1 << (BITS - 1 - n)),
                                                   ALU.is_ge, ALU.mult))
                            link(dve.tensor_tensor(thr[:], thr[:], add[:], ALU.bitwise_or))
                    link(dve.tensor_scalar(need[:], sums[:, 0:E], -1.0, float(cap), ALU.mult, ALU.add))
                    link(dve.tensor_copy(sel[:], tmp[:]))
                    dve.tensor_tensor(tmp[:], lg[:], over_t(thr[:].bitcast(F32)), ALU.is_equal
                                      ).then_inc(count_in, 1)
                    dve.wait_ge(count_in, BITS + 2)
                    link(dve.tensor_scalar(wt[:], lg[:], gate, None, ALU.mult))

                def ranks(n):
                    dve.wait_ge(counted, n)
                    link(dve.tensor_copy(totals[:], c.banks[4][:, 0:NT * E].rearrange("p (t e) -> p e t", e=E)))
                    link(dve.tensor_tensor_scan(through[:].rearrange("p e t -> p (e t)"),
                                                not_first[:].rearrange("p e t -> p (e t)"),
                                                totals[:].rearrange("p e t -> p (e t)"), 0.0, ALU.mult, ALU.add))
                    link(dve.tensor_tensor(through[:], through[:], totals[:], ALU.subtract))
                    link(dve.tensor_tensor(pos[:], c.banks[3][:, 0:NT * E].rearrange("p (t e) -> p t e", e=E),
                                           through[:].rearrange("p e t -> p t e"), ALU.add))

                if top2:
                    ranks(1)
                    link(dve.tensor_scalar(tmp[:], pos[:], float(cap), None, ALU.is_lt))
                    link(dve.tensor_tensor(sel[:], sel[:], tmp[:], ALU.mult))
                else:
                    ranks(BITS + 2)
                    link(dve.tensor_tensor(pos[:], pos[:], over_t(need[:]), ALU.is_lt))
                    link(dve.tensor_tensor(tmp[:], tmp[:], pos[:], ALU.mult))
                    dve.tensor_tensor(sel[:], sel[:], tmp[:], ALU.add).then_inc(count_in, 1)
                    ranks(BITS + 3)
                link(dve.tensor_scalar(tmp[:], sel[:], -4096.0, 4096.0, ALU.mult, ALU.add))
                link(dve.tensor_tensor(pos_i[:], pos[:], tmp[:], ALU.add))
                link(dve.tensor_scalar(hi_i[:], pos_i[:], 4, None, ALU.logical_shift_right))
                link(dve.tensor_scalar(lo_i[:], pos_i[:], 15, None, ALU.bitwise_and))
                link(dve.tensor_copy(hi_f[:], hi_i[:]))
                link(dve.tensor_copy(lo_f[:], lo_i[:]))
                for q in range(NT // CT):
                    at = slice(q * CT, (q + 1) * CT)
                    if q >= 2:
                        dve.wait_ge(rows_used, q - 1)
                    flat = "p t e -> p (t e)"
                    n = CT * E
                    rows = one_lo[q % 2][:].rearrange("p t e v l -> p (t e) v l")
                    dve.tensor_tensor(one_hi[q % 2][:].rearrange("p t e h -> p (t e) h"),
                                      hi_f[:, at].rearrange(flat).unsqueeze(2).to_broadcast([P, n, HI]),
                                      iota_hi[:].unsqueeze(1).to_broadcast([P, n, HI]), ALU.is_equal)
                    link(dve.tensor_tensor(rows[:, :, 2],
                                           lo_f[:, at].rearrange(flat).unsqueeze(2).to_broadcast([P, n, 16]),
                                           iota_hi[:, 0:16].unsqueeze(1).to_broadcast([P, n, 16]), ALU.is_equal))
                    dve.tensor_tensor(one_lo[q % 2][:, :, :, 0, :], one_lo[q % 2][:, :, :, 2, :],
                                      ids[:, at].unsqueeze(2).unsqueeze(3).to_broadcast([P, CT, E, 16]), ALU.mult)
                    dve.tensor_tensor(rows[:, :, 1], rows[:, :, 2],
                                      wt[:, at].rearrange(flat).unsqueeze(2).to_broadcast([P, n, 16]), ALU.mult
                                      ).then_inc(rows_ready, 1)
                dve.wait_ge(rows_used, NT // CT)
                for g in range(2):
                    link(dve.tensor_tensor(spread[:], lists_bank[g][:, 0:GE * 48].rearrange(
                        "p (e v) -> p e v", e=GE), diag[:].unsqueeze(2).to_broadcast([P, GE, 48]), ALU.mult))
                    link(dve.tensor_reduce(lists[:, g], spread[:].rearrange("p e v -> p v e"), AX.X, ALU.add))
                link(dve.tensor_scalar(idx_f[:], lists[:, :, 32:48], -1.0, 1.0, ALU.mult, ALU.add))
                link(dve.tensor_tensor(idx_f[:], idx_f[:], spare[:].unsqueeze(1).to_broadcast([P, 2, 16]), ALU.mult))
                link(dve.tensor_tensor(idx_f[:], idx_f[:], lists[:, :, 0:16], ALU.add))
                dve.tensor_copy(idx_i[:], idx_f[:]).then_inc(lists_ready, 1)
                dve.wait_ge(lists_ready, 1)


def experts(nc, c, kind, E, T, CH, weights, x_rows, dst, base=None):
    shared = kind == "shared"
    M = 4 * CH
    U = M + 1
    TW = T * P
    W = 3072
    PIECE = W // 4
    YB = 2 if T == 2 else 1
    gate_fn = ACT.Silu if kind == "top2" else ACT.Gelu
    with ExitStack() as ctx:
        def sb(name, shape, dt=F32):
            return ctx.enter_context(nc.sbuf_tensor(f"{name}_{kind}", shape, dt))

        def sem(name):
            return nc.alloc_semaphore(name=f"{name}_{kind}")

        wn = 1 if shared else 2
        w_raw = [sb(f"w_raw{i}", [P, W]) for i in range(wn)]
        w_hi = [sb(f"w_hi{i}", [P, W], F32R) for i in range(wn)]
        w_lo = [sb(f"w_lo{i}", [P, W], F32R) for i in range(wn)]
        xg = [sb(f"xg{i}", [P, T, D]) for i in range(2)]
        x_hi, x_lo = sb("x_hi", [P, KT, TW], F32R), sb("x_lo", [P, KT, TW], F32R)
        gated = [sb(f"gated{i}", [P, TW]) for i in range(2)]
        h = [sb(f"h{i}", [P, TW]) for i in range(2)]
        h_hi = [sb(f"h_hi{i}", [P, TW], F32R) for i in range(2)]
        h_lo = [sb(f"h_lo{i}", [P, TW], F32R) for i in range(2)]
        ys = [sb(f"ys{i}", [P, T, D]) for i in range(2)]
        if shared:
            res = [sb(f"res{i}", [P, T, D]) for i in range(2)]
        else:
            idx = [sb(f"idx{i}", [P, T], I32) for i in range(2)]
            wt = [sb(f"wt{i}", [P, T]) for i in range(2)]

        s = Semaphores(sem)
        y_credit = YB * T

        def use_ab(e, m):
            return e * U + 1 + m

        def parity(par, n):
            return (par * U + n) % 2

        def a_w(w, k, m):
            return w[:, k * 512 + m * P:k * 512 + (m + 1) * P]

        def b_w(w, k, m):
            return w[:, 1024 + k * 512 + m * P:1024 + k * 512 + (m + 1) * P]

        def o_w(w, m):
            return w[:, 2048 + m * D:2048 + (m + 1) * D]

        def chunk_par(par, cc):
            return 0 if shared else (par * CH + cc) % 2

        with nc.Block() as block:

            @block.sync
            def _(sp):
                def load_w(chunk, buf, n):
                    if not (isinstance(n, int) and n == 0):
                        sp.wait_ge(s["w_loaded"], 16 * n)
                    c.settle(sp)
                    sp.dma_start(w_raw[buf][:], weights[bass.ds(chunk, 1)].rearrange("o p w -> p (o w)")
                                 ).then_inc(s["w_loaded"], 16)

                load_w(0, 0, 0)
                if shared:
                    for e in range(E):
                        par = e % 2
                        if e >= 2:
                            sp.wait_ge(s["x_turned"], e - 1 + 1)
                        sp.dma_start(xg[par][:], c.row_group(x_rows, e, T)
                                     ).then_inc(s["rows_in1" if par else "rows_in"], 16)
                        if e >= 2:
                            sp.wait_ge(s["y_read"], y_credit + T * (e - 1))
                            sp.dma_start(c.row_group(dst, e - 2, T), ys[par][:]
                                         ).then_inc(s["stored1" if par else "stored0"], 16)
                        sp.dma_start(res[par][:], c.row_group(base, e, T)
                                     ).then_inc(s["res_in1" if par else "res_in"], 16)
                    for e in range(E - 2, E):
                        sp.wait_ge(s["y_read"], y_credit + T * (e + 1))
                        sp.dma_start(c.row_group(dst, e, T), ys[e % 2][:]
                                     ).then_inc(s["stored1" if e % 2 else "stored0"], 16)
                    sp.wait_ge(s["stored0"], 16 * (E // 2))
                    sp.wait_ge(s["stored1"], 16 * (E // 2))
                else:
                    load_w(1, 1, 1)
                    with sp.Fori(0, E // 2) as i:
                        for par in range(2):
                            for cc in range(CH):
                                n = (2 * i + par) * CH + cc
                                sp.wait_ge(s["w_lo"], 4 * (n + 1))
                                load_w((n + 2) % (E * CH), chunk_par(par, cc), n + 2)
                    sp.wait_ge(s["w_loaded"], 16 * (E * CH + 2))

            @block.gpsimd
            def _(pool):
                if shared:
                    return

                def gather(e, par, n):
                    at = bass.ds(e * T, T)
                    pool.tensor_copy(wt[par][:], c.wt[:, at]).then_inc(s["wt_copied"], 1)
                    pool.tensor_copy(idx[par][:], c.idx[:, at]).then_inc(s["idx_copied"], 1)
                    pool.wait_ge(s["idx_copied"], n + 1)
                    c.settle(pool)
                    for t in range(T):
                        pool.indirect_dma_start(
                            out=xg[par][:, t, :], out_offset=None, in_=x_rows,
                            in_offset=bass.IndirectOffsetOnAxis(ap=idx[par][:, t:t + 1].bitcast(U32), axis=0)
                        ).then_inc(s["rows_in"], 16)

                pool.sem_inc(s["ys_free"], 2)
                gather(0, 0, 0)
                with pool.Fori(0, E // 2) as i:
                    for par in range(2):
                        e = 2 * i + par
                        pool.wait_ge(s["x_turned"], e + 1)
                        pool.wait_ge(s["rows_in"], 16 * T * (e + 1))
                        gather((e + 1) % E, 1 - par, e + 1)
                        pool.wait_ge(s["y_read"], y_credit + T * (e + 1))
                        c.settle(pool)
                        for t in range(T):
                            pool.indirect_dma_start(
                                out=dst, in_=ys[par][:, t, :], in_offset=None,
                                out_offset=bass.IndirectOffsetOnAxis(ap=idx[par][:, t:t + 1].bitcast(U32), axis=0),
                                compute_op=ALU.add).then_inc(s["added"], 16)
                        pool.wait_ge(s["added"], 16 * T * (e + 1))
                        pool.sem_inc(s["ys_free"], 1)
                pool.wait_ge(s["rows_in"], 16 * T * (E + 1))

            @block.scalar
            def _(act):
                def hi_piece(buf, j):
                    at = slice(j * PIECE, (j + 1) * PIECE)
                    act.copy(w_hi[buf][:, at], w_raw[buf][:, at]).then_inc(s["w_hi"], 1)

                def x_part(n, pair):
                    act.wait_ge(s["x_turned"], n + 2)
                    if T == 4:
                        for k in range(KT):
                            last = act.copy(x_hi[:, k], c.banks[2 * pair + k][:])
                    else:
                        last = act.copy(x_hi[:].rearrange("p k t -> p (k t)"), c.banks[2 * pair][:])
                    last.then_inc(s["x_hi"], 1)

                act.wait_ge(s["w_loaded"], 16)
                for j in range(4):
                    hi_piece(0, j)
                x_part(0, 0)

                def expert(e, par):
                    for m in range(M):
                        cc, g = m // 4, e * M + m
                        pair = c.banks[2 * parity(par, 1 + m):][:2]
                        act.wait_ge(s["ab_filled"], g + 1)
                        act.activation(gated[m % 2][:], pair[1][:, 0:TW], gate_fn).then_inc(s["gate_done"], 1)
                        if not shared:
                            n = e * CH + cc
                            buf = 1 - chunk_par(par, cc)
                            act.wait_ge(s["w_loaded"], 16 * (n + 2))
                            act.wait_ge(s["y_done"], 4 * n + 2)
                            hi_piece(buf, m % 4)
                        act.wait_ge(s["pair_read"], use_ab(e, m) + 1)
                        act.wait_ge(s["y_done"], g + 1)
                        act.copy(h_hi[m % 2][:], h[m % 2][:]).then_inc(s["h_hi"], 1)
                    if not (shared and e == E - 1):
                        x_part(e + 1, parity(par, U))

                c.over_experts(act, E, expert, shared)

            @block.vector
            def _(dve):
                def lo_piece(buf, j, n):
                    at = slice(j * PIECE, (j + 1) * PIECE)
                    dve.wait_ge(s["w_hi"], n)
                    dve.tensor_tensor(w_lo[buf][:, at], w_raw[buf][:, at], w_hi[buf][:, at].bitcast(F32),
                                      ALU.subtract).then_inc(s["w_lo"], 1)

                def x_part(n, pair):
                    dve.wait_ge(s["x_hi"], n + 1)
                    if T == 4:
                        for k in range(KT):
                            last = dve.tensor_tensor(x_lo[:, k], c.banks[2 * pair + k][:],
                                                     x_hi[:, k].bitcast(F32), ALU.subtract)
                    else:
                        flat = "p k t -> p (k t)"
                        last = dve.tensor_tensor(x_lo[:].rearrange(flat), c.banks[2 * pair][:],
                                                 x_hi[:].bitcast(F32).rearrange(flat), ALU.subtract)
                    last.then_inc(s["pair_read"], 1)

                dve.sem_inc(s["y_read"], y_credit)
                for j in range(4):
                    lo_piece(0, j, j + 1)
                x_part(0, 0)

                def expert(e, par):
                    for m in range(M):
                        cc, g = m // 4, e * M + m
                        pair = c.banks[2 * parity(par, 1 + m):][:2]
                        dve.wait_ge(s["gate_done"], g + 1)
                        dve.tensor_tensor(h[m % 2][:], pair[0][:, 0:TW], gated[m % 2][:], ALU.mult
                                          ).then_inc(s["pair_read"], 1)
                        if not shared:
                            lo_piece(1 - chunk_par(par, cc), m % 4, 4 * (e * CH + cc + 1) + m % 4 + 1)
                        dve.wait_ge(s["h_hi"], g + 1)
                        dve.tensor_tensor(h_lo[m % 2][:], h[m % 2][:], h_hi[m % 2][:].bitcast(F32), ALU.subtract
                                          ).then_inc(s["h_lo"], 1)
                    if not (shared and e == E - 1):
                        x_part(e + 1, parity(par, U))
                    dve.wait_ge(s["y_done"], (e + 1) * M + 2)
                    if shared:
                        dve.wait_ge(s["res_in1" if par else "res_in"], 16 * (e // 2 + 1))
                        wait(dve, s["stored1" if par else "stored0"], 16 * (e // 2))
                    else:
                        dve.wait_ge(s["ys_free"], e + 1)
                        dve.wait_ge(s["wt_copied"], e + 1)
                    for t in range(T):
                        bank = c.banks[4 + (par % YB) * T + t][:, 0:D]
                        if shared:
                            dve.scalar_tensor_tensor(ys[par][:, t, :], bank, c.tgate[:, 3:4], res[par][:, t, :],
                                                     ALU.mult, ALU.add).then_inc(s["y_read"], 1)
                        else:
                            dve.tensor_scalar(ys[par][:, t, :], bank, wt[par][:, t:t + 1], None, ALU.mult
                                              ).then_inc(s["y_read"], 1)

                c.over_experts(dve, E, expert, shared)

            @block.tensor
            def _(pe):
                pe.sem_inc(s["y_done"], 2)
                pe.sem_inc(s["x_turned"], 1)

                def turn_rows(buf, pair):
                    for k in range(KT):
                        for t in range(T):
                            if T == 4:
                                out = c.banks[2 * pair + k][:, t * P:(t + 1) * P]
                            else:
                                out = c.banks[2 * pair][:, k * TW + t * P:k * TW + (t + 1) * P]
                            last = pe.transpose(out, xg[buf][:, t, k * P:(k + 1) * P], c.ident[:])
                    last.then_inc(s["x_turned"], 1)

                pe.wait_ge(s["rows_in"], 16 if shared else 16 * T)
                turn_rows(0, 0)

                def ab(e, par, m):
                    cc = m // 4
                    buf = chunk_par(par, cc)
                    if m % 4 == 0:
                        pe.wait_ge(s["w_lo"], 4 if shared else 4 * (e * CH + cc + 1))
                    pe.wait_ge(s["pair_read"], use_ab(e, m) - (0 if m == 0 else 1))
                    pair = c.banks[2 * parity(par, 1 + m):][:2]
                    for bank, part in zip(pair, (a_w, b_w)):
                        for k in range(KT):
                            last = split_matmul(pe, bank[:, 0:TW],
                                                (part(w_hi[buf], k, m % 4), part(w_lo[buf], k, m % 4)),
                                                (x_hi[:, k], x_lo[:, k]), first=k == 0, last=k == KT - 1)
                    last.then_inc(s["ab_filled"], 1)

                def y(e, par, m):
                    buf = chunk_par(par, m // 4)
                    pe.wait_ge(s["h_lo"], e * M + m + 1)
                    if m == 0:
                        pe.wait_ge(s["y_read"], T * (e + 1))
                    for t in range(T):
                        at = slice(t * P, (t + 1) * P)
                        last = split_matmul(pe, c.banks[4 + (par % YB) * T + t][:, 0:D],
                                            (h_hi[m % 2][:, at], h_lo[m % 2][:, at]),
                                            (o_w(w_hi[buf], m % 4), o_w(w_lo[buf], m % 4)),
                                            first=m == 0, last=m == M - 1)
                    last.then_inc(s["y_done"], 1)

                def expert(e, par):
                    for m in range(M):
                        ab(e, par, m)
                        if m:
                            y(e, par, m - 1)
                    if not (shared and e == E - 1):
                        if shared:
                            pe.wait_ge(s["rows_in" if par else "rows_in1"], 16 * ((e + 1) // 2 + 1))
                        else:
                            pe.wait_ge(s["rows_in"], 16 * T * (e + 2))
                        pe.wait_ge(s["pair_read"], (e + 1) * U - 1)
                        turn_rows(1 - par, parity(par, U))
                    y(e, par, M - 1)

                c.over_experts(pe, E, expert, shared)


class Shared:

    def rows(self, x, b):
        return x[bass.ds(b * S, S), :].rearrange("(t p) f -> p t f", p=P)

    def ctx_rows(self, b):
        return self.ctx_t[bass.ds(b, 1)].rearrange("o p k t -> p (o k) t")

    def tokens(self, x):
        return x.rearrange("(t p) f -> p t f", p=P)

    def row_group(self, x, n, tiles):
        return x[n * tiles * P:(n + 1) * tiles * P, :].rearrange("(t p) f -> p t f", p=P)

    def settle(self, eng):
        eng.sem_inc(self.passed, 1)

    def over_experts(self, eng, count, expert, unrolled):
        if unrolled:
            for e in range(count):
                expert(e, e % 2)
        else:
            with eng.Fori(0, count // 2) as i:
                expert(2 * i, 0)
                expert(2 * i + 1, 1)

    def by_position(self, x):
        return x.rearrange("(a t) (u d) -> (t u) a d", a=H * ST, d=HD)


def build(nc, ins, out):
    c = Shared()
    with ExitStack() as ctx:
        c.sems = ctx

        def sb(name, shape, dt=F32):
            return ctx.enter_context(nc.sbuf_tensor(name, shape, dt))

        def sem(name):
            return ctx.enter_context(nc.semaphore(name))

        def dram(name, shape, dt=F32):
            return nc.dram_tensor(name, shape, dt, kind="Internal").ap()

        c.banks = [ctx.enter_context(nc.psum_tensor(f"bank{i}", [P, 512], F32)) for i in range(8)]
        c.ident, c.ident_b = sb("ident", [P, P]), sb("ident_b", [P, P], BF16)
        c.mask_q, c.mask_k = sb("mask_q", [P, P], BF16), sb("mask_k", [P, P], BF16)
        c.minus_half = sb("minus_half", [P, 2])
        c.gates, c.tgate = sb("gates", [P, 4]), sb("tgate", [P, 4])
        c.logits = sb("logits", [P, NT, 16])
        c.passed = sem("passed")
        c.gates_loaded, c.gates_ready = sem("gates_loaded"), sem("gates_ready")
        c.const_set, c.ident_b_ready = sem("const_set"), sem("ident_b_ready")
        c.g_xattn, c.g_ffn = ins["g_xattn"], ins["g_ffn"]
        c.ctx_t = ins["ctx_t"]
        c.router_b = ins["L0_ffn_router_b"]
        c.qkv_dram = [dram(f"{n}_dram", [S, D]) for n in ("q", "k", "v")]
        c.ao_dram = dram("ao_dram", [S, D])
        c.idx_dram, c.wt_dram = dram("idx_dram", [SLOTS], I32), dram("wt_dram", [SLOTS])
        c.idx, c.wt = sb("idx", [P, SLOT_TILES], I32), sb("wt", [P, SLOT_TILES])
        c.zeros_set, c.spare_zeroed = sem("zeros_set"), sem("spare_zeroed")
        x0, xn0 = dram("x0", [N + SPARE, D]), dram("xn0", [N + SPARE, D])
        x1, xn1 = dram("x1", [N, D]), dram("xn1", [N, D])
        c.with_spare = [x0, xn0]

        with nc.sbuf_tensor("zeros", [P, SPARE // P * D], F32) as c.zeros:
            constants(nc, c)
        layer_0 = nc.snapshot_sems()
        attention(nc, c, 0, ins["x"], [ins[f"L0_xattn_{w}"] for w in ("Wq", "Wk", "Wv", "Wp")],
                  [ins[f"L0_xattn_{w}"] for w in ("bq", "bk", "bv", "bp")], None,
                  ins["L0_ffn_router_w"], c.logits[:, :, 0:8], 8, x0, xn0)
        route(nc, c, 0, c.logits[:, :, 0:8], 8)
        experts(nc, c, "top2", 8, 4, 1, ins["L0_ffn"], xn0, x0)
        nc.clear_and_free_semaphores(nc.allocated_since(layer_0))
        nc.all_engine_barrier()
        attention(nc, c, 1, x0, [ins[f"L1_xattn_W_{w}"] for w in "QKVO"],
                  [ins[f"L1_xattn_b_{w}"] for w in "QKVO"], ins["mask"],
                  ins["L1_ffn_gate_w"], c.logits[:, :, 0:16], 16, x1, xn1)
        experts(nc, c, "shared", 4, 4, 1, ins["L1_shared"], xn1, out, x1)
        route(nc, c, 1, c.logits[:, :, 0:16], 16)
        experts(nc, c, "choice", 16, 2, 2, ins["L1_ffn"], xn1, out)


def kernel(**inputs):
    import numpy as np
    import concourse.bacc as bacc
    from concourse.bass_utils import run_bass_kernel_spmd

    def by_row_tile(w):
        return w.reshape(-1, P, w.shape[-1]).transpose(1, 0, 2)

    def chunks(up, gate, down):
        e, _, hid = up.shape
        n = hid // 512
        parts = [w.reshape(e, KT, P, n, 512).transpose(0, 3, 2, 1, 4).reshape(e * n, P, -1) for w in (up, gate)]
        parts.append(down.reshape(e, n, 4, P, D).transpose(0, 1, 3, 2, 4).reshape(e * n, P, -1))
        return np.concatenate(parts, axis=2)

    a = {name: np.asarray(value) for name, value in inputs.items()}
    arrays = {
        "x": a["x"].reshape(N, D),
        "ctx_t": a["ctx_1024"].transpose(0, 2, 1).reshape(B, KT, P, S).transpose(0, 2, 1, 3),
        "mask": a["mask_BxS2_bk0"].reshape(B, ST, P).transpose(2, 0, 1),
        "g_xattn": a["g_xattn"][None], "g_ffn": a["g_ffn"][None],
        "L0_ffn_router_w": by_row_tile(a["L0_ffn_router_w"].T),
        "L0_ffn_router_b": a["L0_ffn_router_b"][None],
        "L1_ffn_gate_w": by_row_tile(a["L1_ffn_gate_w"].T),
        "L0_ffn": chunks(a["L0_ffn_W"], a["L0_ffn_V"], a["L0_ffn_W_out"]),
        "L1_ffn": chunks(a["L1_ffn_Wu"].transpose(0, 2, 1), a["L1_ffn_Wg"].transpose(0, 2, 1),
                         a["L1_ffn_Wd"].transpose(0, 2, 1)),
        "L1_shared": chunks(a["L1_ffn_Su"].T[None], a["L1_ffn_Sg"].T[None], a["L1_ffn_Sd"].T[None]),
    }
    for w in ("Wq", "Wk", "Wv", "Wp"):
        arrays[f"L0_xattn_{w}"] = by_row_tile(a[f"L0_xattn_{w}"].T)
        arrays[f"L0_xattn_b{w[1]}"] = a[f"L0_xattn_b{w[1]}"][None]
    for w in "QKVO":
        arrays[f"L1_xattn_W_{w}"] = by_row_tile(a[f"L1_xattn_W_{w}"])
        arrays[f"L1_xattn_b_{w}"] = a[f"L1_xattn_b_{w}"][None]
    arrays = {name: np.ascontiguousarray(value) for name, value in arrays.items()}

    nc = bacc.Bacc("TRN2", target_bir_lowering=False, num_devices=1)
    ins = {name: nc.dram_tensor(name, value.shape, mybir.dt.from_np(value.dtype), kind="ExternalInput").ap()
           for name, value in arrays.items()}
    out = nc.dram_tensor("out", [N, D], F32, kind="ExternalOutput").ap()
    build(nc, ins, out)
    result = run_bass_kernel_spmd(nc, [arrays], core_ids=[0])
    return result.results[0]["out"].reshape(B, S, D)
```

```python
from contextlib import ExitStack

import concourse.bass as bass
import concourse.mybir as mybir

ACT = mybir.ActivationFunctionType
ALU = mybir.AluOpType
AX = mybir.AxisListType
F32 = mybir.dt.float32
F32R = mybir.dt.float32r
BF16 = mybir.dt.bfloat16
U8 = mybir.dt.uint8
I32 = mybir.dt.int32
U32 = mybir.dt.uint32

P = 128
D = 256
KT = D // P
B = 8
S = 256
ST = S // P
N = B * S
NT = N // P
H = 16
HD = D // H
HB = H // 2
NEG = -float(2 ** 100)
EPS = 1e-5
SLOTS = 4096
SLOT_TILES = SLOTS // P
SPARE = 512


def wait(eng, sem, value):
    if isinstance(value, int) and value <= 0:
        return
    eng.wait_ge(sem, value)


class Steps:

    def __init__(self, eng, sem):
        self.eng, self.sem, self.base, self.n = eng, sem, 0, 0

    def at(self, base):
        self.base, self.n = base, 0

    def mark(self, instruction):
        instruction.then_inc(self.sem, 1)
        self.n += 1

    def wait(self):
        self.eng.wait_ge(self.sem, self.base + self.n)


class Semaphores(dict):

    def __init__(self, take):
        super().__init__()
        self.take = take

    def __missing__(self, name):
        self[name] = self.take(name)
        return self[name]


def split_matmul(pe, out, lhs, rhs, first=True, last=True):
    (lh, ll), (rh, rl) = lhs, rhs
    pe.matmul(out, lh, rh, start=first, stop=False)
    pe.matmul(out, lh, rl, start=False, stop=False)
    return pe.matmul(out, ll, rh, start=False, stop=last)


def bcast(row, n):
    return row.to_broadcast([n, row.shape[-1]])


def constants(nc, c):
    with nc.Block() as block:

        @block.sync
        def _(sp):
            sp.dma_start(c.gates[:, 0:2], bcast(c.g_xattn, P)).then_inc(c.gates_loaded, 16)
            sp.dma_start(c.gates[:, 2:4], bcast(c.g_ffn, P)).then_inc(c.gates_loaded, 16)
            sp.wait_ge(c.zeros_set, 1)
            for x in c.with_spare:
                sp.dma_start(x[N:N + SPARE, :].rearrange("(t p) f -> p t f", p=P),
                             c.zeros[:].rearrange("p (t f) -> p t f", f=D)).then_inc(c.spare_zeroed, 16)
            sp.wait_ge(c.spare_zeroed, 16 * len(c.with_spare))

        @block.scalar
        def _(act):
            act.wait_ge(c.gates_loaded, 32)
            act.activation(c.tgate[:], c.gates[:], ACT.Tanh).then_inc(c.gates_ready, 1)
            act.wait_ge(c.gates_ready, 1)

        @block.gpsimd
        def _(pool):
            pool.memset(c.zeros[:], 0.0).then_inc(c.zeros_set, 1)
            pool.memset(c.ident[:], 0.0).then_inc(c.const_set, 1)
            pool.memset(c.mask_q[:], 0.0).then_inc(c.const_set, 1)
            pool.memset(c.mask_k[:], 0.0).then_inc(c.const_set, 1)
            pool.memset(c.minus_half[:], -0.5).then_inc(c.const_set, 1)
            pool.wait_ge(c.const_set, 4)
            pool.affine_select(out=c.ident[:], in_=c.ident[:], compare_op=ALU.not_equal, fill=1.0,
                               base=0, pattern=[[-1, P]], channel_multiplier=1).then_inc(c.const_set, 1)
            pool.affine_select(out=c.mask_q[:], in_=c.mask_q[:], compare_op=ALU.is_ge, fill=NEG,
                               base=0, pattern=[[-1, P]], channel_multiplier=1).then_inc(c.const_set, 1)
            pool.affine_select(out=c.mask_k[:], in_=c.mask_k[:], compare_op=ALU.is_ge, fill=NEG,
                               base=0, pattern=[[1, P]], channel_multiplier=-1).then_inc(c.const_set, 1)
            pool.wait_ge(c.const_set, 7)

        @block.vector
        def _(dve):
            dve.wait_ge(c.const_set, 7)
            dve.tensor_copy(c.ident_b[:], c.ident[:]).then_inc(c.ident_b_ready, 1)
            dve.wait_ge(c.ident_b_ready, 1)


def attention(nc, c, layer, x_src, weights, biases, mask, router, logits, experts, x_dst, xn_dst):
    causal = layer == 0
    with ExitStack() as ctx:
        def sb(name, shape, dt=F32):
            return ctx.enter_context(nc.sbuf_tensor(f"{name}_{layer}", shape, dt))

        def sem(name):
            return nc.alloc_semaphore(name=f"{name}_{layer}")

        w_raw = sb("w_raw", [P, 4, KT, D])
        w_hi = sb("w_hi", [P, 4, KT, D], F32R)
        w_lo = sb("w_lo", [P, 4, KT, D], F32R)
        bias = sb("bias", [P, 4, D])
        rw = sb("rw", [P, KT, experts])
        xb = [sb(f"xb{i}", [P, ST, D]) for i in range(2)]
        ctxf = [sb(f"ctxf{i}", [P, KT, S]) for i in range(2)]
        stats = sb("stats", [P, ST, 6])
        moments = sb("moments", [P, ST, 2])
        rstd = sb("rstd", [P, ST])
        xn = sb("xn", [P, ST, D])
        xt_hi, xt_lo = sb("xt_hi", [P, KT, S], F32R), sb("xt_lo", [P, KT, S], F32R)
        ct_hi, ct_lo = sb("ct_hi", [P, KT, S], F32R), sb("ct_lo", [P, KT, S], F32R)
        qkv_f = [sb(f"{n}_f", [P, ST, D]) for n in ("q", "k", "v")] if causal else None
        qk_pos = [sb(f"{n}_pos", [P, H, ST, HD]) for n in ("q", "k")]
        cols = [sb(f"{n}_cols", [P, HB, ST, 2, 4, HD], F32R) for n in ("q", "k")]
        q_st = [sb(f"q_st{i}", [P, HB * S], F32R) for i in range(2)]
        k_st = [sb(f"k_st{i}", [P, HB * S], F32R) for i in range(2)]
        v_st = [sb(f"v_st{i}", [P, H, ST, 32]) for i in range(2)]
        blocks = 3 if causal else 2
        mx_raw = sb("mx_raw", [P, 2, 2, 4, blocks])
        mx = sb("mx", [P, 2, 2, 4, ST])
        m_rows = [sb(f"m_rows{g}", [16, P], F32R) for g in range(2)]
        probs = [sb(f"probs{i}", [P, ST * S]) for i in range(8)]
        o_t = sb("o_t", [P, 4, S])
        rsum = sb("rsum", [P, ST, H])
        ao = sb("ao", [P, ST * D])
        ao_tok = sb("ao_tok", [P, ST, D]) if causal else None
        at_hi, at_lo = sb("at_hi", [P, KT, S], F32R), sb("at_lo", [P, KT, S], F32R)
        xr = sb("xr", [P, ST, D])
        proj = sb("proj", [P, ST, D])
        x_new = sb("x_new", [P, ST, D])
        stats2 = sb("stats2", [P, ST, 6])
        moments2 = sb("moments2", [P, ST, 2])
        rstd2 = sb("rstd2", [P, ST])
        xn2 = sb("xn2", [P, ST, D])
        xn2_t = sb("xn2_t", [P, KT, S])
        if not causal:
            mask_b = sb("mask_b", [P, B, ST], U8)
            mask_neg = sb("mask_neg", [P, B, ST])
            mask_keep = sb("mask_keep", [P, B, ST])

        ORDER = (1, 0, 2)
        pa, ps, pt, po = c.banks[0:2], c.banks[2:4], c.banks[4:6], c.banks[6:8]

        s = Semaphores(sem)

        def run(eng, step):
            step(0, 0, has_a=True, has_c=False)
            with eng.Fori(0, (B - 2) // 2) as i:
                step(2 * i + 1, 1, has_a=True, has_c=True)
                step(2 * i + 2, 0, has_a=True, has_c=True)
            step(B - 1, 1, has_a=False, has_c=True)

        with nc.Block() as block:

            @block.sync
            def _(sp):
                sp.dma_start(xb[0][:], c.rows(x_src, 0)).then_inc(s["x_loaded"], 16)
                sp.dma_start(ctxf[0][:], c.ctx_rows(0)).then_inc(s["ctx_loaded"], 16)
                for n, w in enumerate(weights):
                    sp.dma_start(w_raw[:, n], w).then_inc(s["w_loaded"], 16)
                for n, b in enumerate(biases):
                    sp.dma_start(bias[:, n], bcast(b, P)).then_inc(s["consts_loaded"], 16)
                sp.dma_start(rw[:], router).then_inc(s["consts_loaded"], 16)
                if not causal:
                    sp.dma_start(mask_b[:], mask).then_inc(s["consts_loaded"], 16)

                def bounce_a(b, par):
                    for rank, n in enumerate(ORDER):
                        sp.wait_ge(s["qkv_ready"], 3 * b + rank + 1)
                        c.settle(sp)
                        wait(sp, s[f"bounced_in{n}"], 16 * b)
                        sp.dma_start(c.tokens(c.qkv_dram[n]), qkv_f[n][:]).then_inc(s[f"bounced_out{n}"], 16)
                    for n in ORDER:
                        sp.wait_ge(s[f"bounced_out{n}"], 16 * (b + 1))
                        c.settle(sp)
                        if n < 2:
                            wait(sp, s["parts_lo"], 2 * b)
                            to = qk_pos[n][:]
                        else:
                            wait(sp, s["pv_done"], 4 * b - 4)
                            to = v_st[par][:, :, :, 0:HD]
                        sp.dma_start(to.rearrange("p h b d -> p (h b) d"), c.by_position(c.qkv_dram[n])
                                     ).then_inc(s[f"bounced_in{n}"], 16)

                def bounce_c(b):
                    sp.wait_ge(s["ao_ready"], 2 * b + 2)
                    sp.dma_start(c.by_position(c.ao_dram),
                                 ao[:].rearrange("p (h d) -> p h d", d=HD)).then_inc(s["ao_out"], 16)
                    sp.wait_ge(s["ao_out"], 16 * (b + 2))
                    sp.wait_ge(s["at_filled"], b + 1)
                    sp.dma_start(ao_tok[:], c.tokens(c.ao_dram)).then_inc(s["ao_in"], 16)

                def store_c(b):
                    sp.wait_ge(s["out_ready"], b + 2)
                    c.settle(sp)
                    sp.dma_start(c.rows(x_dst, b), x_new[:]).then_inc(s["x_stored"], 16)
                    sp.wait_ge(s["xn2_ready"], b + 1)
                    c.settle(sp)
                    sp.dma_start(c.rows(xn_dst, b), xn2[:]).then_inc(s["xn_stored"], 16)

                def load_residual(b):
                    sp.wait_ge(s["out_ready"], b + 1)
                    c.settle(sp)
                    sp.dma_start(xr[:], c.rows(x_src, b)).then_inc(s["xr_loaded"], 16)

                def step(t, par, has_a, has_c):
                    if has_c:
                        load_residual(t - 1)
                        if causal:
                            bounce_c(t - 1)
                    if has_a:
                        if causal:
                            bounce_a(t + 1, 1 - par)
                        nxt = (t + 2) % B
                        sp.wait_ge(s["xn_ready"], t + 1)
                        c.settle(sp)
                        sp.wait_ge(s["x_loaded"], 16 * (t + 2))
                        c.settle(sp)
                        sp.dma_start(xb[par][:], c.rows(x_src, nxt)).then_inc(s["x_loaded"], 16)
                        sp.wait_ge(s["ctx_lo"], t + 1)
                        c.settle(sp)
                        sp.wait_ge(s["ctx_loaded"], 16 * (t + 2))
                        c.settle(sp)
                        sp.dma_start(ctxf[par][:], c.ctx_rows(nxt)).then_inc(s["ctx_loaded"], 16)
                    if has_c:
                        store_c(t - 1)

                sp.wait_ge(s["x_loaded"], 16)
                sp.dma_start(xb[1][:], c.rows(x_src, 1)).then_inc(s["x_loaded"], 16)
                sp.wait_ge(s["ctx_loaded"], 16)
                sp.dma_start(ctxf[1][:], c.ctx_rows(1)).then_inc(s["ctx_loaded"], 16)
                sp.sem_inc(s["x_stored"], 16)
                sp.sem_inc(s["xn_stored"], 16)
                sp.sem_inc(s["ao_out"], 16)
                if causal:
                    bounce_a(0, 0)
                run(sp, step)
                load_residual(B - 1)
                if causal:
                    bounce_c(B - 1)
                store_c(B - 1)
                sp.wait_ge(s["x_stored"], 16 * (B + 1))
                sp.wait_ge(s["xn_stored"], 16 * (B + 1))
                sp.wait_ge(s["x_loaded"], 16 * (B + 1))
                sp.wait_ge(s["ctx_loaded"], 16 * (B + 1))

            @block.gpsimd
            def _(pool):
                for v in v_st:
                    pool.memset(v[:], 1.0).then_inc(s["presets"], 1)
                for n in range(2):
                    pool.memset(cols[n][:].bitcast(F32), 0.0).then_inc(s["presets"], 1)
                pool.wait_ge(s["presets"], 4)
                pool.memset(cols[0][:, :, :, :, 3, 0:1].bitcast(F32).rearrange("p a b h o -> p (a b h) o"), 1.0
                            ).then_inc(s["presets"], 1)
                pool.memset(cols[1][:, :, :, :, 3, 1:2].bitcast(F32).rearrange("p a b h o -> p (a b h) o"), 1.0
                            ).then_inc(s["presets"], 1)
                pool.wait_ge(s["presets"], 6)
                if not causal:
                    pool.wait_ge(s["mask_ready"], 1)

                def part_a(b, par):
                    pool.wait_ge(s["moments_ready"], b + 1)
                    pool.tensor_tensor(rstd[:], rstd[:], c.minus_half[:], ALU.pow).then_inc(s["rstd_ready"], 1)
                    pool.wait_ge(s["ctx_hi"], b + 1)
                    pool.tensor_tensor(ct_lo[:], ctxf[par][:], ct_hi[:].bitcast(F32), ALU.subtract
                                       ).then_inc(s["ctx_lo"], 1)

                def parts_lo(b):
                    for n, (hi, lo) in enumerate(((0, 2), (0, 1))):
                        pool.wait_ge(s["parts_hi"], 2 * b + n + 1)
                        if n == 1 and not causal:
                            pool.tensor_copy(
                                cols[1][:, :, :, :, 3, 0],
                                mask_neg[:, bass.ds(b, 1), :].to_broadcast([P, HB, ST]).unsqueeze(3)
                                .to_broadcast([P, HB, ST, 2])).then_inc(s["mask_placed"], 1)
                        for half in range(2):
                            last = pool.tensor_tensor(
                                cols[n][:, :, :, half, lo, :],
                                qk_pos[n][:, half * HB:(half + 1) * HB, :, :],
                                cols[n][:, :, :, half, hi, :].bitcast(F32), ALU.subtract)
                        last.then_inc(s["parts_lo"], 1)

                def part_c(b):
                    pool.wait_ge(s["moments2_ready"], b + 1)
                    pool.tensor_tensor(rstd2[:], rstd2[:], c.minus_half[:], ALU.pow).then_inc(s["rstd2_ready"], 1)

                def step(t, par, has_a, has_c):
                    if has_a:
                        part_a(t + 1, 1 - par)
                    if has_c:
                        part_c(t - 1)
                    if has_a:
                        parts_lo(t + 1)

                part_a(0, 0)
                parts_lo(0)
                run(pool, step)
                part_c(B - 1)

            @block.scalar
            def _(act):
                for n in range(4):
                    act.wait_ge(s["w_loaded"], 64)
                    act.copy(w_hi[:, n], w_raw[:, n]).then_inc(s["w_hi_ready"], 1)

                def part_a(b, par):
                    act.wait_ge(s["ctx_loaded"], 16 * (b + 1))
                    wait(act, s["proj_filled"], 3 * b)
                    act.copy(ct_hi[:], ctxf[par][:]).then_inc(s["ctx_hi"], 1)
                    act.wait_ge(s["xt_filled"], b + 1)
                    act.copy(xt_hi[:].rearrange("p k t -> p (k t)"), pa[0][:]).then_inc(s["xt_hi"], 1)

                def parts_hi(b, which):
                    act.wait_ge(s["presets"], 6)
                    for n in which:
                        slots = ((0, 1), (0, 2))[n]
                        if causal:
                            act.wait_ge(s[f"bounced_in{n}"], 16 * (b + 1))
                        else:
                            act.wait_ge(s["k_masked"] if n else s["qkv_ready"], b + 1 if n else 3 * b + 2)
                        wait(act, s["cols_filled"], 8 * b)
                        for slot in slots:
                            for half in range(2):
                                last = act.copy(cols[n][:, :, :, half, slot, :],
                                                qk_pos[n][:, half * HB:(half + 1) * HB, :, :])
                        last.then_inc(s["parts_hi"], 1)

                def maxima(b, par, g):
                    act.wait_ge(s["m_filled"], 2 * b + g + 1)
                    wait(act, s[f"m_placed{g}"], 32 * b)
                    act.mul(m_rows[g][:], pa[0][0:16, 0:P], -1.0).then_inc(s["m_copied"], 1)
                    act.wait_ge(s["m_copied"], 2 * b + g + 1)
                    for half in range(2):
                        r = 64 * half + 49
                        act.dma_start(q_st[par][r:r + 1, g * 1024:(g + 1) * 1024].bitcast(F32),
                                      m_rows[g][half * 8:half * 8 + 8, :].bitcast(F32)
                                      ).then_inc(s[f"m_placed{g}"], 16)

                def stacks(b, par, which):
                    for j in which:
                        act.wait_ge(s["cols_filled"], 8 * b + 2 * j + 1)
                        st, u = (q_st, k_st)[j // 2][par], 2 * (j % 2)
                        act.copy(st[:, u * 512:(u + 1) * 512], pa[0][:]).then_inc(s["stacks_act"], 1)

                def exps(b, quads):
                    for g in quads:
                        wait(act, s["pv_done"], 4 * b + g - 1)
                        for j in range(4):
                            i = 4 * g + j
                            act.wait_ge(s["scores_t_filled"], 16 * b + i + 1)
                            w = 384 if causal else 512
                            act.activation(probs[i % 8][:, 0:w], pt[i % 2][:, 0:w], ACT.Exp,
                                           scale=float(HD) ** -0.5).then_inc(s["exp_done"], 1)

                def at_part(b):
                    act.wait_ge(s["at_filled"], b + 2)
                    act.copy(at_hi[:].rearrange("p k t -> p (k t)"), pa[1][:]).then_inc(s["at_hi"], 1)

                def xn2_turned(b):
                    act.wait_ge(s["xn2_t_filled"], b + 1)
                    act.copy(xn2_t[:].rearrange("p k t -> p (k t)"), pa[0][:]).then_inc(s["xn2_t_ready"], 1)

                def step(t, par, has_a, has_c):
                    if has_a:
                        part_a(t + 1, 1 - par)
                    maxima(t, par, 0)
                    if has_c:
                        at_part(t - 1)
                    maxima(t, par, 1)
                    exps(t, (0, 1))
                    if has_a:
                        parts_hi(t + 1, (0,))
                    exps(t, (2,))
                    if has_a:
                        parts_hi(t + 1, (1,))
                    if has_c:
                        xn2_turned(t - 1)
                    if has_a:
                        stacks(t + 1, 1 - par, (0, 1))
                    exps(t, (3,))
                    if has_a:
                        stacks(t + 1, 1 - par, (2, 3))

                part_a(0, 0)
                parts_hi(0, (0, 1))
                stacks(0, 0, range(4))
                run(act, step)
                at_part(B - 1)
                xn2_turned(B - 1)

            @block.vector
            def _(dve):
                dve.sem_inc(s["out_ready"], 1)
                dve.sem_inc(s["logits_ready"], 1)
                chain_a, chain_c = Steps(dve, s["dve_a"]), Steps(dve, s["dve_c"])
                for n in range(4):
                    dve.wait_ge(s["w_hi_ready"], n + 1)
                    dve.tensor_tensor(w_lo[:, n], w_raw[:, n], w_hi[:, n].bitcast(F32), ALU.subtract
                                      ).then_inc(s["w_ready"], 1)
                dve.wait_ge(s["consts_loaded"], 16 * (5 if causal else 6))
                if not causal:
                    dve.tensor_copy(mask_neg[:], mask_b[:]).then_inc(s["dve_w"], 1)
                    dve.wait_ge(s["dve_w"], 1)
                    dve.tensor_scalar(mask_keep[:], mask_neg[:], -1.0, 1.0, ALU.mult, ALU.add
                                      ).then_inc(s["dve_w"], 1)
                    dve.wait_ge(s["dve_w"], 2)
                    dve.tensor_scalar(mask_neg[:], mask_neg[:], NEG, None, ALU.mult).then_inc(s["mask_ready"], 1)
                    dve.wait_ge(s["mask_ready"], 1)

                def moments_of(chain, x, st, mo, to, ready):
                    for i in range(ST):
                        chain.mark(dve.bn_stats(st[:, i, :], x[:, i, :]))
                    chain.wait()
                    c.settle(dve)
                    for i in range(ST):
                        chain.mark(dve.bn_aggr(mo[:, i, :], st[:, i, :]))
                    chain.wait()
                    dve.tensor_scalar(to[:], mo[:, :, 1], EPS, None, ALU.add).then_inc(ready, 1)

                def norm_stats(b, par):
                    chain_a.at(4 * b)
                    dve.wait_ge(s["x_loaded"], 16 * (b + 1))
                    moments_of(chain_a, xb[par], stats, moments, rstd, s["moments_ready"])

                def norm_apply(b, par):
                    dve.wait_ge(s["rstd_ready"], b + 1)
                    wait(dve, s["xt_filled"], b)
                    for i in range(ST):
                        last = dve.tensor_scalar(xn[:, i, :], xb[par][:, i, :], moments[:, i, 0:1],
                                                 rstd[:, i:i + 1], ALU.subtract, ALU.mult)
                    last.then_inc(s["xn_ready"], 1)

                def projections(b, par):
                    dve.wait_ge(s["xt_hi"], b + 1)
                    dve.tensor_tensor(xt_lo[:].rearrange("p k t -> p (k t)"), pa[0][:],
                                      xt_hi[:].bitcast(F32).rearrange("p k t -> p (k t)"), ALU.subtract
                                      ).then_inc(s["xt_lo"], 1)
                    for rank, n in enumerate(ORDER):
                        dve.wait_ge(s["proj_filled"], 3 * b + rank + 1)
                        bank = pa[(rank + 1) % 2][:]
                        if causal:
                            wait(dve, s[f"bounced_out{n}"], 16 * b)
                            to, row = qkv_f[n][:], bias[:, n].unsqueeze(1).to_broadcast([P, ST, D])
                            bank = bank.rearrange("p (t f) -> p t f", t=ST)
                        else:
                            if n < 2:
                                wait(dve, s["parts_lo"], 2 * b)
                                to = qk_pos[n][:].rearrange("p h b d -> p b h d")
                            else:
                                wait(dve, s["pv_done"], 4 * b - 4)
                                dve.wait_ge(s["presets"], 6)
                                to = v_st[par][:, :, :, 0:HD].rearrange("p h b d -> p b h d")
                            row = (bias[:, n].rearrange("p (h d) -> p h d", d=HD).unsqueeze(1)
                                   .to_broadcast([P, ST, H, HD]))
                            bank = bank.rearrange("p (t h d) -> p t h d", t=ST, d=HD)
                        dve.tensor_tensor(to, bank, row, ALU.add).then_inc(s["qkv_ready"], 1)
                        if n == 1 and not causal:
                            dve.wait_ge(s["qkv_ready"], 3 * b + 1)
                            for t in range(ST):
                                last = dve.tensor_scalar(qk_pos[1][:, :, t, :], qk_pos[1][:, :, t, :],
                                                         mask_keep[:, bass.ds(b, 1), t], None, ALU.mult)
                            last.then_inc(s["k_masked"], 1)

                def maxes(b, g):
                    for k in range(4):
                        for half in range(2):
                            i = 8 * g + 2 * k + half
                            dve.wait_ge(s["scores_filled"], 16 * b + i + 1)
                            to = (mx_raw if causal else mx)[:, g, half, k, :]
                            w = 384 if causal else 512
                            dve.tensor_reduce(to, ps[i % 2][:, 0:w].rearrange("p (a k) -> p a k", a=blocks),
                                              AX.X, ALU.max).then_inc(s["maxes"], 1)
                    if causal:
                        dve.wait_ge(s["maxes"], 16 * b + 8 * (g + 1))
                        raw = mx_raw[:, g].rearrange("p h k a -> p (h k) a")
                        out = mx[:, g].rearrange("p h k a -> p (h k) a")
                        dve.tensor_copy(out[:, :, 0], raw[:, :, 0])
                        dve.tensor_tensor(out[:, :, 1], raw[:, :, 1], raw[:, :, 2], ALU.max
                                          ).then_inc(s["mx_ready"], 1)

                def stacks(b, par, which):
                    for j in which:
                        dve.wait_ge(s["cols_filled"], 8 * b + 2 * j + 2)
                        st, u = (q_st, k_st)[j // 2][par], 2 * (j % 2) + 1
                        dve.tensor_copy(st[:, u * 512:(u + 1) * 512], pa[1][:]).then_inc(s["stacks_dve"], 1)

                def normalise(b):
                    chain_c.at(6 * b)
                    for t in range(ST):
                        dve.wait_ge(s["o_filled"], 2 * b + t + 1)
                        sums = pa[t][:].rearrange("p (g h e) -> p g h e", h=2, e=32)
                        inv = rsum[:, t, :].rearrange("p (g h) -> p g h", h=2)
                        chain_c.mark(dve.reciprocal(inv, sums[:, :, :, HD]))
                        chain_c.wait()
                        if causal:
                            dve.wait_ge(s["ao_out"], 16 * (b + 1))
                            to = ao[:].rearrange("p (h g b d) -> p b g h d", h=2, b=ST, d=HD)[:, t]
                        else:
                            dve.wait_ge(s["at_filled"], b + 1)
                            to = ao[:].rearrange("p (b h g d) -> p b g h d", b=ST, h=2, d=HD)[:, t]
                        dve.tensor_tensor(to, sums[:, :, :, 0:HD],
                                          inv.unsqueeze(3).to_broadcast([P, HB, 2, HD]), ALU.mult
                                          ).then_inc(s["ao_ready"], 1)

                def at_part(b):
                    dve.wait_ge(s["at_hi"], b + 1)
                    dve.tensor_tensor(at_lo[:].rearrange("p k t -> p (k t)"), pa[1][:],
                                      at_hi[:].bitcast(F32).rearrange("p k t -> p (k t)"), ALU.subtract
                                      ).then_inc(s["at_lo"], 1)

                def residual(b):
                    dve.wait_ge(s["out_filled"], b + 1)
                    dve.tensor_tensor(proj[:], pa[1][:].rearrange("p (t f) -> p t f", t=ST),
                                      bias[:, 3].unsqueeze(1).to_broadcast([P, ST, D]), ALU.add
                                      ).then_inc(s["proj_copied"], 1)
                    dve.wait_ge(s["proj_copied"], b + 1)
                    dve.wait_ge(s["xr_loaded"], 16 * (b + 1))
                    dve.wait_ge(s["x_stored"], 16 * (b + 1))
                    dve.scalar_tensor_tensor(x_new[:], proj[:], c.tgate[:, layer:layer + 1], xr[:],
                                             ALU.mult, ALU.add).then_inc(s["out_ready"], 1)
                    dve.wait_ge(s["out_ready"], b + 2)
                    chain_c.at(6 * b + 2)
                    moments_of(chain_c, x_new, stats2, moments2, rstd2, s["moments2_ready"])

                def norm2_apply(b):
                    dve.wait_ge(s["rstd2_ready"], b + 1)
                    dve.wait_ge(s["xn_stored"], 16 * (b + 1))
                    for i in range(ST):
                        last = dve.tensor_scalar(xn2[:, i, :], x_new[:, i, :], moments2[:, i, 0:1],
                                                 rstd2[:, i:i + 1], ALU.subtract, ALU.mult)
                    last.then_inc(s["xn2_ready"], 1)

                def outputs(b, quads):
                    for g in quads:
                        dve.wait_ge(s["pv_done"], 4 * b + g + 1)
                        dve.tensor_copy(o_t[:, g, :], po[g % 2][:, 0:S]).then_inc(s["o_copied"], 1)

                def take_logits(b):
                    dve.wait_ge(s["logits_filled"], b + 1)
                    at = bass.ds(ST * b, ST)
                    dve.tensor_copy(logits[:, at, :], pa[1][:, 0:ST * experts].rearrange(
                        "p (t e) -> p t e", t=ST)).then_inc(s["logits_ready"], 1)

                def step(t, par, has_a, has_c):
                    if has_a:
                        norm_stats(t + 1, 1 - par)
                    if has_c:
                        normalise(t - 1)
                    if has_a:
                        norm_apply(t + 1, 1 - par)
                    maxes(t, 0)
                    if has_a:
                        projections(t + 1, 1 - par)
                    maxes(t, 1)
                    if has_c:
                        at_part(t - 1)
                        residual(t - 1)
                    outputs(t, (0,))
                    if has_c:
                        norm2_apply(t - 1)
                    outputs(t, (1,))
                    if has_c:
                        take_logits(t - 1)
                    if has_a:
                        stacks(t + 1, 1 - par, range(4))
                    outputs(t, (2, 3))

                norm_stats(0, 0)
                norm_apply(0, 0)
                projections(0, 0)
                stacks(0, 0, range(4))
                run(dve, step)
                normalise(B - 1)
                at_part(B - 1)
                residual(B - 1)
                norm2_apply(B - 1)
                take_logits(B - 1)

            @block.tensor
            def _(pe):
                pe.sem_inc(s["at_filled"], 1)

                def turn(bank, x):
                    for k in range(KT):
                        for i in range(ST):
                            last = pe.transpose(bank[:, k * S + i * P:k * S + (i + 1) * P],
                                                x[:, i, k * P:(k + 1) * P], c.ident[:])
                    return last

                def project(bank, hi, lo, n):
                    for i in range(ST):
                        for k in range(KT):
                            at = slice(i * P, (i + 1) * P)
                            last = split_matmul(pe, bank[:, i * D:(i + 1) * D], (hi[:, k, at], lo[:, k, at]),
                                                (w_hi[:, n, k, :], w_lo[:, n, k, :]),
                                                first=k == 0, last=k == KT - 1)
                    return last

                def a1(b, z):
                    pe.wait_ge(s["xn_ready"], b + 1)
                    if z is not None:
                        pe.wait_ge(s["ao_ready"], 2 * z + 2)
                    turn(pa[0], xn).then_inc(s["xt_filled"], 1)
                    pe.wait_ge(s["w_ready"], 4)
                    pe.wait_ge(s["ctx_lo"], b + 1)
                    project(pa[1], ct_hi, ct_lo, 1).then_inc(s["proj_filled"], 1)
                    pe.wait_ge(s["xt_lo"], b + 1)
                    project(pa[0], xt_hi, xt_lo, 0).then_inc(s["proj_filled"], 1)
                    pe.wait_ge(s["qkv_ready"], 3 * b + 1)
                    project(pa[1], ct_hi, ct_lo, 2).then_inc(s["proj_filled"], 1)

                def a2(b, t, has_c, which):
                    for n in which:
                        pe.wait_ge(s["parts_lo"], 2 * b + n + 1)
                        if n == 1 and not causal:
                            pe.wait_ge(s["mask_placed"], b + 1)
                        for u in range(4):
                            j = 2 * n + u // 2
                            if j == 0:
                                if t is None:
                                    pe.wait_ge(s["qkv_ready"], 3 * b + 3)
                                elif has_c and u == 1:
                                    pe.wait_ge(s["logits_ready"], t + 1)
                                elif not has_c:
                                    pe.wait_ge(s["qkv_ready"], 3 * b + 3)
                                    pe.wait_ge(s["m_copied"], 2 * t + 2)
                            else:
                                pe.wait_ge(s["stacks_dve"] if u % 2 else s["stacks_act"], 4 * b + j)
                            for v in range(4):
                                hb = 4 * u + v
                                last = pe.transpose(
                                    pa[u % 2][:, v * P:(v + 1) * P],
                                    cols[n][:, hb // 2, hb % 2].bitcast(F32).rearrange("p h a d -> p (h a d)"),
                                    c.ident[:])
                            last.then_inc(s["cols_filled"], 1)

                def scores(b, par, g, ns=range(4)):
                    q, k = q_st[par], k_st[par]
                    for n in ns:
                        for half in range(2):
                            i = 8 * g + 2 * n + half
                            rows = slice(64 * half, 64 * half + 49)
                            at = (4 * g + n) * S
                            wait(pe, s["maxes"], 16 * b + i - 1)
                            bank = ps[i % 2]
                            if causal:
                                pe.matmul(bank[:, 0:P], q[rows, at:at + P], k[rows, at:at + P],
                                          start=True, stop=False)
                                pe.matmul(bank[:, 0:P], c.ident_b[:], c.mask_q[:], start=False, stop=True)
                                pe.matmul(bank[:, P:3 * P], q[rows, at + P:at + S], k[rows, at:at + S],
                                          start=True, stop=False)
                                last = pe.matmul(bank[:, S:3 * P], c.ident_b[:], c.mask_q[:],
                                                 start=False, stop=True)
                            else:
                                for t in range(ST):
                                    last = pe.matmul(bank[:, t * S:(t + 1) * S],
                                                     q[rows, at + t * P:at + (t + 1) * P],
                                                     k[rows, at:at + S], start=True, stop=True)
                            last.then_inc(s["scores_filled"], 1)

                def turn_maxes(b, g, a):
                    if causal:
                        pe.wait_ge(s["mx_ready"], 2 * b + g + 1)
                    else:
                        pe.wait_ge(s["maxes"], 16 * b + 8 * (g + 1))
                    if g:
                        pe.wait_ge(s["m_copied"], 2 * b + 1)
                    elif a is not None:
                        pe.wait_ge(s["qkv_ready"], 3 * a + 2)
                    pe.transpose(pa[0][0:16, 0:P], mx[:, g].rearrange("p h k t -> p (h k t)"), c.ident[:]
                                 ).then_inc(s["m_filled"], 1)

                def scores_t(b, par, g):
                    q, k = q_st[par], k_st[par]
                    for j in range(4):
                        half, h8, i = j % 2, 2 * g + j // 2, 4 * g + j
                        rows = slice(64 * half, 64 * half + 50)
                        at = h8 * S
                        wait(pe, s["exp_done"], 16 * b + i - 1)
                        bank = pt[i % 2]
                        if causal:
                            pe.matmul(bank[:, 0:S], k[rows, at:at + P], q[rows, at:at + S],
                                      start=True, stop=False)
                            pe.matmul(bank[:, 0:P], c.ident_b[:], c.mask_k[:], start=False, stop=True)
                            pe.matmul(bank[:, S:3 * P], k[rows, at + P:at + S], q[rows, at + P:at + S],
                                      start=True, stop=False)
                            last = pe.matmul(bank[:, S:3 * P], c.ident_b[:], c.mask_k[:],
                                             start=False, stop=True)
                        else:
                            for t in range(ST):
                                last = pe.matmul(bank[:, t * S:(t + 1) * S],
                                                 k[rows, at + t * P:at + (t + 1) * P],
                                                 q[rows, at:at + S], start=True, stop=True)
                        last.then_inc(s["scores_t_filled"], 1)

                def values(b, par, g):
                    pe.wait_ge(s["exp_done"], 16 * b + 4 * g + 4)
                    wait(pe, s["o_copied"], 4 * b + g - 1)
                    for t in range(ST):
                        for j in range(4):
                            h = (j % 2) * HB + 2 * g + j // 2
                            q0, w = (P, P) if causal and t else (0, S)
                            last = pe.matmul(po[g % 2][32 * j:32 * j + 32, q0:q0 + w], v_st[par][:, h, t, :],
                                             probs[(4 * g + j) % 8][:, t * S:t * S + w],
                                             start=t == 0, stop=t == ST - 1)
                    last.then_inc(s["pv_done"], 1)

                def c0(b, t):
                    pe.wait_ge(s["o_copied"], 4 * b + 4)
                    pe.wait_ge(s["stacks_act"], 4 * t + 4)
                    pe.wait_ge(s["stacks_dve"], 4 * t + 4)
                    pe.wait_ge(s["logits_ready"], b + 1)
                    for n in range(ST):
                        for g in range(4):
                            last = pe.transpose(pa[n][:, g * P:(g + 1) * P], o_t[:, g, n * P:(n + 1) * P],
                                                c.ident[:])
                        last.then_inc(s["o_filled"], 1)

                def c1a(b, a):
                    if causal:
                        pe.wait_ge(s["ao_in"], 16 * (b + 1))
                    pe.wait_ge(s["ao_ready"], 2 * b + 2)
                    if a is not None:
                        pe.wait_ge(s["qkv_ready"], 3 * a + 3)
                    x = ao_tok if causal else ao[:].rearrange("p (t f) -> p t f", t=ST)
                    turn(pa[1], x).then_inc(s["at_filled"], 1)

                def c1b(b):
                    pe.wait_ge(s["at_lo"], b + 1)
                    project(pa[1], at_hi, at_lo, 3).then_inc(s["out_filled"], 1)

                def c2(b, t):
                    pe.wait_ge(s["xn2_ready"], b + 1)
                    if t is not None:
                        pe.wait_ge(s["m_copied"], 2 * t + 2)
                    turn(pa[0], xn2).then_inc(s["xn2_t_filled"], 1)
                    pe.wait_ge(s["xn2_t_ready"], b + 1)
                    for i in range(ST):
                        for k in range(KT):
                            last = pe.matmul(pa[1][:, i * experts:(i + 1) * experts],
                                             xn2_t[:, k, i * P:(i + 1) * P], rw[:, k, :],
                                             start=k == 0, stop=k == KT - 1)
                    last.then_inc(s["logits_filled"], 1)

                def step(t, par, has_a, has_c):
                    a = t + 1 if has_a else None
                    if has_c:
                        c0(t - 1, t)
                    pe.wait_ge(s["stacks_act"], 4 * t + 4)
                    pe.wait_ge(s["stacks_dve"], 4 * t + 4)
                    scores(t, par, 0)
                    if has_a:
                        a1(t + 1, t - 1 if has_c else None)
                    scores(t, par, 1, (0, 1))
                    if not has_a:
                        pe.wait_ge(s["ao_ready"], 2 * t)
                    turn_maxes(t, 0, a)
                    scores(t, par, 1, (2, 3))
                    if has_c:
                        c1a(t - 1, a)
                    turn_maxes(t, 1, a)
                    pe.wait_ge(s["m_placed0"], 32 * (t + 1))
                    scores_t(t, par, 0)
                    if has_c:
                        c1b(t - 1)
                    scores_t(t, par, 1)
                    if causal:
                        pe.wait_ge(s["bounced_in2"], 16 * (t + 1))
                    else:
                        pe.wait_ge(s["qkv_ready"], 3 * t + 3)
                    values(t, par, 0)
                    pe.wait_ge(s["m_placed1"], 32 * (t + 1))
                    scores_t(t, par, 2)
                    values(t, par, 1)
                    if has_c:
                        c2(t - 1, t)
                    if has_a:
                        a2(t + 1, t, has_c, (0,))
                    scores_t(t, par, 3)
                    if has_a:
                        a2(t + 1, t, has_c, (1,))
                    values(t, par, 2)
                    values(t, par, 3)

                a1(0, None)
                a2(0, None, False, (0, 1))
                run(pe, step)
                c0(B - 1, B - 1)
                c1a(B - 1, None)
                c1b(B - 1)
                c2(B - 1, None)


def route(nc, c, layer, logits, experts):
    top2 = layer == 0
    E, cap = experts, SLOTS // experts
    HI = cap // 16
    GE = P // HI
    CT = 4
    BITS = 30
    with ExitStack() as ctx:
        def sb(name, shape, dt=F32):
            return ctx.enter_context(nc.sbuf_tensor(f"{name}_r{layer}", shape, dt))

        def sem(name):
            return nc.alloc_semaphore(name=f"{name}_r{layer}")

        iota_hi_i, iota_hi = sb("iota_hi_i", [P, HI], I32), sb("iota_hi", [P, HI])
        ids_i, ids = sb("ids_i", [P, NT], I32), sb("ids", [P, NT])
        spare_p, spare_i, spare = sb("spare_p", [P, 16], I32), sb("spare_i", [P, 16], I32), sb("spare", [P, 16])
        before, ones = sb("before", [P, P]), sb("ones", [P, P])
        diag = sb("diag", [P, GE])
        rank_e = sb("rank_e", [P, E])
        not_first = sb("not_first", [P, E, NT])
        rb = sb("rb", [P, E])
        lg, tmp, tmp2 = sb("lg", [P, NT, E]), sb("tmp", [P, NT, E]), sb("tmp2", [P, NT, E])
        best, best2, pick = sb("best", [P, NT]), sb("best2", [P, NT]), sb("pick", [P, NT])
        ratio, p1, p2 = sb("ratio", [P, NT]), sb("p1", [P, NT]), sb("p2", [P, NT])
        one1, one2 = sb("one1", [P, NT, E]), sb("one2", [P, NT, E])
        sel, wt = sb("sel", [P, NT, E]), sb("wt", [P, NT, E])
        totals, through = sb("totals", [P, E, NT]), sb("through", [P, E, NT])
        pos, pos_i = sb("pos", [P, NT, E]), sb("pos_i", [P, NT, E], I32)
        hi_i, lo_i = sb("hi_i", [P, NT, E], I32), sb("lo_i", [P, NT, E], I32)
        hi_f, lo_f = sb("hi_f", [P, NT, E]), sb("lo_f", [P, NT, E])
        one_hi = [sb(f"one_hi{i}", [P, CT, E, HI]) for i in range(2)]
        one_lo = [sb(f"one_lo{i}", [P, CT, E, 3, 16]) for i in range(2)]
        spread, lists = sb("spread", [P, GE, 48]), sb("lists", [P, 2, 48])
        idx_f, idx_i = sb("idx_f", [P, 2, 16]), sb("idx_i", [P, 2, 16], I32)
        if not top2:
            thr, cand = sb("thr", [P, E], I32), sb("cand", [P, E], I32)
            part, add = sb("part", [P, E]), sb("add", [P, E], I32)
            need = sb("need", [P, E])

        tables, loaded = sem("tables"), sem("loaded")
        step_done, exp_ready = sem("step_done"), sem("exp_ready")
        counted, count_in = sem("counted"), sem("count_in")
        rows_ready, rows_used = sem("rows_ready"), sem("rows_used")
        lists_out, lists_in = sem("lists_out"), sem("lists_in")
        lists_ready = sem("lists_ready")
        sums, lists_bank = c.banks[0], c.banks[1:3]
        counts = {"n": 0}

        with nc.Block() as block:

            @block.sync
            def _(sp):
                if top2:
                    sp.dma_start(rb[:], bcast(c.router_b, P)).then_inc(loaded, 16)
                sp.wait_ge(lists_ready, 1)
                sp.dma_start(c.idx_dram.rearrange("(g p l) -> p g l", g=2, l=16), idx_i[:]).then_inc(lists_out, 16)
                sp.dma_start(c.wt_dram.rearrange("(g p l) -> p g l", g=2, l=16), lists[:, :, 16:32]
                             ).then_inc(lists_out, 16)
                sp.wait_ge(lists_out, 32)
                with nc.allow_non_contiguous_dma(reason="4096 words of lists, once"):
                    sp.dma_start(c.idx[:], c.idx_dram.rearrange("(t p) -> p t", p=P)).then_inc(lists_in, 16)
                    sp.dma_start(c.wt[:], c.wt_dram.rearrange("(t p) -> p t", p=P)).then_inc(lists_in, 16)
                sp.wait_ge(lists_in, 32)

            @block.gpsimd
            def _(pool):
                pool.iota(iota_hi_i[:], [[1, HI]], base=0, channel_multiplier=0).then_inc(tables, 1)
                pool.iota(ids_i[:], [[P, NT]], base=0, channel_multiplier=1).then_inc(tables, 1)
                pool.iota(spare_p[:], [[1, 16]], base=0, channel_multiplier=16).then_inc(tables, 1)
                pool.memset(before[:], 1.0).then_inc(tables, 1)
                pool.memset(ones[:], 1.0).then_inc(tables, 1)
                pool.memset(diag[:], 1.0).then_inc(tables, 1)
                for e in range(E):
                    pool.memset(rank_e[:, e:e + 1], float(E - e)).then_inc(tables, 1)
                pool.memset(not_first[:], 1.0).then_inc(tables, 1)
                pool.wait_ge(tables, 7 + E)
                pool.memset(not_first[:, :, 0:1], 0.0).then_inc(tables, 1)
                pool.affine_select(out=before[:], in_=before[:], compare_op=ALU.is_gt, fill=0.0, base=0,
                                   pattern=[[1, P]], channel_multiplier=-1).then_inc(tables, 1)
                pool.affine_select(out=diag[:], in_=diag[:], compare_op=ALU.is_ge, fill=0.0, base=0,
                                   pattern=[[-HI, GE]], channel_multiplier=1).then_inc(tables, 1)
                pool.wait_ge(tables, 10 + E)
                pool.affine_select(out=diag[:], in_=diag[:], compare_op=ALU.is_ge, fill=0.0, base=HI - 1,
                                   pattern=[[HI, GE]], channel_multiplier=-1).then_inc(tables, 1)
                pool.wait_ge(tables, 11 + E)

            @block.scalar
            def _(act):
                act.wait_ge(exp_ready, 1)
                if top2:
                    act.activation(ratio[:], ratio[:], ACT.Exp).then_inc(exp_ready, 1)
                else:
                    act.activation(lg[:], lg[:], ACT.Exp).then_inc(exp_ready, 1)

            @block.tensor
            def _(pe):
                pe.wait_ge(tables, 11 + E)
                flat = "p a b -> p (a b)"
                if not top2:
                    for n in range(BITS + 1):
                        pe.wait_ge(count_in, n + 1)
                        pe.matmul(sums[:, 0:E], ones[:], part[:], start=True, stop=True).then_inc(counted, 1)
                for n in range(1 if top2 else 2):
                    pe.wait_ge(count_in, n + 1 + (0 if top2 else BITS + 1))
                    x = (sel if n or top2 else tmp)[:].rearrange(flat)
                    pe.matmul(c.banks[3][:, 0:NT * E], before[:], x, start=True, stop=True)
                    pe.matmul(c.banks[4][:, 0:NT * E], ones[:], x, start=True, stop=True).then_inc(counted, 1)
                for q in range(NT // CT):
                    pe.wait_ge(rows_ready, q + 1)
                    for g in range(2):
                        for t in range(CT):
                            last = pe.matmul(lists_bank[g][:, 0:GE * 48],
                                             one_hi[q % 2][:, t, g * GE:(g + 1) * GE].rearrange(flat),
                                             one_lo[q % 2][:, t, g * GE:(g + 1) * GE].rearrange(
                                                 "p e v l -> p (e v l)"),
                                             start=q == 0 and t == 0, stop=q == NT // CT - 1 and t == CT - 1)
                    last.then_inc(rows_used, 1)

            @block.vector
            def _(dve):
                def link(instruction):
                    counts["n"] += 1
                    instruction.then_inc(step_done, 1)
                    dve.wait_ge(step_done, counts["n"])

                def over_e(x):
                    return x.unsqueeze(2).to_broadcast([P, NT, E])

                def over_t(x):
                    return x.unsqueeze(1).to_broadcast([P, NT, E])

                dve.wait_ge(tables, 11 + E)
                dve.tensor_copy(iota_hi[:], iota_hi_i[:])
                dve.tensor_copy(ids[:], ids_i[:])
                link(dve.tensor_scalar(spare_i[:], spare_p[:], cap - 1, None, ALU.bitwise_and))
                link(dve.tensor_scalar(spare[:], spare_i[:], float(N), None, ALU.add))
                gate = c.tgate[:, 2 + layer:3 + layer]
                if top2:
                    dve.wait_ge(loaded, 16)
                    link(dve.tensor_tensor(lg[:], logits, over_t(rb[:]), ALU.add))

                    def first_best(x, top, one):
                        link(dve.tensor_reduce(top[:], x[:], AX.X, ALU.max))
                        link(dve.tensor_tensor(tmp[:], x[:], over_e(top[:]), ALU.is_equal))
                        link(dve.tensor_tensor(tmp[:], tmp[:], over_t(rank_e[:]), ALU.mult))
                        link(dve.tensor_reduce(pick[:], tmp[:], AX.X, ALU.max))
                        link(dve.tensor_tensor(one[:], tmp[:], over_e(pick[:]), ALU.is_equal))

                    first_best(lg, best, one1)
                    link(dve.scalar_tensor_tensor(tmp2[:], one1[:], -3e38, lg[:], ALU.mult, ALU.add))
                    first_best(tmp2, best2, one2)
                    dve.tensor_tensor(ratio[:], best2[:], best[:], ALU.subtract).then_inc(exp_ready, 1)
                    dve.wait_ge(exp_ready, 2)
                    link(dve.tensor_scalar(p1[:], ratio[:], 1.0, None, ALU.add))
                    link(dve.reciprocal(p1[:], p1[:]))
                    link(dve.tensor_tensor(p2[:], ratio[:], p1[:], ALU.mult))
                    link(dve.tensor_tensor(wt[:], one1[:], over_e(p1[:]), ALU.mult))
                    link(dve.tensor_tensor(tmp[:], one2[:], over_e(p2[:]), ALU.mult))
                    link(dve.tensor_tensor(wt[:], wt[:], tmp[:], ALU.add))
                    link(dve.tensor_scalar(wt[:], wt[:], gate, None, ALU.mult))
                    counts["n"] += 0
                    dve.tensor_tensor(sel[:], one1[:], one2[:], ALU.add).then_inc(count_in, 1)
                else:
                    link(dve.tensor_reduce(best[:], logits, AX.X, ALU.max))
                    dve.tensor_tensor(lg[:], logits, over_e(best[:]), ALU.subtract).then_inc(exp_ready, 1)
                    dve.wait_ge(exp_ready, 2)
                    link(dve.tensor_reduce(best2[:], lg[:], AX.X, ALU.add))
                    link(dve.reciprocal(best2[:], best2[:]))
                    link(dve.tensor_tensor(lg[:], lg[:], over_e(best2[:]), ALU.mult))
                    link(dve.memset(thr[:], 0))
                    for n in range(BITS + 1):
                        last = n == BITS
                        if not last:
                            link(dve.tensor_scalar(cand[:], thr[:], 1 << (BITS - 1 - n), None, ALU.bitwise_or))
                        link(dve.tensor_tensor(tmp[:], lg[:], over_t((thr if last else cand)[:].bitcast(F32)),
                                               ALU.is_gt if last else ALU.is_ge))
                        dve.tensor_reduce(part[:], tmp[:].rearrange("p t e -> p e t"), AX.X, ALU.add
                                          ).then_inc(count_in, 1)
                        dve.wait_ge(counted, n + 1)
                        if not last:
                            link(dve.tensor_scalar(add[:], sums[:, 0:E], float(cap), float(1 << (BITS - 1 - n)),
                                                   ALU.is_ge, ALU.mult))
                            link(dve.tensor_tensor(thr[:], thr[:], add[:], ALU.bitwise_or))
                    link(dve.tensor_scalar(need[:], sums[:, 0:E], -1.0, float(cap), ALU.mult, ALU.add))
                    link(dve.tensor_copy(sel[:], tmp[:]))
                    dve.tensor_tensor(tmp[:], lg[:], over_t(thr[:].bitcast(F32)), ALU.is_equal
                                      ).then_inc(count_in, 1)
                    dve.wait_ge(count_in, BITS + 2)
                    link(dve.tensor_scalar(wt[:], lg[:], gate, None, ALU.mult))

                def ranks(n):
                    dve.wait_ge(counted, n)
                    link(dve.tensor_copy(totals[:], c.banks[4][:, 0:NT * E].rearrange("p (t e) -> p e t", e=E)))
                    link(dve.tensor_tensor_scan(through[:].rearrange("p e t -> p (e t)"),
                                                not_first[:].rearrange("p e t -> p (e t)"),
                                                totals[:].rearrange("p e t -> p (e t)"), 0.0, ALU.mult, ALU.add))
                    link(dve.tensor_tensor(through[:], through[:], totals[:], ALU.subtract))
                    link(dve.tensor_tensor(pos[:], c.banks[3][:, 0:NT * E].rearrange("p (t e) -> p t e", e=E),
                                           through[:].rearrange("p e t -> p t e"), ALU.add))

                if top2:
                    ranks(1)
                    link(dve.tensor_scalar(tmp[:], pos[:], float(cap), None, ALU.is_lt))
                    link(dve.tensor_tensor(sel[:], sel[:], tmp[:], ALU.mult))
                else:
                    ranks(BITS + 2)
                    link(dve.tensor_tensor(pos[:], pos[:], over_t(need[:]), ALU.is_lt))
                    link(dve.tensor_tensor(tmp[:], tmp[:], pos[:], ALU.mult))
                    dve.tensor_tensor(sel[:], sel[:], tmp[:], ALU.add).then_inc(count_in, 1)
                    ranks(BITS + 3)
                link(dve.tensor_scalar(tmp[:], sel[:], -4096.0, 4096.0, ALU.mult, ALU.add))
                link(dve.tensor_tensor(pos_i[:], pos[:], tmp[:], ALU.add))
                link(dve.tensor_scalar(hi_i[:], pos_i[:], 4, None, ALU.logical_shift_right))
                link(dve.tensor_scalar(lo_i[:], pos_i[:], 15, None, ALU.bitwise_and))
                link(dve.tensor_copy(hi_f[:], hi_i[:]))
                link(dve.tensor_copy(lo_f[:], lo_i[:]))
                for q in range(NT // CT):
                    at = slice(q * CT, (q + 1) * CT)
                    if q >= 2:
                        dve.wait_ge(rows_used, q - 1)
                    flat = "p t e -> p (t e)"
                    n = CT * E
                    rows = one_lo[q % 2][:].rearrange("p t e v l -> p (t e) v l")
                    dve.tensor_tensor(one_hi[q % 2][:].rearrange("p t e h -> p (t e) h"),
                                      hi_f[:, at].rearrange(flat).unsqueeze(2).to_broadcast([P, n, HI]),
                                      iota_hi[:].unsqueeze(1).to_broadcast([P, n, HI]), ALU.is_equal)
                    link(dve.tensor_tensor(rows[:, :, 2],
                                           lo_f[:, at].rearrange(flat).unsqueeze(2).to_broadcast([P, n, 16]),
                                           iota_hi[:, 0:16].unsqueeze(1).to_broadcast([P, n, 16]), ALU.is_equal))
                    dve.tensor_tensor(one_lo[q % 2][:, :, :, 0, :], one_lo[q % 2][:, :, :, 2, :],
                                      ids[:, at].unsqueeze(2).unsqueeze(3).to_broadcast([P, CT, E, 16]), ALU.mult)
                    dve.tensor_tensor(rows[:, :, 1], rows[:, :, 2],
                                      wt[:, at].rearrange(flat).unsqueeze(2).to_broadcast([P, n, 16]), ALU.mult
                                      ).then_inc(rows_ready, 1)
                dve.wait_ge(rows_used, NT // CT)
                for g in range(2):
                    link(dve.tensor_tensor(spread[:], lists_bank[g][:, 0:GE * 48].rearrange(
                        "p (e v) -> p e v", e=GE), diag[:].unsqueeze(2).to_broadcast([P, GE, 48]), ALU.mult))
                    link(dve.tensor_reduce(lists[:, g], spread[:].rearrange("p e v -> p v e"), AX.X, ALU.add))
                link(dve.tensor_scalar(idx_f[:], lists[:, :, 32:48], -1.0, 1.0, ALU.mult, ALU.add))
                link(dve.tensor_tensor(idx_f[:], idx_f[:], spare[:].unsqueeze(1).to_broadcast([P, 2, 16]), ALU.mult))
                link(dve.tensor_tensor(idx_f[:], idx_f[:], lists[:, :, 0:16], ALU.add))
                dve.tensor_copy(idx_i[:], idx_f[:]).then_inc(lists_ready, 1)
                dve.wait_ge(lists_ready, 1)


def experts(nc, c, kind, E, T, CH, weights, x_rows, dst, base=None):
    shared = kind == "shared"
    M = 4 * CH
    U = M + 1
    TW = T * P
    W = 3072
    PIECE = W // 4
    YB = 2 if T == 2 else 1
    gate_fn = ACT.Silu if kind == "top2" else ACT.Gelu
    with ExitStack() as ctx:
        def sb(name, shape, dt=F32):
            return ctx.enter_context(nc.sbuf_tensor(f"{name}_{kind}", shape, dt))

        def sem(name):
            return nc.alloc_semaphore(name=f"{name}_{kind}")

        wn = 1 if shared else 2
        w_raw = [sb(f"w_raw{i}", [P, W]) for i in range(wn)]
        w_hi = [sb(f"w_hi{i}", [P, W], F32R) for i in range(wn)]
        w_lo = [sb(f"w_lo{i}", [P, W], F32R) for i in range(wn)]
        xg = [sb(f"xg{i}", [P, T, D]) for i in range(2)]
        x_hi = [sb(f"x_hi{i}", [P, KT, TW], F32R) for i in range(2)]
        x_lo = [sb(f"x_lo{i}", [P, KT, TW], F32R) for i in range(2)]
        gated = [sb(f"gated{i}", [P, TW]) for i in range(2)]
        h = [sb(f"h{i}", [P, TW]) for i in range(2)]
        h_hi = [sb(f"h_hi{i}", [P, TW], F32R) for i in range(2)]
        h_lo = [sb(f"h_lo{i}", [P, TW], F32R) for i in range(2)]
        ys = [sb(f"ys{i}", [P, T, D]) for i in range(2)]
        if shared:
            res = [sb(f"res{i}", [P, T, D]) for i in range(2)]
        else:
            from_rows = [sb(f"from_rows{i}", [P, T], I32) for i in range(2)]
            to_rows = [sb(f"to_rows{i}", [P, T], I32) for i in range(2)]
            wt = [sb(f"wt{i}", [P, T]) for i in range(2)]

        s = Semaphores(sem)
        y_credit = YB * T

        def use_ab(e, m, left):
            return e * U + 1 + m + (1 if m == M - 1 and left else 0)

        def pair_of(par, m, left):
            return c.banks[2 * (use_ab(par, m, left) % 2):][:2]

        def turn_pair(par):
            return (par * U + M) % 2

        def a_w(w, k, m):
            return w[:, k * 512 + m * P:k * 512 + (m + 1) * P]

        def b_w(w, k, m):
            return w[:, 1024 + k * 512 + m * P:1024 + k * 512 + (m + 1) * P]

        def o_w(w, m):
            return w[:, 2048 + m * D:2048 + (m + 1) * D]

        def chunk_par(par, cc):
            return 0 if shared else (par * CH + cc) % 2

        def piece_of(e, par, m, left):
            n, buf, j = e * CH + m // 4, chunk_par(par, m // 4), m % 4
            if j == 0:
                return n, buf, 3
            if m // 4 == CH - 1 and not left:
                return None
            return n + 1, 1 - buf, j - 1

        with nc.Block() as block:

            @block.sync
            def _(sp):
                def load_w(chunk, buf):
                    sp.dma_start(w_raw[buf][:], weights[bass.ds(chunk, 1)].rearrange("o p w -> p (o w)")
                                 ).then_inc(s["w_loaded"], 16)

                load_w(0, 0)
                if shared:
                    for e in range(E):
                        par = e % 2
                        if e >= 2:
                            sp.wait_ge(s["x_turned"], e)
                        sp.dma_start(xg[par][:], c.row_group(x_rows, e, T)).then_inc(s[f"rows_in{par}"], 16)
                        if e >= 2:
                            sp.wait_ge(s["y_read"], y_credit + T * (e - 1))
                            sp.dma_start(c.row_group(dst, e - 2, T), ys[par][:]).then_inc(s[f"stored{par}"], 16)
                        sp.dma_start(res[par][:], c.row_group(base, e, T)).then_inc(s[f"res_in{par}"], 16)
                    for e in range(E - 2, E):
                        sp.wait_ge(s["y_read"], y_credit + T * (e + 1))
                        sp.dma_start(c.row_group(dst, e, T), ys[e % 2][:]).then_inc(s[f"stored{e % 2}"], 16)
                    sp.wait_ge(s["stored0"], 16 * (E // 2))
                    sp.wait_ge(s["stored1"], 16 * (E // 2))
                else:
                    sp.wait_ge(s["w_loaded"], 16)
                    load_w(1, 1)

                    def refill(n, buf):
                        sp.wait_ge(s["w_lo"], 4 * (n + 1))
                        c.settle(sp)
                        sp.wait_ge(s["w_loaded"], 16 * (n + 2))
                        c.settle(sp)
                        load_w(n + 2, buf)

                    with sp.Fori(0, E // 2 - 1) as i:
                        for j in range(2 * CH):
                            refill(2 * CH * i + j, j % 2)
                    for n in range((E - 2) * CH, E * CH - 2):
                        refill(n, n % 2)
                    sp.wait_ge(s["w_loaded"], 16 * E * CH)

            @block.gpsimd
            def _(pool):
                if shared:
                    return

                def gather(e, par):
                    pool.tensor_copy(from_rows[par][:], c.idx[:, bass.ds(e * T, T)]).then_inc(s["from_copied"], 1)
                    pool.wait_ge(s["from_copied"], e + 1)
                    c.settle(pool)
                    for t in range(T):
                        pool.indirect_dma_start(
                            out=xg[par][:, t, :], out_offset=None, in_=x_rows,
                            in_offset=bass.IndirectOffsetOnAxis(
                                ap=from_rows[par][:, t:t + 1].bitcast(U32), axis=0)
                        ).then_inc(s[f"rows_in{par}"], 16)

                pool.sem_inc(s["ys_free"], 2)
                gather(0, 0)
                gather(1, 1)

                def expert(e, par, k, left):
                    pool.tensor_copy(wt[par][:], c.wt[:, bass.ds(e * T, T)]).then_inc(s["wt_copied"], 1)
                    pool.tensor_copy(to_rows[par][:], c.idx[:, bass.ds(e * T, T)]).then_inc(s["to_copied"], 1)
                    if left >= 2:
                        pool.wait_ge(s["x_turned"], e + 2)
                        gather(e + 2, par)
                    pool.wait_ge(s["to_copied"], e + 1)
                    pool.wait_ge(s["y_read"], y_credit + T * (e + 1))
                    c.settle(pool)
                    for t in range(T):
                        pool.indirect_dma_start(
                            out=dst, in_=ys[par][:, t, :], in_offset=None,
                            out_offset=bass.IndirectOffsetOnAxis(
                                ap=to_rows[par][:, t:t + 1].bitcast(U32), axis=0),
                            compute_op=ALU.add).then_inc(s["added"], 16)
                    pool.wait_ge(s["added"], 16 * T * (e + 1))
                    pool.sem_inc(s["ys_free"], 1)

                c.over_experts(pool, E, expert, shared)

            @block.scalar
            def _(act):
                def hi_piece(n, buf, j):
                    at = slice(j * PIECE, (j + 1) * PIECE)
                    if j < 3:
                        act.wait_ge(s["w_loaded"], 16 * (n + 1))
                        wait(act, s["y_done"], 4 * n - 2)
                    act.copy(w_hi[buf][:, at], w_raw[buf][:, at]).then_inc(s["w_hi"], 1)

                def x_part(n, par, pair):
                    act.wait_ge(s["x_turned"], n + 2)
                    if T == 4:
                        for k in range(KT):
                            last = act.copy(x_hi[par][:, k], c.banks[2 * pair + k][:])
                    else:
                        last = act.copy(x_hi[par][:].rearrange("p k t -> p (k t)"), c.banks[2 * pair][:])
                    last.then_inc(s["x_hi"], 1)

                for j in range(4 if shared else 3):
                    hi_piece(0, 0, j)
                x_part(0, 0, 0)

                def expert(e, par, k, left):
                    for m in range(M):
                        g = e * M + m
                        if m == M - 1 and left:
                            x_part(e + 1, 1 - par, turn_pair(par))
                        act.wait_ge(s["ab_filled"], g + 1)
                        act.activation(gated[m % 2][:], pair_of(par, m, left)[1][:, 0:TW], gate_fn
                                       ).then_inc(s["gate_done"], 1)
                        piece = None if shared else piece_of(e, par, m, left)
                        if piece:
                            hi_piece(*piece)
                        act.wait_ge(s["pair_read"], use_ab(e, m, left) + 2)
                        act.wait_ge(s["y_done"], g + 1)
                        act.copy(h_hi[m % 2][:], h[m % 2][:]).then_inc(s["h_hi"], 1)

                c.over_experts(act, E, expert, shared)

            @block.vector
            def _(dve):
                def lo_piece(n, buf, j):
                    at = slice(j * PIECE, (j + 1) * PIECE)
                    dve.wait_ge(s["w_hi"], 4 * n + j + 1)
                    dve.tensor_tensor(w_lo[buf][:, at], w_raw[buf][:, at], w_hi[buf][:, at].bitcast(F32),
                                      ALU.subtract).then_inc(s["w_lo"], 1)

                def x_part(n, par, pair):
                    dve.wait_ge(s["x_hi"], n + 1)
                    if T == 4:
                        for k in range(KT):
                            last = dve.tensor_tensor(x_lo[par][:, k], c.banks[2 * pair + k][:],
                                                     x_hi[par][:, k].bitcast(F32), ALU.subtract)
                    else:
                        flat = "p k t -> p (k t)"
                        last = dve.tensor_tensor(x_lo[par][:].rearrange(flat), c.banks[2 * pair][:],
                                                 x_hi[par][:].bitcast(F32).rearrange(flat), ALU.subtract)
                    last.then_inc(s["pair_read"], 1)

                dve.sem_inc(s["y_read"], y_credit)
                dve.sem_inc(s["pair_read"], 1)
                for j in range(4 if shared else 3):
                    lo_piece(0, 0, j)
                x_part(0, 0, 0)

                def hidden(e, par, m, left):
                    g = e * M + m
                    dve.wait_ge(s["gate_done"], g + 1)
                    dve.tensor_tensor(h[m % 2][:], pair_of(par, m, left)[0][:, 0:TW], gated[m % 2][:], ALU.mult
                                      ).then_inc(s["pair_read"], 1)
                    piece = None if shared else piece_of(e, par, m, left)
                    if piece:
                        lo_piece(*piece)
                    dve.wait_ge(s["h_hi"], g + 1)
                    dve.tensor_tensor(h_lo[m % 2][:], h[m % 2][:], h_hi[m % 2][:].bitcast(F32), ALU.subtract
                                      ).then_inc(s["h_lo"], 1)

                hidden(0, 0, 0, 1)

                def expert(e, par, k, left):
                    for m in range(1, M):
                        if m == M - 1 and left:
                            x_part(e + 1, 1 - par, turn_pair(par))
                        hidden(e, par, m, left)
                    if left:
                        hidden(e + 1, 1 - par, 0, left - 1)
                    dve.wait_ge(s["y_done"], (e + 1) * M + 2)
                    if shared:
                        dve.wait_ge(s[f"res_in{par}"], 16 * (k + 1))
                        wait(dve, s[f"stored{par}"], 16 * k)
                    else:
                        dve.wait_ge(s["ys_free"], e + 1)
                        dve.wait_ge(s["wt_copied"], e + 1)
                    for t in range(T):
                        bank = c.banks[4 + (par % YB) * T + t][:, 0:D]
                        if shared:
                            dve.scalar_tensor_tensor(ys[par][:, t, :], bank, c.tgate[:, 3:4], res[par][:, t, :],
                                                     ALU.mult, ALU.add).then_inc(s["y_read"], 1)
                        else:
                            dve.tensor_scalar(ys[par][:, t, :], bank, wt[par][:, t:t + 1], None, ALU.mult
                                              ).then_inc(s["y_read"], 1)

                c.over_experts(dve, E, expert, shared)

            @block.tensor
            def _(pe):
                pe.sem_inc(s["y_done"], 2)
                pe.sem_inc(s["x_turned"], 1)

                def turn_rows(par, pair):
                    for k in range(KT):
                        for t in range(T):
                            if T == 4:
                                out = c.banks[2 * pair + k][:, t * P:(t + 1) * P]
                            else:
                                out = c.banks[2 * pair][:, k * TW + t * P:k * TW + (t + 1) * P]
                            last = pe.transpose(out, xg[par][:, t, k * P:(k + 1) * P], c.ident[:])
                    last.then_inc(s["x_turned"], 1)

                rows_count = 16 if shared else 16 * T

                def ab(e, par, m, left):
                    buf = chunk_par(par, m // 4)
                    if m % 4 == 0:
                        pe.wait_ge(s["w_lo"], 4 if shared else 4 * (e * CH + m // 4) + 3)
                    pe.wait_ge(s["pair_read"], use_ab(e, m, left))
                    for bank, part in zip(pair_of(par, m, left), (a_w, b_w)):
                        for k in range(KT):
                            last = split_matmul(pe, bank[:, 0:TW],
                                                (part(w_hi[buf], k, m % 4), part(w_lo[buf], k, m % 4)),
                                                (x_hi[par][:, k], x_lo[par][:, k]), first=k == 0, last=k == KT - 1)
                    last.then_inc(s["ab_filled"], 1)

                def y(e, par, m):
                    buf = chunk_par(par, m // 4)
                    pe.wait_ge(s["h_lo"], e * M + m + 1)
                    if m % 4 == 0 and not shared:
                        pe.wait_ge(s["w_lo"], 4 * (e * CH + m // 4) + 4)
                    if m == 0:
                        pe.wait_ge(s["y_read"], T * (e + 1))
                    for t in range(T):
                        at = slice(t * P, (t + 1) * P)
                        last = split_matmul(pe, c.banks[4 + (par % YB) * T + t][:, 0:D],
                                            (h_hi[m % 2][:, at], h_lo[m % 2][:, at]),
                                            (o_w(w_hi[buf], m % 4), o_w(w_lo[buf], m % 4)),
                                            first=m == 0, last=m == M - 1)
                    last.then_inc(s["y_done"], 1)

                pe.wait_ge(s["rows_in0"], rows_count)
                turn_rows(0, 0)
                pe.wait_ge(s["pair_read"], 2)
                ab(0, 0, 0, 1)
                ab(0, 0, 1, 1)

                def expert(e, par, k, left):
                    for m in range(2, M):
                        if m == M - 1 and left:
                            pe.wait_ge(s[f"rows_in{1 - par}"], rows_count * (k + 1 + par))
                            pe.wait_ge(s["pair_read"], e * U + M)
                            turn_rows(1 - par, turn_pair(par))
                        ab(e, par, m, left)
                        y(e, par, m - 2)
                    for m in range(2):
                        if left:
                            ab(e + 1, 1 - par, m, left - 1)
                        y(e, par, M - 2 + m)

                c.over_experts(pe, E, expert, shared)


class Shared:

    def rows(self, x, b):
        return x[bass.ds(b * S, S), :].rearrange("(t p) f -> p t f", p=P)

    def ctx_rows(self, b):
        return self.ctx_t[bass.ds(b, 1)].rearrange("o p k t -> p (o k) t")

    def tokens(self, x):
        return x.rearrange("(t p) f -> p t f", p=P)

    def row_group(self, x, n, tiles):
        return x[n * tiles * P:(n + 1) * tiles * P, :].rearrange("(t p) f -> p t f", p=P)

    def settle(self, eng):
        eng.sem_inc(self.passed, 1)

    def over_experts(self, eng, count, expert, unrolled):
        if unrolled:
            for e in range(count):
                expert(e, e % 2, e // 2, min(2, count - 1 - e))
            return
        with eng.Fori(0, count // 2 - 1) as i:
            expert(2 * i, 0, i, 2)
            expert(2 * i + 1, 1, i, 2)
        expert(count - 2, 0, count // 2 - 1, 1)
        expert(count - 1, 1, count // 2 - 1, 0)

    def by_position(self, x):
        return x.rearrange("(a t) (u d) -> (t u) a d", a=H * ST, d=HD)


def build(nc, ins, out):
    c = Shared()
    with ExitStack() as ctx:
        c.sems = ctx

        def sb(name, shape, dt=F32):
            return ctx.enter_context(nc.sbuf_tensor(name, shape, dt))

        def sem(name):
            return ctx.enter_context(nc.semaphore(name))

        def dram(name, shape, dt=F32):
            return nc.dram_tensor(name, shape, dt, kind="Internal").ap()

        c.banks = [ctx.enter_context(nc.psum_tensor(f"bank{i}", [P, 512], F32)) for i in range(8)]
        c.ident, c.ident_b = sb("ident", [P, P]), sb("ident_b", [P, P], BF16)
        c.mask_q, c.mask_k = sb("mask_q", [P, P], BF16), sb("mask_k", [P, P], BF16)
        c.minus_half = sb("minus_half", [P, 2])
        c.gates, c.tgate = sb("gates", [P, 4]), sb("tgate", [P, 4])
        c.logits = sb("logits", [P, NT, 16])
        c.passed = sem("passed")
        c.gates_loaded, c.gates_ready = sem("gates_loaded"), sem("gates_ready")
        c.const_set, c.ident_b_ready = sem("const_set"), sem("ident_b_ready")
        c.g_xattn, c.g_ffn = ins["g_xattn"], ins["g_ffn"]
        c.ctx_t = ins["ctx_t"]
        c.router_b = ins["L0_ffn_router_b"]
        c.qkv_dram = [dram(f"{n}_dram", [S, D]) for n in ("q", "k", "v")]
        c.ao_dram = dram("ao_dram", [S, D])
        c.idx_dram, c.wt_dram = dram("idx_dram", [SLOTS], I32), dram("wt_dram", [SLOTS])
        c.idx, c.wt = sb("idx", [P, SLOT_TILES], I32), sb("wt", [P, SLOT_TILES])
        c.zeros_set, c.spare_zeroed = sem("zeros_set"), sem("spare_zeroed")
        x0, xn0 = dram("x0", [N + SPARE, D]), dram("xn0", [N + SPARE, D])
        x1, xn1 = dram("x1", [N, D]), dram("xn1", [N, D])
        c.with_spare = [x0, xn0]

        with nc.sbuf_tensor("zeros", [P, SPARE // P * D], F32) as c.zeros:
            constants(nc, c)
        layer_0 = nc.snapshot_sems()
        attention(nc, c, 0, ins["x"], [ins[f"L0_xattn_{w}"] for w in ("Wq", "Wk", "Wv", "Wp")],
                  [ins[f"L0_xattn_{w}"] for w in ("bq", "bk", "bv", "bp")], None,
                  ins["L0_ffn_router_w"], c.logits[:, :, 0:8], 8, x0, xn0)
        route(nc, c, 0, c.logits[:, :, 0:8], 8)
        experts(nc, c, "top2", 8, 4, 1, ins["L0_ffn"], xn0, x0)
        nc.clear_and_free_semaphores(nc.allocated_since(layer_0))
        nc.all_engine_barrier()
        attention(nc, c, 1, x0, [ins[f"L1_xattn_W_{w}"] for w in "QKVO"],
                  [ins[f"L1_xattn_b_{w}"] for w in "QKVO"], ins["mask"],
                  ins["L1_ffn_gate_w"], c.logits[:, :, 0:16], 16, x1, xn1)
        experts(nc, c, "shared", 4, 4, 1, ins["L1_shared"], xn1, out, x1)
        route(nc, c, 1, c.logits[:, :, 0:16], 16)
        experts(nc, c, "choice", 16, 2, 2, ins["L1_ffn"], xn1, out)


def kernel(**inputs):
    import numpy as np
    import concourse.bacc as bacc
    from concourse.bass_utils import run_bass_kernel_spmd

    def by_row_tile(w):
        return w.reshape(-1, P, w.shape[-1]).transpose(1, 0, 2)

    def chunks(up, gate, down):
        e, _, hid = up.shape
        n = hid // 512
        parts = [w.reshape(e, KT, P, n, 512).transpose(0, 3, 2, 1, 4).reshape(e * n, P, -1) for w in (up, gate)]
        parts.append(down.reshape(e, n, 4, P, D).transpose(0, 1, 3, 2, 4).reshape(e * n, P, -1))
        return np.concatenate(parts, axis=2)

    a = {name: np.asarray(value) for name, value in inputs.items()}
    arrays = {
        "x": a["x"].reshape(N, D),
        "ctx_t": a["ctx_1024"].transpose(0, 2, 1).reshape(B, KT, P, S).transpose(0, 2, 1, 3),
        "mask": a["mask_BxS2_bk0"].reshape(B, ST, P).transpose(2, 0, 1),
        "g_xattn": a["g_xattn"][None], "g_ffn": a["g_ffn"][None],
        "L0_ffn_router_w": by_row_tile(a["L0_ffn_router_w"].T),
        "L0_ffn_router_b": a["L0_ffn_router_b"][None],
        "L1_ffn_gate_w": by_row_tile(a["L1_ffn_gate_w"].T),
        "L0_ffn": chunks(a["L0_ffn_W"], a["L0_ffn_V"], a["L0_ffn_W_out"]),
        "L1_ffn": chunks(a["L1_ffn_Wu"].transpose(0, 2, 1), a["L1_ffn_Wg"].transpose(0, 2, 1),
                         a["L1_ffn_Wd"].transpose(0, 2, 1)),
        "L1_shared": chunks(a["L1_ffn_Su"].T[None], a["L1_ffn_Sg"].T[None], a["L1_ffn_Sd"].T[None]),
    }
    for w in ("Wq", "Wk", "Wv", "Wp"):
        arrays[f"L0_xattn_{w}"] = by_row_tile(a[f"L0_xattn_{w}"].T)
        arrays[f"L0_xattn_b{w[1]}"] = a[f"L0_xattn_b{w[1]}"][None]
    for w in "QKVO":
        arrays[f"L1_xattn_W_{w}"] = by_row_tile(a[f"L1_xattn_W_{w}"])
        arrays[f"L1_xattn_b_{w}"] = a[f"L1_xattn_b_{w}"][None]
    arrays = {name: np.ascontiguousarray(value) for name, value in arrays.items()}

    nc = bacc.Bacc("TRN2", target_bir_lowering=False, num_devices=1)
    ins = {name: nc.dram_tensor(name, value.shape, mybir.dt.from_np(value.dtype), kind="ExternalInput").ap()
           for name, value in arrays.items()}
    out = nc.dram_tensor("out", [N, D], F32, kind="ExternalOutput").ap()
    build(nc, ins, out)
    result = run_bass_kernel_spmd(nc, [arrays], core_ids=[0])
    return result.results[0]["out"].reshape(B, S, D)
```

```python
from contextlib import ExitStack

import concourse.bass as bass
import concourse.mybir as mybir

ACT = mybir.ActivationFunctionType
ALU = mybir.AluOpType
AX = mybir.AxisListType
F32 = mybir.dt.float32
F32R = mybir.dt.float32r
BF16 = mybir.dt.bfloat16
U8 = mybir.dt.uint8
I32 = mybir.dt.int32
U32 = mybir.dt.uint32

P = 128
D = 256
KT = D // P
B = 8
S = 256
ST = S // P
N = B * S
NT = N // P
H = 16
HD = D // H
HB = H // 2
NEG = -float(2 ** 100)
EPS = 1e-5
SLOTS = 4096
SLOT_TILES = SLOTS // P
SPARE = 512


def wait(eng, sem, value):
    if isinstance(value, int) and value <= 0:
        return
    eng.wait_ge(sem, value)


class Steps:

    def __init__(self, eng, sem):
        self.eng, self.sem, self.base, self.n = eng, sem, 0, 0

    def at(self, base):
        self.base, self.n = base, 0

    def mark(self, instruction):
        instruction.then_inc(self.sem, 1)
        self.n += 1

    def wait(self):
        self.eng.wait_ge(self.sem, self.base + self.n)


class Semaphores(dict):

    def __init__(self, take):
        super().__init__()
        self.take = take

    def __missing__(self, name):
        self[name] = self.take(name)
        return self[name]


def split_matmul(pe, out, lhs, rhs, first=True, last=True):
    (lh, ll), (rh, rl) = lhs, rhs
    pe.matmul(out, lh, rh, start=first, stop=False)
    pe.matmul(out, lh, rl, start=False, stop=False)
    return pe.matmul(out, ll, rh, start=False, stop=last)


def bcast(row, n):
    return row.to_broadcast([n, row.shape[-1]])


def constants(nc, c):
    with nc.Block() as block:

        @block.sync
        def _(sp):
            sp.dma_start(c.gates[:, 0:2], bcast(c.g_xattn, P)).then_inc(c.gates_loaded, 16)
            sp.dma_start(c.gates[:, 2:4], bcast(c.g_ffn, P)).then_inc(c.gates_loaded, 16)
            sp.wait_ge(c.zeros_set, 1)
            for x in c.with_spare:
                sp.dma_start(x[N:N + SPARE, :].rearrange("(t p) f -> p t f", p=P),
                             c.zeros[:].rearrange("p (t f) -> p t f", f=D)).then_inc(c.spare_zeroed, 16)

        @block.gpsimd
        def _(pool):
            pool.memset(c.zeros[:], 0.0).then_inc(c.zeros_set, 1)
            pool.memset(c.ident[:], 0.0).then_inc(c.const_set, 1)
            pool.memset(c.mask_q[:], 0.0).then_inc(c.const_set, 1)
            pool.memset(c.mask_k[:], 0.0).then_inc(c.const_set, 1)
            pool.memset(c.minus_half[:], -0.5).then_inc(c.const_set, 1)
            pool.wait_ge(c.const_set, 4)
            pool.affine_select(out=c.ident[:], in_=c.ident[:], compare_op=ALU.not_equal, fill=1.0,
                               base=0, pattern=[[-1, P]], channel_multiplier=1).then_inc(c.const_set, 1)
            pool.affine_select(out=c.mask_q[:], in_=c.mask_q[:], compare_op=ALU.is_ge, fill=NEG,
                               base=0, pattern=[[-1, P]], channel_multiplier=1).then_inc(c.const_set, 1)
            pool.affine_select(out=c.mask_k[:], in_=c.mask_k[:], compare_op=ALU.is_ge, fill=NEG,
                               base=0, pattern=[[1, P]], channel_multiplier=-1).then_inc(c.const_set, 1)
            pool.wait_ge(c.const_set, 7)

        @block.vector
        def _(dve):
            dve.wait_ge(c.const_set, 7)
            dve.tensor_copy(c.ident_b[:], c.ident[:]).then_inc(c.ident_b_ready, 1)
            dve.wait_ge(c.ident_b_ready, 1)


def attention(nc, c, layer, x_src, weights, biases, mask, router, logits, experts, x_dst, xn_dst):
    causal = layer == 0
    with ExitStack() as ctx:
        def sb(name, shape, dt=F32):
            return ctx.enter_context(nc.sbuf_tensor(f"{name}_{layer}", shape, dt))

        def sem(name):
            return nc.alloc_semaphore(name=f"{name}_{layer}")

        w_raw = sb("w_raw", [P, 4, KT, D])
        w_hi = sb("w_hi", [P, 4, KT, D], F32R)
        w_lo = sb("w_lo", [P, 4, KT, D], F32R)
        bias = sb("bias", [P, 4, D])
        rw = sb("rw", [P, KT, experts])
        xb = [sb(f"xb{i}", [P, ST, D]) for i in range(2)]
        ctxf = [sb(f"ctxf{i}", [P, KT, S]) for i in range(2)]
        stats = sb("stats", [P, ST, 6])
        moments = sb("moments", [P, ST, 2])
        rstd = sb("rstd", [P, ST])
        xn = sb("xn", [P, ST, D])
        xt_hi, xt_lo = sb("xt_hi", [P, KT, S], F32R), sb("xt_lo", [P, KT, S], F32R)
        ct_hi, ct_lo = sb("ct_hi", [P, KT, S], F32R), sb("ct_lo", [P, KT, S], F32R)
        qkv_f = [sb(f"{n}_f", [P, ST, D]) for n in ("q", "k", "v")] if causal else None
        qk_pos = [sb(f"{n}_pos", [P, H, ST, HD]) for n in ("q", "k")]
        cols = [sb(f"{n}_cols", [P, HB, ST, 2, 4, HD], F32R) for n in ("q", "k")]
        q_st = [sb(f"q_st{i}", [P, HB * S], F32R) for i in range(2)]
        k_st = [sb(f"k_st{i}", [P, HB * S], F32R) for i in range(2)]
        v_st = [sb(f"v_st{i}", [P, H, ST, 32]) for i in range(2)]
        blocks = 3 if causal else 2
        mx_raw = sb("mx_raw", [P, 2, 2, 4, blocks])
        mx = sb("mx", [P, 2, 2, 4, ST])
        m_rows = [sb(f"m_rows{g}", [16, P], F32R) for g in range(2)]
        probs = [sb(f"probs{i}", [P, ST * S]) for i in range(8)]
        o_t = sb("o_t", [P, 4, S])
        rsum = sb("rsum", [P, ST, H])
        ao = sb("ao", [P, ST * D])
        ao_tok = sb("ao_tok", [P, ST, D]) if causal else None
        at_hi, at_lo = sb("at_hi", [P, KT, S], F32R), sb("at_lo", [P, KT, S], F32R)
        xr = sb("xr", [P, ST, D])
        proj = sb("proj", [P, ST, D])
        x_new = sb("x_new", [P, ST, D])
        stats2 = sb("stats2", [P, ST, 6])
        moments2 = sb("moments2", [P, ST, 2])
        rstd2 = sb("rstd2", [P, ST])
        xn2 = sb("xn2", [P, ST, D])
        xn2_t = sb("xn2_t", [P, KT, S])
        if not causal:
            mask_b = sb("mask_b", [P, B, ST], U8)
            mask_neg = sb("mask_neg", [P, B, ST])
            mask_keep = sb("mask_keep", [P, B, ST])

        ORDER = (1, 0, 2)
        pa, ps, po = c.banks[0:2], c.banks[2:6], c.banks[6:8]

        s = Semaphores(sem)

        def run(eng, step):
            step(0, 0, has_a=True, has_c=False)
            with eng.Fori(0, (B - 2) // 2) as i:
                step(2 * i + 1, 1, has_a=True, has_c=True)
                step(2 * i + 2, 0, has_a=True, has_c=True)
            step(B - 1, 1, has_a=False, has_c=True)

        with nc.Block() as block:

            @block.sync
            def _(sp):
                sp.dma_start(xb[0][:], c.rows(x_src, 0)).then_inc(s["x_loaded"], 16)
                sp.dma_start(ctxf[0][:], c.ctx_rows(0)).then_inc(s["ctx_loaded"], 16)
                for n in (*ORDER, 3):
                    sp.dma_start(w_raw[:, n], weights[n]).then_inc(s[f"w_loaded{n}"], 16)
                for n, b in enumerate(biases):
                    sp.dma_start(bias[:, n], bcast(b, P)).then_inc(s["consts_loaded"], 16)
                sp.dma_start(rw[:], router).then_inc(s["consts_loaded"], 16)
                if not causal:
                    sp.dma_start(mask_b[:], mask).then_inc(s["consts_loaded"], 16)

                def bounce_a(b, par):
                    for rank, n in enumerate(ORDER):
                        sp.wait_ge(s["qkv_ready"], 3 * b + rank + 1)
                        c.settle(sp)
                        wait(sp, s[f"bounced_in{n}"], 16 * b)
                        sp.dma_start(c.tokens(c.qkv_dram[n]), qkv_f[n][:]).then_inc(s[f"bounced_out{n}"], 16)
                    for n in ORDER:
                        sp.wait_ge(s[f"bounced_out{n}"], 16 * (b + 1))
                        c.settle(sp)
                        if n < 2:
                            wait(sp, s["parts_lo"], 2 * b)
                            to = qk_pos[n][:]
                        else:
                            wait(sp, s["pv_done"], 4 * b - 4)
                            to = v_st[par][:, :, :, 0:HD]
                        sp.dma_start(to.rearrange("p h b d -> p (h b) d"), c.by_position(c.qkv_dram[n])
                                     ).then_inc(s[f"bounced_in{n}"], 16)

                def bounce_c(b):
                    sp.wait_ge(s["ao_ready"], 2 * b + 2)
                    sp.dma_start(c.by_position(c.ao_dram),
                                 ao[:].rearrange("p (h d) -> p h d", d=HD)).then_inc(s["ao_out"], 16)
                    sp.wait_ge(s["ao_out"], 16 * (b + 2))
                    sp.wait_ge(s["at_filled"], b + 1)
                    sp.dma_start(ao_tok[:], c.tokens(c.ao_dram)).then_inc(s["ao_in"], 16)

                def store_c(b):
                    sp.wait_ge(s["out_ready"], b + 2)
                    c.settle(sp)
                    sp.dma_start(c.rows(x_dst, b), x_new[:]).then_inc(s["x_stored"], 16)
                    sp.wait_ge(s["xn2_ready"], b + 1)
                    c.settle(sp)
                    sp.dma_start(c.rows(xn_dst, b), xn2[:]).then_inc(s["xn_stored"], 16)

                def load_residual(b):
                    sp.wait_ge(s["out_ready"], b + 1)
                    c.settle(sp)
                    sp.dma_start(xr[:], c.rows(x_src, b)).then_inc(s["xr_loaded"], 16)

                def step(t, par, has_a, has_c):
                    if has_a:
                        nxt = (t + 2) % B
                        sp.wait_ge(s["xn_ready"], t + 1)
                        c.settle(sp)
                        sp.wait_ge(s["x_loaded"], 16 * (t + 2))
                        c.settle(sp)
                        sp.dma_start(xb[par][:], c.rows(x_src, nxt)).then_inc(s["x_loaded"], 16)
                        sp.wait_ge(s["ctx_lo"], t + 1)
                        c.settle(sp)
                        sp.wait_ge(s["ctx_loaded"], 16 * (t + 2))
                        c.settle(sp)
                        sp.dma_start(ctxf[par][:], c.ctx_rows(nxt)).then_inc(s["ctx_loaded"], 16)
                    if has_c:
                        load_residual(t - 1)
                        if causal:
                            bounce_c(t - 1)
                    if has_a:
                        if causal:
                            bounce_a(t + 1, 1 - par)
                    if has_c:
                        store_c(t - 1)

                sp.wait_ge(s["x_loaded"], 16)
                sp.dma_start(xb[1][:], c.rows(x_src, 1)).then_inc(s["x_loaded"], 16)
                sp.wait_ge(s["ctx_loaded"], 16)
                sp.dma_start(ctxf[1][:], c.ctx_rows(1)).then_inc(s["ctx_loaded"], 16)
                sp.sem_inc(s["x_stored"], 16)
                sp.sem_inc(s["xn_stored"], 16)
                sp.sem_inc(s["ao_out"], 16)
                if causal:
                    bounce_a(0, 0)
                run(sp, step)
                load_residual(B - 1)
                if causal:
                    bounce_c(B - 1)
                store_c(B - 1)
                sp.wait_ge(c.spare_zeroed, 16 * len(c.with_spare))
                sp.wait_ge(s["x_stored"], 16 * (B + 1))
                sp.wait_ge(s["xn_stored"], 16 * (B + 1))
                sp.wait_ge(s["x_loaded"], 16 * (B + 1))
                sp.wait_ge(s["ctx_loaded"], 16 * (B + 1))

            @block.gpsimd
            def _(pool):
                for v in v_st:
                    pool.memset(v[:], 1.0).then_inc(s["presets"], 1)
                for n in range(2):
                    pool.memset(cols[n][:].bitcast(F32), 0.0).then_inc(s["presets"], 1)
                pool.wait_ge(s["presets"], 4)
                pool.memset(cols[0][:, :, :, :, 3, 0:1].bitcast(F32).rearrange("p a b h o -> p (a b h) o"), 1.0
                            ).then_inc(s["presets"], 1)
                pool.memset(cols[1][:, :, :, :, 3, 1:2].bitcast(F32).rearrange("p a b h o -> p (a b h) o"), 1.0
                            ).then_inc(s["presets"], 1)
                pool.wait_ge(s["presets"], 6)
                if not causal:
                    pool.wait_ge(s["mask_ready"], 1)

                def norm(b):
                    pool.wait_ge(s["moments_ready"], b + 1)
                    pool.tensor_tensor(rstd[:], rstd[:], c.minus_half[:], ALU.pow).then_inc(s["rstd_ready"], 1)

                def part_a(b, par):
                    pool.wait_ge(s["ctx_hi"], b + 1)
                    pool.tensor_tensor(ct_lo[:], ctxf[par][:], ct_hi[:].bitcast(F32), ALU.subtract
                                       ).then_inc(s["ctx_lo"], 1)

                def mask_keys(b):
                    if causal:
                        return
                    pool.wait_ge(s["qkv_ready"], 3 * b + 1)
                    for t in range(ST):
                        last = pool.tensor_tensor(
                            qk_pos[1][:, :, t, :], qk_pos[1][:, :, t, :],
                            mask_keep[:, bass.ds(b, 1), t].unsqueeze(2).to_broadcast([P, H, HD]), ALU.mult)
                    last.then_inc(s["k_masked"], 1)

                def parts_lo(b):
                    for n, (hi, lo) in enumerate(((0, 2), (0, 1))):
                        pool.wait_ge(s["parts_hi"], 2 * b + n + 1)
                        if n == 1 and not causal:
                            pool.tensor_copy(
                                cols[1][:, :, :, :, 3, 0],
                                mask_neg[:, bass.ds(b, 1), :].to_broadcast([P, HB, ST]).unsqueeze(3)
                                .to_broadcast([P, HB, ST, 2])).then_inc(s["mask_placed"], 1)
                        for half in range(2):
                            last = pool.tensor_tensor(
                                cols[n][:, :, :, half, lo, :],
                                qk_pos[n][:, half * HB:(half + 1) * HB, :, :],
                                cols[n][:, :, :, half, hi, :].bitcast(F32), ALU.subtract)
                        last.then_inc(s["parts_lo"], 1)

                def part_c(b):
                    pool.wait_ge(s["moments2_ready"], b + 1)
                    pool.tensor_tensor(rstd2[:], rstd2[:], c.minus_half[:], ALU.pow).then_inc(s["rstd2_ready"], 1)

                def step(t, par, has_a, has_c):
                    if has_a:
                        part_a(t + 1, 1 - par)
                        mask_keys(t + 1)
                        norm(t + 2)
                    if has_c:
                        part_c(t - 1)
                    if has_a:
                        parts_lo(t + 1)

                norm(0)
                part_a(0, 0)
                mask_keys(0)
                parts_lo(0)
                norm(1)
                run(pool, step)
                part_c(B - 1)

            @block.scalar
            def _(act):
                def part_a(b, par):
                    act.wait_ge(s["ctx_loaded"], 16 * (b + 1))
                    wait(act, s["proj_filled"], 3 * b)
                    act.copy(ct_hi[:], ctxf[par][:]).then_inc(s["ctx_hi"], 1)
                    act.wait_ge(s["xt_filled"], b + 1)
                    act.copy(xt_hi[:].rearrange("p k t -> p (k t)"), pa[0][:]).then_inc(s["xt_hi"], 1)

                def parts_hi(b, which):
                    act.wait_ge(s["presets"], 6)
                    for n in which:
                        slots = ((0, 1), (0, 2))[n]
                        if causal:
                            act.wait_ge(s[f"bounced_in{n}"], 16 * (b + 1))
                        else:
                            act.wait_ge(s["k_masked"] if n else s["qkv_ready"], b + 1 if n else 3 * b + 2)
                        wait(act, s["cols_filled"], 8 * b)
                        for slot in slots:
                            for half in range(2):
                                last = act.copy(cols[n][:, :, :, half, slot, :],
                                                qk_pos[n][:, half * HB:(half + 1) * HB, :, :])
                        last.then_inc(s["parts_hi"], 1)

                def maxima(b, par, g):
                    act.wait_ge(s["m_filled"], 2 * b + g + 1)
                    wait(act, s[f"m_placed{g}"], 32 * b)
                    act.mul(m_rows[g][:], po[g][0:16, 0:P], -1.0).then_inc(s["m_copied"], 1)
                    act.wait_ge(s["m_copied"], 2 * b + g + 1)
                    for half in range(2):
                        r = 64 * half + 49
                        act.dma_start(q_st[par][r:r + 1, g * 1024:(g + 1) * 1024].bitcast(F32),
                                      m_rows[g][half * 8:half * 8 + 8, :].bitcast(F32)
                                      ).then_inc(s[f"m_placed{g}"], 16)

                def stacks(b, par, which):
                    for j in which:
                        act.wait_ge(s["cols_filled"], 8 * b + 2 * j + 1)
                        st, u = (q_st, k_st)[j // 2][par], 2 * (j % 2)
                        act.copy(st[:, u * 512:(u + 1) * 512], pa[0][:]).then_inc(s["stacks_act"], 1)

                def exps(b, quads):
                    for g in quads:
                        wait(act, s["pv_done"], 4 * b + g - 1)
                        for j in range(4):
                            i = 4 * g + j
                            act.wait_ge(s["scores_t_filled"], 16 * b + i + 1)
                            w = 384 if causal else 512
                            act.activation(probs[i % 8][:, 0:w], ps[i % 4][:, 0:w], ACT.Exp,
                                           scale=float(HD) ** -0.5).then_inc(s["exp_done"], 1)

                def at_part(b):
                    act.wait_ge(s["at_filled"], b + 2)
                    act.copy(at_hi[:].rearrange("p k t -> p (k t)"), pa[1][:]).then_inc(s["at_hi"], 1)

                def xn2_turned(b):
                    act.wait_ge(s["xn2_t_filled"], b + 1)
                    act.copy(xn2_t[:].rearrange("p k t -> p (k t)"), pa[0][:]).then_inc(s["xn2_t_ready"], 1)

                def step(t, par, has_a, has_c):
                    if has_a:
                        part_a(t + 1, 1 - par)
                    maxima(t, par, 0)
                    if has_c:
                        at_part(t - 1)
                    maxima(t, par, 1)
                    exps(t, (0, 1))
                    if has_a:
                        parts_hi(t + 1, (0,))
                    exps(t, (2,))
                    if has_c:
                        xn2_turned(t - 1)
                    if has_a:
                        parts_hi(t + 1, (1,))
                    if has_a:
                        stacks(t + 1, 1 - par, (0, 1))
                    exps(t, (3,))
                    if has_a:
                        stacks(t + 1, 1 - par, (2, 3))

                def weight_hi(n):
                    act.wait_ge(s[f"w_loaded{n}"], 16)
                    act.copy(w_hi[:, n], w_raw[:, n]).then_inc(s["w_hi_ready"], 1)

                weight_hi(ORDER[0])
                weight_hi(ORDER[1])
                part_a(0, 0)
                weight_hi(ORDER[2])
                weight_hi(3)
                if causal:
                    act.wait_ge(c.gates_loaded, 32)
                    act.activation(c.tgate[:], c.gates[:], ACT.Tanh).then_inc(c.gates_ready, 1)
                parts_hi(0, (0, 1))
                stacks(0, 0, range(4))
                run(act, step)
                at_part(B - 1)
                xn2_turned(B - 1)

            @block.vector
            def _(dve):
                dve.sem_inc(s["out_ready"], 1)
                dve.sem_inc(s["logits_ready"], 1)
                chain_a, chain_c = Steps(dve, s["dve_a"]), Steps(dve, s["dve_c"])

                def weight_lo(rank, n):
                    dve.wait_ge(s["w_hi_ready"], rank + 1)
                    dve.tensor_tensor(w_lo[:, n], w_raw[:, n], w_hi[:, n].bitcast(F32), ALU.subtract
                                      ).then_inc(s["w_ready"], 1)

                dve.wait_ge(s["consts_loaded"], 16 * (5 if causal else 6))
                if not causal:
                    dve.tensor_copy(mask_neg[:], mask_b[:]).then_inc(s["dve_w"], 1)
                    dve.wait_ge(s["dve_w"], 1)
                    dve.tensor_scalar(mask_keep[:], mask_neg[:], -1.0, 1.0, ALU.mult, ALU.add
                                      ).then_inc(s["dve_w"], 1)
                    dve.wait_ge(s["dve_w"], 2)
                    dve.tensor_scalar(mask_neg[:], mask_neg[:], NEG, None, ALU.mult).then_inc(s["mask_ready"], 1)
                    dve.wait_ge(s["mask_ready"], 1)

                def moments_of(chain, x, st, mo, to, ready):
                    for i in range(ST):
                        chain.mark(dve.bn_stats(st[:, i, :], x[:, i, :]))
                    chain.wait()
                    c.settle(dve)
                    for i in range(ST):
                        chain.mark(dve.bn_aggr(mo[:, i, :], st[:, i, :]))
                    chain.wait()
                    dve.tensor_scalar(to[:], mo[:, :, 1], EPS, None, ALU.add).then_inc(ready, 1)

                def norm_stats(b, par):
                    chain_a.at(4 * b)
                    dve.wait_ge(s["x_loaded"], 16 * (b + 1))
                    moments_of(chain_a, xb[par], stats, moments, rstd, s["moments_ready"])

                def norm_apply(b, par):
                    dve.wait_ge(s["rstd_ready"], b + 1)
                    wait(dve, s["xt_filled"], b)
                    for i in range(ST):
                        last = dve.tensor_scalar(xn[:, i, :], xb[par][:, i, :], moments[:, i, 0:1],
                                                 rstd[:, i:i + 1], ALU.subtract, ALU.mult)
                    last.then_inc(s["xn_ready"], 1)

                def low_rows(b):
                    dve.wait_ge(s["xt_hi"], b + 1)
                    dve.tensor_tensor(xt_lo[:].rearrange("p k t -> p (k t)"), pa[0][:],
                                      xt_hi[:].bitcast(F32).rearrange("p k t -> p (k t)"), ALU.subtract
                                      ).then_inc(s["xt_lo"], 1)
                    if isinstance(b, int) and b == 0:
                        weight_lo(2, ORDER[2])
                        weight_lo(3, 3)
                        dve.wait_ge(c.gates_ready, 1)

                def projections(b, par, ranks):
                    for rank in ranks:
                        n = ORDER[rank]
                        dve.wait_ge(s["proj_filled"], 3 * b + rank + 1)
                        bank = pa[(rank + 1) % 2][:]
                        if causal:
                            wait(dve, s[f"bounced_out{n}"], 16 * b)
                            to, row = qkv_f[n][:], bias[:, n].unsqueeze(1).to_broadcast([P, ST, D])
                            bank = bank.rearrange("p (t f) -> p t f", t=ST)
                        else:
                            if n < 2:
                                wait(dve, s["parts_lo"], 2 * b)
                                to = qk_pos[n][:].rearrange("p h b d -> p b h d")
                            else:
                                wait(dve, s["pv_done"], 4 * b - 4)
                                dve.wait_ge(s["presets"], 6)
                                to = v_st[par][:, :, :, 0:HD].rearrange("p h b d -> p b h d")
                            row = (bias[:, n].rearrange("p (h d) -> p h d", d=HD).unsqueeze(1)
                                   .to_broadcast([P, ST, H, HD]))
                            bank = bank.rearrange("p (t h d) -> p t h d", t=ST, d=HD)
                        dve.tensor_tensor(to, bank, row, ALU.add).then_inc(s["qkv_ready"], 1)

                def maxes(b, g, ks):
                    for k in ks:
                        for half in range(2):
                            i = 8 * g + 2 * k + half
                            dve.wait_ge(s["scores_filled"], 16 * b + i + 1)
                            to = (mx_raw if causal else mx)[:, g, half, k, :]
                            w = 384 if causal else 512
                            dve.tensor_reduce(to, ps[i % 4][:, 0:w].rearrange("p (a k) -> p a k", a=blocks),
                                              AX.X, ALU.max).then_inc(s["maxes"], 1)
                    if causal and 3 in ks:
                        dve.wait_ge(s["maxes"], 16 * b + 8 * (g + 1))
                        raw = mx_raw[:, g].rearrange("p h k a -> p (h k) a")
                        out = mx[:, g].rearrange("p h k a -> p (h k) a")
                        dve.tensor_copy(out[:, :, 0], raw[:, :, 0])
                        dve.tensor_tensor(out[:, :, 1], raw[:, :, 1], raw[:, :, 2], ALU.max
                                          ).then_inc(s["mx_ready"], 1)

                def stacks(b, par, which):
                    for j in which:
                        dve.wait_ge(s["cols_filled"], 8 * b + 2 * j + 2)
                        st, u = (q_st, k_st)[j // 2][par], 2 * (j % 2) + 1
                        dve.tensor_copy(st[:, u * 512:(u + 1) * 512], pa[1][:]).then_inc(s["stacks_dve"], 1)

                def normalise(b):
                    chain_c.at(6 * b)
                    for t in range(ST):
                        dve.wait_ge(s["o_filled"], 2 * b + t + 1)
                        sums = po[t][:].rearrange("p (g h e) -> p g h e", h=2, e=32)
                        inv = rsum[:, t, :].rearrange("p (g h) -> p g h", h=2)
                        chain_c.mark(dve.reciprocal(inv, sums[:, :, :, HD]))
                        chain_c.wait()
                        if causal:
                            dve.wait_ge(s["ao_out"], 16 * (b + 1))
                            to = ao[:].rearrange("p (h g b d) -> p b g h d", h=2, b=ST, d=HD)[:, t]
                        else:
                            dve.wait_ge(s["at_filled"], b + 1)
                            to = ao[:].rearrange("p (b h g d) -> p b g h d", b=ST, h=2, d=HD)[:, t]
                        dve.tensor_tensor(to, sums[:, :, :, 0:HD],
                                          inv.unsqueeze(3).to_broadcast([P, HB, 2, HD]), ALU.mult
                                          ).then_inc(s["ao_ready"], 1)

                def at_part(b):
                    dve.wait_ge(s["at_hi"], b + 1)
                    dve.tensor_tensor(at_lo[:].rearrange("p k t -> p (k t)"), pa[1][:],
                                      at_hi[:].bitcast(F32).rearrange("p k t -> p (k t)"), ALU.subtract
                                      ).then_inc(s["at_lo"], 1)

                def residual(b):
                    dve.wait_ge(s["out_filled"], b + 1)
                    dve.tensor_tensor(proj[:], pa[1][:].rearrange("p (t f) -> p t f", t=ST),
                                      bias[:, 3].unsqueeze(1).to_broadcast([P, ST, D]), ALU.add
                                      ).then_inc(s["proj_copied"], 1)
                    dve.wait_ge(s["proj_copied"], b + 1)
                    dve.wait_ge(s["xr_loaded"], 16 * (b + 1))
                    dve.wait_ge(s["x_stored"], 16 * (b + 1))
                    dve.scalar_tensor_tensor(x_new[:], proj[:], c.tgate[:, layer:layer + 1], xr[:],
                                             ALU.mult, ALU.add).then_inc(s["out_ready"], 1)
                    dve.wait_ge(s["out_ready"], b + 2)
                    chain_c.at(6 * b + 2)
                    moments_of(chain_c, x_new, stats2, moments2, rstd2, s["moments2_ready"])

                def norm2_apply(b):
                    dve.wait_ge(s["rstd2_ready"], b + 1)
                    dve.wait_ge(s["xn_stored"], 16 * (b + 1))
                    for i in range(ST):
                        last = dve.tensor_scalar(xn2[:, i, :], x_new[:, i, :], moments2[:, i, 0:1],
                                                 rstd2[:, i:i + 1], ALU.subtract, ALU.mult)
                    last.then_inc(s["xn2_ready"], 1)

                def outputs(b, quads):
                    for g in quads:
                        dve.wait_ge(s["pv_done"], 4 * b + g + 1)
                        dve.tensor_copy(o_t[:, g, :], po[g % 2][:, 0:S]).then_inc(s["o_copied"], 1)

                def take_logits(b):
                    dve.wait_ge(s["logits_filled"], b + 1)
                    at = bass.ds(ST * b, ST)
                    dve.tensor_copy(logits[:, at, :], pa[1][:, 0:ST * experts].rearrange(
                        "p (t e) -> p t e", t=ST)).then_inc(s["logits_ready"], 1)

                def step(t, par, has_a, has_c):
                    maxes(t, 0, (0, 1))
                    if has_c:
                        normalise(t - 1)
                    maxes(t, 0, (2, 3))
                    if has_a:
                        low_rows(t + 1)
                        projections(t + 1, 1 - par, (0,))
                    maxes(t, 1, (0,))
                    if has_a:
                        projections(t + 1, 1 - par, (1,))
                    maxes(t, 1, (1,))
                    if has_a:
                        projections(t + 1, 1 - par, (2,))
                    maxes(t, 1, (2, 3))
                    if has_c:
                        at_part(t - 1)
                    if has_a:
                        norm_stats(t + 2, par)
                    if has_c:
                        residual(t - 1)
                    outputs(t, (0,))
                    if has_c:
                        norm2_apply(t - 1)
                    outputs(t, (1,))
                    if has_c:
                        take_logits(t - 1)
                    if has_a:
                        norm_apply(t + 2, par)
                        stacks(t + 1, 1 - par, range(4))
                    outputs(t, (2, 3))

                norm_stats(0, 0)
                weight_lo(0, ORDER[0])
                weight_lo(1, ORDER[1])
                norm_apply(0, 0)
                low_rows(0)
                projections(0, 0, range(3))
                stacks(0, 0, range(4))
                norm_stats(1, 1)
                norm_apply(1, 1)
                run(dve, step)
                normalise(B - 1)
                at_part(B - 1)
                residual(B - 1)
                norm2_apply(B - 1)
                take_logits(B - 1)

            @block.tensor
            def _(pe):
                pe.sem_inc(s["at_filled"], 1)

                def turn(bank, x):
                    for k in range(KT):
                        for i in range(ST):
                            last = pe.transpose(bank[:, k * S + i * P:k * S + (i + 1) * P],
                                                x[:, i, k * P:(k + 1) * P], c.ident[:])
                    return last

                def project(bank, hi, lo, n):
                    for i in range(ST):
                        for k in range(KT):
                            at = slice(i * P, (i + 1) * P)
                            last = split_matmul(pe, bank[:, i * D:(i + 1) * D], (hi[:, k, at], lo[:, k, at]),
                                                (w_hi[:, n, k, :], w_lo[:, n, k, :]),
                                                first=k == 0, last=k == KT - 1)
                    return last

                def a1_keys(b):
                    pe.wait_ge(s["xn_ready"], b + 1)
                    turn(pa[0], xn).then_inc(s["xt_filled"], 1)
                    pe.wait_ge(s["w_ready"], 1)
                    pe.wait_ge(s["ctx_lo"], b + 1)
                    project(pa[1], ct_hi, ct_lo, 1).then_inc(s["proj_filled"], 1)

                def a1_queries(b):
                    pe.wait_ge(s["xt_lo"], b + 1)
                    pe.wait_ge(s["w_ready"], 2)
                    project(pa[0], xt_hi, xt_lo, 0).then_inc(s["proj_filled"], 1)

                def a1_values(b):
                    pe.wait_ge(s["w_ready"], 4)
                    pe.wait_ge(s["qkv_ready"], 3 * b + 1)
                    project(pa[1], ct_hi, ct_lo, 2).then_inc(s["proj_filled"], 1)

                def a2(b, t, has_c, which):
                    for n in which:
                        pe.wait_ge(s["parts_lo"], 2 * b + n + 1)
                        if n == 1 and not causal:
                            pe.wait_ge(s["mask_placed"], b + 1)
                        for u in range(4):
                            j = 2 * n + u // 2
                            if j == 0:
                                if t is None:
                                    pe.wait_ge(s["qkv_ready"], 3 * b + 3)
                                elif has_c and u == 1:
                                    pe.wait_ge(s["logits_ready"], t + 1)
                                elif not has_c:
                                    pe.wait_ge(s["qkv_ready"], 3 * b + 3)
                            else:
                                pe.wait_ge(s["stacks_dve"] if u % 2 else s["stacks_act"], 4 * b + j)
                            for v in range(4):
                                hb = 4 * u + v
                                last = pe.transpose(
                                    pa[u % 2][:, v * P:(v + 1) * P],
                                    cols[n][:, hb // 2, hb % 2].bitcast(F32).rearrange("p h a d -> p (h a d)"),
                                    c.ident[:])
                            last.then_inc(s["cols_filled"], 1)

                def scores(b, par, g, ns=range(4)):
                    q, k = q_st[par], k_st[par]
                    for n in ns:
                        for half in range(2):
                            i = 8 * g + 2 * n + half
                            rows = slice(64 * half, 64 * half + 49)
                            at = (4 * g + n) * S
                            if i == 0:
                                wait(pe, s["exp_done"], 16 * b)
                            if i >= 4:
                                pe.wait_ge(s["maxes"], 16 * b + i - 3)
                            bank = ps[i % 4]
                            if causal:
                                pe.matmul(bank[:, 0:P], q[rows, at:at + P], k[rows, at:at + P],
                                          start=True, stop=False)
                                pe.matmul(bank[:, 0:P], c.ident_b[:], c.mask_q[:], start=False, stop=True)
                                pe.matmul(bank[:, P:3 * P], q[rows, at + P:at + S], k[rows, at:at + S],
                                          start=True, stop=False)
                                last = pe.matmul(bank[:, S:3 * P], c.ident_b[:], c.mask_q[:],
                                                 start=False, stop=True)
                            else:
                                for t in range(ST):
                                    last = pe.matmul(bank[:, t * S:(t + 1) * S],
                                                     q[rows, at + t * P:at + (t + 1) * P],
                                                     k[rows, at:at + S], start=True, stop=True)
                            last.then_inc(s["scores_filled"], 1)

                def turn_maxes(b, g, has_c):
                    if has_c:
                        pe.wait_ge(s["ao_ready"], 2 * b)
                    if causal:
                        pe.wait_ge(s["mx_ready"], 2 * b + g + 1)
                    else:
                        pe.wait_ge(s["maxes"], 16 * b + 8 * (g + 1))
                    pe.transpose(po[g][0:16, 0:P], mx[:, g].rearrange("p h k t -> p (h k t)"), c.ident[:]
                                 ).then_inc(s["m_filled"], 1)

                def scores_t(b, par, g):
                    q, k = q_st[par], k_st[par]
                    for j in range(4):
                        half, h8, i = j % 2, 2 * g + j // 2, 4 * g + j
                        rows = slice(64 * half, 64 * half + 50)
                        at = h8 * S
                        if i >= 4:
                            pe.wait_ge(s["exp_done"], 16 * b + i - 3)
                        bank = ps[i % 4]
                        if causal:
                            pe.matmul(bank[:, 0:S], k[rows, at:at + P], q[rows, at:at + S],
                                      start=True, stop=False)
                            pe.matmul(bank[:, 0:P], c.ident_b[:], c.mask_k[:], start=False, stop=True)
                            pe.matmul(bank[:, S:3 * P], k[rows, at + P:at + S], q[rows, at + P:at + S],
                                      start=True, stop=False)
                            last = pe.matmul(bank[:, S:3 * P], c.ident_b[:], c.mask_k[:],
                                             start=False, stop=True)
                        else:
                            for t in range(ST):
                                last = pe.matmul(bank[:, t * S:(t + 1) * S],
                                                 k[rows, at + t * P:at + (t + 1) * P],
                                                 q[rows, at:at + S], start=True, stop=True)
                        last.then_inc(s["scores_t_filled"], 1)

                def values(b, par, g):
                    pe.wait_ge(s["exp_done"], 16 * b + 4 * g + 4)
                    wait(pe, s["o_copied"], 4 * b + g - 1)
                    for t in range(ST):
                        for j in range(4):
                            h = (j % 2) * HB + 2 * g + j // 2
                            q0, w = (P, P) if causal and t else (0, S)
                            last = pe.matmul(po[g % 2][32 * j:32 * j + 32, q0:q0 + w], v_st[par][:, h, t, :],
                                             probs[(4 * g + j) % 8][:, t * S:t * S + w],
                                             start=t == 0, stop=t == ST - 1)
                    last.then_inc(s["pv_done"], 1)

                def c0(b):
                    pe.wait_ge(s["o_copied"], 4 * b + 4)
                    for n in range(ST):
                        for g in range(4):
                            last = pe.transpose(po[n][:, g * P:(g + 1) * P], o_t[:, g, n * P:(n + 1) * P],
                                                c.ident[:])
                        last.then_inc(s["o_filled"], 1)

                def c1a(b, a):
                    if causal:
                        pe.wait_ge(s["ao_in"], 16 * (b + 1))
                    pe.wait_ge(s["ao_ready"], 2 * b + 2)
                    if a is not None:
                        pe.wait_ge(s["qkv_ready"], 3 * a + 3)
                    x = ao_tok if causal else ao[:].rearrange("p (t f) -> p t f", t=ST)
                    turn(pa[1], x).then_inc(s["at_filled"], 1)

                def c1b(b):
                    pe.wait_ge(s["at_lo"], b + 1)
                    project(pa[1], at_hi, at_lo, 3).then_inc(s["out_filled"], 1)

                def c2_turn(b):
                    pe.wait_ge(s["xn2_ready"], b + 1)
                    turn(pa[0], xn2).then_inc(s["xn2_t_filled"], 1)

                def c2_logits(b):
                    pe.wait_ge(s["xn2_t_ready"], b + 1)
                    for i in range(ST):
                        for k in range(KT):
                            last = pe.matmul(pa[1][:, i * experts:(i + 1) * experts],
                                             xn2_t[:, k, i * P:(i + 1) * P], rw[:, k, :],
                                             start=k == 0, stop=k == KT - 1)
                    last.then_inc(s["logits_filled"], 1)

                def step(t, par, has_a, has_c):
                    a = t + 1 if has_a else None
                    if has_c:
                        c0(t - 1)
                    pe.wait_ge(s["stacks_act"], 4 * t + 4)
                    pe.wait_ge(s["stacks_dve"], 4 * t + 4)
                    scores(t, par, 0)
                    if has_a:
                        a1_keys(t + 1)
                    if causal:
                        turn_maxes(t, 0, has_c)
                    scores(t, par, 1, (0,))
                    if not causal:
                        turn_maxes(t, 0, has_c)
                    if has_a:
                        a1_queries(t + 1)
                    scores(t, par, 1, (1,))
                    if has_a:
                        a1_values(t + 1)
                    scores(t, par, 1, (2, 3))
                    if has_c:
                        c1a(t - 1, a)
                    turn_maxes(t, 1, has_c)
                    pe.wait_ge(s["m_placed0"], 32 * (t + 1))
                    scores_t(t, par, 0)
                    if has_c:
                        c1b(t - 1)
                    scores_t(t, par, 1)
                    if causal:
                        pe.wait_ge(s["bounced_in2"], 16 * (t + 1))
                    else:
                        pe.wait_ge(s["qkv_ready"], 3 * t + 3)
                    values(t, par, 0)
                    pe.wait_ge(s["m_placed1"], 32 * (t + 1))
                    scores_t(t, par, 2)
                    if has_c:
                        c2_turn(t - 1)
                    values(t, par, 1)
                    if has_c:
                        c2_logits(t - 1)
                    if has_a:
                        a2(t + 1, t, has_c, (0,))
                    scores_t(t, par, 3)
                    if has_a:
                        a2(t + 1, t, has_c, (1,))
                    values(t, par, 2)
                    values(t, par, 3)

                a1_keys(0)
                a1_queries(0)
                a1_values(0)
                a2(0, None, False, (0, 1))
                run(pe, step)
                c0(B - 1)
                c1a(B - 1, None)
                c1b(B - 1)
                c2_turn(B - 1)
                c2_logits(B - 1)


class Routing:
    BITS = 30

    def __init__(self, nc, c, ctx, layer, logits, experts, sums):
        top2 = layer == 0
        E, cap = experts, SLOTS // experts
        HI = cap // 16
        GE = P // HI
        CT = 4
        BITS = Routing.BITS
        def sb(name, shape, dt=F32):
            return ctx.enter_context(nc.sbuf_tensor(f"{name}_r{layer}", shape, dt))

        def sem(name):
            return nc.alloc_semaphore(name=f"{name}_r{layer}")

        iota_hi_i, iota_hi = sb("iota_hi_i", [P, HI], I32), sb("iota_hi", [P, HI])
        ids_i, ids = sb("ids_i", [P, NT], I32), sb("ids", [P, NT])
        spare_p, spare_i, spare = sb("spare_p", [P, 16], I32), sb("spare_i", [P, 16], I32), sb("spare", [P, 16])
        before, ones = sb("before", [P, P]), sb("ones", [P, P])
        diag = sb("diag", [P, GE])
        rank_e = sb("rank_e", [P, E])
        not_first = sb("not_first", [P, E, NT])
        rb = sb("rb", [P, E])
        lg, tmp, tmp2 = sb("lg", [P, NT, E]), sb("tmp", [P, NT, E]), sb("tmp2", [P, NT, E])
        best, best2, pick = sb("best", [P, NT]), sb("best2", [P, NT]), sb("pick", [P, NT])
        ratio, p1, p2 = sb("ratio", [P, NT]), sb("p1", [P, NT]), sb("p2", [P, NT])
        one1, one2 = sb("one1", [P, NT, E]), sb("one2", [P, NT, E])
        sel, wt = sb("sel", [P, NT, E]), sb("wt", [P, NT, E])
        totals, through = sb("totals", [P, E, NT]), sb("through", [P, E, NT])
        pos, pos_i = sb("pos", [P, NT, E]), sb("pos_i", [P, NT, E], I32)
        hi_i, lo_i = sb("hi_i", [P, NT, E], I32), sb("lo_i", [P, NT, E], I32)
        hi_f, lo_f = sb("hi_f", [P, NT, E]), sb("lo_f", [P, NT, E])
        one_hi = [sb(f"one_hi{i}", [P, CT, E, HI]) for i in range(2)]
        one_lo = [sb(f"one_lo{i}", [P, CT, E, 3, 16]) for i in range(2)]
        spread, lists = sb("spread", [P, GE, 48]), sb("lists", [P, 2, 48])
        idx_f, idx_i = sb("idx_f", [P, 2, 16]), sb("idx_i", [P, 2, 16], I32)
        if not top2:
            thr, cand = sb("thr", [P, E], I32), sb("cand", [P, E], I32)
            part, add = sb("part", [P, E]), sb("add", [P, E], I32)
            need = sb("need", [P, E])

        tables, loaded = sem("tables"), sem("loaded")
        step_done, exp_ready = sem("step_done"), sem("exp_ready")
        counted, count_in = sem("counted"), sem("count_in")
        rows_ready, rows_used = sem("rows_ready"), sem("rows_used")
        lists_out, lists_in = sem("lists_out"), sem("lists_in")
        lists_ready = sem("lists_ready")
        lists_bank = c.banks[1:3]
        counts = {"n": 0}

        dve, pe = nc.vector, nc.tensor

        def link(instruction):
            counts["n"] += 1
            instruction.then_inc(step_done, 1)
            dve.wait_ge(step_done, counts["n"])

        def over_e(x):
            return x.unsqueeze(2).to_broadcast([P, NT, E])

        def over_t(x):
            return x.unsqueeze(1).to_broadcast([P, NT, E])

        gate = c.tgate[:, 2 + layer:3 + layer]

        def vector_start():
            dve.wait_ge(tables, 11 + E)
            dve.tensor_copy(iota_hi[:], iota_hi_i[:])
            dve.tensor_copy(ids[:], ids_i[:])
            link(dve.tensor_scalar(spare_i[:], spare_p[:], cap - 1, None, ALU.bitwise_and))
            link(dve.tensor_scalar(spare[:], spare_i[:], float(N), None, ALU.add))
            if not top2:
                link(dve.tensor_reduce(best[:], logits, AX.X, ALU.max))
                dve.tensor_tensor(lg[:], logits, over_e(best[:]), ALU.subtract).then_inc(exp_ready, 1)
                dve.wait_ge(exp_ready, 2)
                link(dve.tensor_reduce(best2[:], lg[:], AX.X, ALU.add))
                link(dve.reciprocal(best2[:], best2[:]))
                link(dve.tensor_tensor(lg[:], lg[:], over_e(best2[:]), ALU.mult))
                link(dve.memset(thr[:], 0))

        def open_bit(n):
            last = n == BITS
            if not last:
                link(dve.tensor_scalar(cand[:], thr[:], 1 << (BITS - 1 - n), None, ALU.bitwise_or))
            link(dve.tensor_tensor(tmp[:], lg[:], over_t((thr if last else cand)[:].bitcast(F32)),
                                   ALU.is_gt if last else ALU.is_ge))
            dve.tensor_reduce(part[:], tmp[:].rearrange("p t e -> p e t"), AX.X, ALU.add).then_inc(count_in, 1)

        def count_bit(n):
            pe.wait_ge(count_in, n + 1)
            pe.matmul(sums[:, 0:E], ones[:], part[:], start=True, stop=True).then_inc(counted, 1)

        def close_bit(n):
            dve.wait_ge(counted, n + 1)
            link(dve.tensor_scalar(add[:], sums[:, 0:E], float(cap), float(1 << (BITS - 1 - n)),
                                   ALU.is_ge, ALU.mult))
            link(dve.tensor_tensor(thr[:], thr[:], add[:], ALU.bitwise_or))

        def vector_end():
            if top2:
                dve.wait_ge(loaded, 16)
                link(dve.tensor_tensor(lg[:], logits, over_t(rb[:]), ALU.add))

                def first_best(x, top, one):
                    link(dve.tensor_reduce(top[:], x[:], AX.X, ALU.max))
                    link(dve.tensor_tensor(tmp[:], x[:], over_e(top[:]), ALU.is_equal))
                    link(dve.tensor_tensor(tmp[:], tmp[:], over_t(rank_e[:]), ALU.mult))
                    link(dve.tensor_reduce(pick[:], tmp[:], AX.X, ALU.max))
                    link(dve.tensor_tensor(one[:], tmp[:], over_e(pick[:]), ALU.is_equal))

                first_best(lg, best, one1)
                link(dve.scalar_tensor_tensor(tmp2[:], one1[:], -3e38, lg[:], ALU.mult, ALU.add))
                first_best(tmp2, best2, one2)
                dve.tensor_tensor(ratio[:], best2[:], best[:], ALU.subtract).then_inc(exp_ready, 1)
                dve.wait_ge(exp_ready, 2)
                link(dve.tensor_scalar(p1[:], ratio[:], 1.0, None, ALU.add))
                link(dve.reciprocal(p1[:], p1[:]))
                link(dve.tensor_tensor(p2[:], ratio[:], p1[:], ALU.mult))
                link(dve.tensor_tensor(wt[:], one1[:], over_e(p1[:]), ALU.mult))
                link(dve.tensor_tensor(tmp[:], one2[:], over_e(p2[:]), ALU.mult))
                link(dve.tensor_tensor(wt[:], wt[:], tmp[:], ALU.add))
                link(dve.tensor_scalar(wt[:], wt[:], gate, None, ALU.mult))
                dve.tensor_tensor(sel[:], one1[:], one2[:], ALU.add).then_inc(count_in, 1)
            else:
                dve.wait_ge(counted, BITS + 1)
                link(dve.tensor_scalar(need[:], sums[:, 0:E], -1.0, float(cap), ALU.mult, ALU.add))
                link(dve.tensor_copy(sel[:], tmp[:]))
                dve.tensor_tensor(tmp[:], lg[:], over_t(thr[:].bitcast(F32)), ALU.is_equal
                                  ).then_inc(count_in, 1)
                dve.wait_ge(count_in, BITS + 2)
                link(dve.tensor_scalar(wt[:], lg[:], gate, None, ALU.mult))

            def ranks(n):
                dve.wait_ge(counted, n)
                link(dve.tensor_copy(totals[:], c.banks[4][:, 0:NT * E].rearrange("p (t e) -> p e t", e=E)))
                link(dve.tensor_tensor_scan(through[:].rearrange("p e t -> p (e t)"),
                                            not_first[:].rearrange("p e t -> p (e t)"),
                                            totals[:].rearrange("p e t -> p (e t)"), 0.0, ALU.mult, ALU.add))
                link(dve.tensor_tensor(through[:], through[:], totals[:], ALU.subtract))
                link(dve.tensor_tensor(pos[:], c.banks[3][:, 0:NT * E].rearrange("p (t e) -> p t e", e=E),
                                       through[:].rearrange("p e t -> p t e"), ALU.add))

            if top2:
                ranks(1)
                link(dve.tensor_scalar(tmp[:], pos[:], float(cap), None, ALU.is_lt))
                link(dve.tensor_tensor(sel[:], sel[:], tmp[:], ALU.mult))
            else:
                ranks(BITS + 2)
                link(dve.tensor_tensor(pos[:], pos[:], over_t(need[:]), ALU.is_lt))
                link(dve.tensor_tensor(tmp[:], tmp[:], pos[:], ALU.mult))
                dve.tensor_tensor(sel[:], sel[:], tmp[:], ALU.add).then_inc(count_in, 1)
                ranks(BITS + 3)
            link(dve.tensor_scalar(tmp[:], sel[:], -4096.0, 4096.0, ALU.mult, ALU.add))
            link(dve.tensor_tensor(pos_i[:], pos[:], tmp[:], ALU.add))
            link(dve.tensor_scalar(hi_i[:], pos_i[:], 4, None, ALU.logical_shift_right))
            link(dve.tensor_scalar(lo_i[:], pos_i[:], 15, None, ALU.bitwise_and))
            link(dve.tensor_copy(hi_f[:], hi_i[:]))
            link(dve.tensor_copy(lo_f[:], lo_i[:]))
            for q in range(NT // CT):
                at = slice(q * CT, (q + 1) * CT)
                if q >= 2:
                    dve.wait_ge(rows_used, q - 1)
                flat = "p t e -> p (t e)"
                n = CT * E
                rows = one_lo[q % 2][:].rearrange("p t e v l -> p (t e) v l")
                dve.tensor_tensor(one_hi[q % 2][:].rearrange("p t e h -> p (t e) h"),
                                  hi_f[:, at].rearrange(flat).unsqueeze(2).to_broadcast([P, n, HI]),
                                  iota_hi[:].unsqueeze(1).to_broadcast([P, n, HI]), ALU.is_equal)
                link(dve.tensor_tensor(rows[:, :, 2],
                                       lo_f[:, at].rearrange(flat).unsqueeze(2).to_broadcast([P, n, 16]),
                                       iota_hi[:, 0:16].unsqueeze(1).to_broadcast([P, n, 16]), ALU.is_equal))
                dve.tensor_tensor(one_lo[q % 2][:, :, :, 0, :], one_lo[q % 2][:, :, :, 2, :],
                                  ids[:, at].unsqueeze(2).unsqueeze(3).to_broadcast([P, CT, E, 16]), ALU.mult)
                dve.tensor_tensor(rows[:, :, 1], rows[:, :, 2],
                                  wt[:, at].rearrange(flat).unsqueeze(2).to_broadcast([P, n, 16]), ALU.mult
                                  ).then_inc(rows_ready, 1)
            dve.wait_ge(rows_used, NT // CT)
            for g in range(2):
                link(dve.tensor_tensor(spread[:], lists_bank[g][:, 0:GE * 48].rearrange(
                    "p (e v) -> p e v", e=GE), diag[:].unsqueeze(2).to_broadcast([P, GE, 48]), ALU.mult))
                link(dve.tensor_reduce(lists[:, g], spread[:].rearrange("p e v -> p v e"), AX.X, ALU.add))
            link(dve.tensor_scalar(idx_f[:], lists[:, :, 32:48], -1.0, 1.0, ALU.mult, ALU.add))
            link(dve.tensor_tensor(idx_f[:], idx_f[:], spare[:].unsqueeze(1).to_broadcast([P, 2, 16]), ALU.mult))
            link(dve.tensor_tensor(idx_f[:], idx_f[:], lists[:, :, 0:16], ALU.add))
            dve.tensor_copy(idx_i[:], idx_f[:]).then_inc(lists_ready, 1)
            dve.wait_ge(lists_ready, 1)

        def tensor_end():
            flat = "p a b -> p (a b)"
            for n in range(1 if top2 else 2):
                pe.wait_ge(count_in, n + 1 + (0 if top2 else BITS + 1))
                x = (sel if n or top2 else tmp)[:].rearrange(flat)
                pe.matmul(c.banks[3][:, 0:NT * E], before[:], x, start=True, stop=True)
                pe.matmul(c.banks[4][:, 0:NT * E], ones[:], x, start=True, stop=True).then_inc(counted, 1)
            for q in range(NT // CT):
                pe.wait_ge(rows_ready, q + 1)
                for g in range(2):
                    for t in range(CT):
                        last = pe.matmul(lists_bank[g][:, 0:GE * 48],
                                         one_hi[q % 2][:, t, g * GE:(g + 1) * GE].rearrange(flat),
                                         one_lo[q % 2][:, t, g * GE:(g + 1) * GE].rearrange(
                                             "p e v l -> p (e v l)"),
                                         start=q == 0 and t == 0, stop=q == NT // CT - 1 and t == CT - 1)
                last.then_inc(rows_used, 1)

        def tables_by(pool):
            pool.iota(iota_hi_i[:], [[1, HI]], base=0, channel_multiplier=0).then_inc(tables, 1)
            pool.iota(ids_i[:], [[P, NT]], base=0, channel_multiplier=1).then_inc(tables, 1)
            pool.iota(spare_p[:], [[1, 16]], base=0, channel_multiplier=16).then_inc(tables, 1)
            pool.memset(before[:], 1.0).then_inc(tables, 1)
            pool.memset(ones[:], 1.0).then_inc(tables, 1)
            pool.memset(diag[:], 1.0).then_inc(tables, 1)
            for e in range(E):
                pool.memset(rank_e[:, e:e + 1], float(E - e)).then_inc(tables, 1)
            pool.memset(not_first[:], 1.0).then_inc(tables, 1)
            pool.wait_ge(tables, 7 + E)
            pool.memset(not_first[:, :, 0:1], 0.0).then_inc(tables, 1)
            pool.affine_select(out=before[:], in_=before[:], compare_op=ALU.is_gt, fill=0.0, base=0,
                               pattern=[[1, P]], channel_multiplier=-1).then_inc(tables, 1)
            pool.affine_select(out=diag[:], in_=diag[:], compare_op=ALU.is_ge, fill=0.0, base=0,
                               pattern=[[-HI, GE]], channel_multiplier=1).then_inc(tables, 1)
            pool.wait_ge(tables, 10 + E)
            pool.affine_select(out=diag[:], in_=diag[:], compare_op=ALU.is_ge, fill=0.0, base=HI - 1,
                               pattern=[[HI, GE]], channel_multiplier=-1).then_inc(tables, 1)
            pool.wait_ge(tables, 11 + E)

        def lists_by(sp):
            sp.wait_ge(lists_ready, 1)
            sp.dma_start(c.idx_dram.rearrange("(g p l) -> p g l", g=2, l=16), idx_i[:]).then_inc(lists_out, 16)
            sp.dma_start(c.wt_dram.rearrange("(g p l) -> p g l", g=2, l=16), lists[:, :, 16:32]
                         ).then_inc(lists_out, 16)
            sp.wait_ge(lists_out, 32)
            with nc.allow_non_contiguous_dma(reason="4096 words of lists, once"):
                sp.dma_start(c.idx[:], c.idx_dram.rearrange("(t p) -> p t", p=P)).then_inc(lists_in, 16)
                sp.dma_start(c.wt[:], c.wt_dram.rearrange("(t p) -> p t", p=P)).then_inc(lists_in, 16)
            sp.wait_ge(lists_in, 32)

        def exp_by(act):
            act.wait_ge(exp_ready, 1)
            if top2:
                act.activation(ratio[:], ratio[:], ACT.Exp).then_inc(exp_ready, 1)
            else:
                act.activation(lg[:], lg[:], ACT.Exp).then_inc(exp_ready, 1)

        self.vector_start, self.vector_end, self.tensor_end = vector_start, vector_end, tensor_end
        self.open_bit, self.count_bit, self.close_bit = open_bit, count_bit, close_bit
        self.tables_by, self.lists_by, self.exp_by = tables_by, lists_by, exp_by
        self.tables, self.tables_total = tables, 11 + E
        self.bias, self.loaded, self.lists_in = rb, loaded, lists_in


def experts(nc, c, kind, E, T, CH, weights, x_rows, dst, base=None, routed=None, ahead=None):
    shared = kind == "shared"
    M = 4 * CH
    U = M + 1
    TW = T * P
    W = 3072
    PIECE = W // 4
    YB = 2 if kind == "choice" else 1
    gate_fn = ACT.Silu if kind == "top2" else ACT.Gelu
    with ExitStack() as ctx:
        def sb(name, shape, dt=F32):
            return ctx.enter_context(nc.sbuf_tensor(f"{name}_{kind}", shape, dt))

        def sem(name):
            return nc.alloc_semaphore(name=f"{name}_{kind}")

        wn = 1 if shared else 2
        w_raw = None if kind == "choice" else [sb(f"w_raw{i}", [P, W]) for i in range(wn)]
        WB = 1 if shared else 2 * CH
        first = 1 if kind == "choice" else 0
        w_hi = [None] * first + [sb(f"w_hi{i}", [P, W], F32R) for i in range(first, WB)]
        w_lo = [None] * first + [sb(f"w_lo{i}", [P, W], F32R) for i in range(first, WB)]
        xg = [sb(f"xg{i}", [P, T, D]) for i in range(2)]
        x_hi = [sb(f"x_hi{i}", [P, KT, TW], F32R) for i in range(2)]
        x_lo = [sb(f"x_lo{i}", [P, KT, TW], F32R) for i in range(2)]
        gated = [sb(f"gated{i}", [P, TW]) for i in range(2)]
        h = [sb(f"h{i}", [P, TW]) for i in range(2)]
        h_hi = [sb(f"h_hi{i}", [P, TW], F32R) for i in range(2)]
        h_lo = [sb(f"h_lo{i}", [P, TW], F32R) for i in range(2)]
        ys = [sb(f"ys{i}", [P, T, D]) for i in range(2)]
        if shared:
            res = [sb(f"res{i}", [P, T, D]) for i in range(2)]
        else:
            from_rows = [sb(f"from_rows{i}", [P, T], I32) for i in range(2)]
            to_rows = [sb(f"to_rows{i}", [P, T], I32) for i in range(2)]
            wt = [sb(f"wt{i}", [P, T]) for i in range(2)]

        s = Semaphores(sem)
        routing = Routing(nc, c, ctx, *routed, c.banks[6]) if routed else None
        if kind == "choice":
            w_raw, w_hi[0], w_lo[0] = ahead.w_raw, ahead.w_hi, ahead.w_lo
            s.update(w_loaded=ahead.loaded, w_hi=ahead.hi_ready, w_lo=ahead.lo_ready)
        y_credit = YB * T

        def use_ab(e, m, left):
            return e * U + 1 + m + (1 if m == M - 1 and left else 0)

        def pair_of(par, m, left):
            return c.banks[2 * (use_ab(par, m, left) % 2):][:2]

        def turn_pair(par):
            return (par * U + M) % 2

        def a_w(w, k, m):
            return w[:, k * 512 + m * P:k * 512 + (m + 1) * P]

        def b_w(w, k, m):
            return w[:, 1024 + k * 512 + m * P:1024 + k * 512 + (m + 1) * P]

        def o_w(w, m):
            return w[:, 2048 + m * D:2048 + (m + 1) * D]

        def chunk_par(par, cc):
            return (par * CH + cc) % WB

        def piece_of(e, par, m, left):
            if m // 4 == CH - 1 and not left:
                return None
            return e * CH + m // 4 + 1, chunk_par(par, m // 4 + 1), m % 4

        with nc.Block() as block:

            @block.sync
            def _(sp):
                def load_w(chunk, buf):
                    sp.dma_start(w_raw[buf][:], weights[bass.ds(chunk, 1)].rearrange("o p w -> p (o w)")
                                 ).then_inc(s["w_loaded"], 16)

                if kind == "top2":
                    sp.dma_start(routing.bias[:], bcast(c.router_b, P)).then_inc(routing.loaded, 16)
                if kind != "choice":
                    load_w(0, 0)
                if shared:
                    for e in range(E):
                        par = e % 2
                        if e >= 2:
                            sp.wait_ge(s["x_turned"], e)
                        sp.dma_start(xg[par][:], c.row_group(x_rows, e, T)).then_inc(s[f"rows_in{par}"], 16)
                        if e >= 2:
                            sp.wait_ge(s["y_read"], y_credit + T * (e - 1))
                            sp.dma_start(c.row_group(dst, e - 2, T), ys[par][:]).then_inc(s[f"stored{par}"], 16)
                        sp.dma_start(res[par][:], c.row_group(base, e, T)).then_inc(s[f"res_in{par}"], 16)
                    for n in range(2):
                        if n:
                            sp.wait_ge(ahead.loaded, 16)
                        sp.dma_start(ahead.w_raw[n][:], ahead.weights[n]).then_inc(ahead.loaded, 16)
                    for e in range(E - 2, E):
                        sp.wait_ge(s["y_read"], y_credit + T * (e + 1))
                        sp.dma_start(c.row_group(dst, e, T), ys[e % 2][:]).then_inc(s[f"stored{e % 2}"], 16)
                    sp.wait_ge(s["stored0"], 16 * (E // 2))
                    sp.wait_ge(s["stored1"], 16 * (E // 2))
                    routing.lists_by(sp)
                    sp.wait_ge(ahead.loaded, 32)
                else:
                    if routing:
                        sp.wait_ge(s["w_loaded"], 16)
                        load_w(1, 1)
                        routing.lists_by(sp)

                    def refill(n, buf):
                        sp.wait_ge(s["w_lo"], 4 * (n + 1))
                        c.settle(sp)
                        sp.wait_ge(s["w_loaded"], 16 * (n + 2))
                        c.settle(sp)
                        load_w(n + 2, buf)

                    with sp.Fori(0, E // 2 - 1) as i:
                        for j in range(2 * CH):
                            refill(2 * CH * i + j, j % 2)
                    for n in range((E - 2) * CH, E * CH - 2):
                        refill(n, n % 2)
                    sp.wait_ge(s["w_loaded"], 16 * E * CH)

            @block.gpsimd
            def _(pool):
                if shared:
                    routing.tables_by(pool)
                    return

                def gather(e, par):
                    pool.tensor_copy(from_rows[par][:], c.idx[:, bass.ds(e * T, T)]).then_inc(s["from_copied"], 1)
                    pool.wait_ge(s["from_copied"], e + 1)
                    c.settle(pool)
                    for t in range(T):
                        pool.indirect_dma_start(
                            out=xg[par][:, t, :], out_offset=None, in_=x_rows,
                            in_offset=bass.IndirectOffsetOnAxis(
                                ap=from_rows[par][:, t:t + 1].bitcast(U32), axis=0)
                        ).then_inc(s[f"rows_in{par}"], 16)

                if routing:
                    routing.tables_by(pool)
                    pool.wait_ge(routing.lists_in, 32)
                pool.sem_inc(s["ys_free"], 2)
                gather(0, 0)
                gather(1, 1)

                def expert(e, par, k, left):
                    pool.tensor_copy(wt[par][:], c.wt[:, bass.ds(e * T, T)]).then_inc(s["wt_copied"], 1)
                    pool.tensor_copy(to_rows[par][:], c.idx[:, bass.ds(e * T, T)]).then_inc(s["to_copied"], 1)
                    if left >= 2:
                        pool.wait_ge(s["x_turned"], e + 2)
                        gather(e + 2, par)
                    pool.wait_ge(s["to_copied"], e + 1)
                    pool.wait_ge(s["y_read"], y_credit + T * (e + 1))
                    c.settle(pool)
                    for t in range(T):
                        pool.indirect_dma_start(
                            out=dst, in_=ys[par][:, t, :], in_offset=None,
                            out_offset=bass.IndirectOffsetOnAxis(
                                ap=to_rows[par][:, t:t + 1].bitcast(U32), axis=0),
                            compute_op=ALU.add).then_inc(s["added"], 16)
                    pool.wait_ge(s["added"], 16 * T * (e + 1))
                    pool.sem_inc(s["ys_free"], 1)

                c.over_experts(pool, E, expert, shared)

            @block.scalar
            def _(act):
                def hi_piece(n, buf, j):
                    at = slice(j * PIECE, (j + 1) * PIECE)
                    act.wait_ge(s["w_loaded"], 16 * (n + 1))
                    if CH == 1:
                        wait(act, s["y_done"], 4 * n - 2)
                    act.copy(w_hi[buf][:, at], w_raw[buf % wn][:, at]).then_inc(s["w_hi"], 1)

                def x_part(n, par, pair):
                    act.wait_ge(s["x_turned"], n + 2)
                    if T == 4:
                        for k in range(KT):
                            last = act.copy(x_hi[par][:, k], c.banks[2 * pair + k][:])
                    else:
                        last = act.copy(x_hi[par][:].rearrange("p k t -> p (k t)"), c.banks[2 * pair][:])
                    last.then_inc(s["x_hi"], 1)

                if routing:
                    routing.exp_by(act)
                for j in range(3):
                    if kind != "choice":
                        hi_piece(0, 0, j)
                x_part(0, 0, 0)
                if kind != "choice":
                    hi_piece(0, 0, 3)

                def expert(e, par, k, left):
                    for m in range(M):
                        g = e * M + m
                        if m == M - 1 and left:
                            x_part(e + 1, 1 - par, turn_pair(par))
                        act.wait_ge(s["ab_filled"], g + 1)
                        act.activation(gated[m % 2][:], pair_of(par, m, left)[1][:, 0:TW], gate_fn
                                       ).then_inc(s["gate_done"], 1)
                        piece = None if shared else piece_of(e, par, m, left)
                        if piece and (m % 4 or CH == 2):
                            hi_piece(*piece)
                        act.wait_ge(s["pair_read"], use_ab(e, m, left) + 2)
                        act.wait_ge(s["y_done"], g + 1)
                        act.copy(h_hi[m % 2][:], h[m % 2][:]).then_inc(s["h_hi"], 1)
                        if piece and not (m % 4 or CH == 2):
                            hi_piece(*piece)

                c.over_experts(act, E, expert, shared)
                if shared:
                    act.wait_ge(ahead.loaded, 32)
                    for j in range(4):
                        at = slice(j * PIECE, (j + 1) * PIECE)
                        act.copy(ahead.w_hi[:, at], ahead.w_raw[0][:, at]).then_inc(ahead.hi_ready, 1)

            @block.vector
            def _(dve):
                def lo_piece(n, buf, j):
                    at = slice(j * PIECE, (j + 1) * PIECE)
                    dve.wait_ge(s["w_hi"], 4 * n + j + 1)
                    dve.tensor_tensor(w_lo[buf][:, at], w_raw[buf % wn][:, at], w_hi[buf][:, at].bitcast(F32),
                                      ALU.subtract).then_inc(s["w_lo"], 1)

                def x_part(n, par, pair):
                    dve.wait_ge(s["x_hi"], n + 1)
                    if T == 4:
                        for k in range(KT):
                            last = dve.tensor_tensor(x_lo[par][:, k], c.banks[2 * pair + k][:],
                                                     x_hi[par][:, k].bitcast(F32), ALU.subtract)
                    else:
                        flat = "p k t -> p (k t)"
                        last = dve.tensor_tensor(x_lo[par][:].rearrange(flat), c.banks[2 * pair][:],
                                                 x_hi[par][:].bitcast(F32).rearrange(flat), ALU.subtract)
                    last.then_inc(s["pair_read"], 1)

                dve.sem_inc(s["y_read"], y_credit)
                dve.sem_inc(s["pair_read"], 1)
                if routing:
                    routing.vector_start()
                if shared:
                    routing.open_bit(0)
                elif routing:
                    routing.vector_end()
                for j in range(3):
                    if kind != "choice":
                        lo_piece(0, 0, j)
                x_part(0, 0, 0)
                if kind != "choice":
                    lo_piece(0, 0, 3)

                def hidden(e, par, m, left):
                    g = e * M + m
                    dve.wait_ge(s["gate_done"], g + 1)
                    dve.tensor_tensor(h[m % 2][:], pair_of(par, m, left)[0][:, 0:TW], gated[m % 2][:], ALU.mult
                                      ).then_inc(s["pair_read"], 1)
                    piece = None if shared else piece_of(e, par, m, left)
                    if piece and (m % 4 or CH == 2):
                        lo_piece(*piece)
                    dve.wait_ge(s["h_hi"], g + 1)
                    dve.tensor_tensor(h_lo[m % 2][:], h[m % 2][:], h_hi[m % 2][:].bitcast(F32), ALU.subtract
                                      ).then_inc(s["h_lo"], 1)
                    if piece and not (m % 4 or CH == 2):
                        lo_piece(*piece)

                def outputs(e, par, k):
                    dve.wait_ge(s["y_done"], (e + 1) * M + 2)
                    if shared:
                        dve.wait_ge(s[f"res_in{par}"], 16 * (k + 1))
                        wait(dve, s[f"stored{par}"], 16 * k)
                    else:
                        dve.wait_ge(s["ys_free"], e + 1)
                        dve.wait_ge(s["wt_copied"], e + 1)
                    for t in range(T):
                        bank = c.banks[4 + (par % YB) * T + t][:, 0:D]
                        if shared:
                            dve.scalar_tensor_tensor(ys[par][:, t, :], bank, c.tgate[:, 3:4], res[par][:, t, :],
                                                     ALU.mult, ALU.add).then_inc(s["y_read"], 1)
                        else:
                            dve.tensor_scalar(ys[par][:, t, :], bank, wt[par][:, t:t + 1], None, ALU.mult
                                              ).then_inc(s["y_read"], 1)

                def expert(e, par, k, left):
                    for m in range(1, M):
                        if m == M - 1 and left:
                            x_part(e + 1, 1 - par, turn_pair(par))
                        hidden(e, par, m, left)
                    if left:
                        hidden(e + 1, 1 - par, 0, left - 1)
                    outputs(e, par, k)

                def shared_expert(e, par, k, left):
                    for m in range(M):
                        g = e * M + m
                        if g < Routing.BITS:
                            routing.close_bit(g)
                            routing.open_bit(g + 1)
                        if m == 1 and e:
                            outputs(e - 1, 1 - par, (e - 1) // 2)
                        if m == M - 1 and left:
                            x_part(e + 1, 1 - par, turn_pair(par))
                        hidden(e, par, m, left)
                    if not left:
                        outputs(e, par, k)

                if not shared:
                    hidden(0, 0, 0, 1)
                c.over_experts(dve, E, shared_expert if shared else expert, shared)
                if shared:
                    routing.vector_end()
                    for j in range(4):
                        at = slice(j * PIECE, (j + 1) * PIECE)
                        dve.wait_ge(ahead.hi_ready, j + 1)
                        dve.tensor_tensor(ahead.w_lo[:, at], ahead.w_raw[0][:, at],
                                          ahead.w_hi[:, at].bitcast(F32), ALU.subtract
                                          ).then_inc(ahead.lo_ready, 1)

            @block.tensor
            def _(pe):
                pe.sem_inc(s["y_done"], 2)
                pe.sem_inc(s["x_turned"], 1)

                def turn_rows(par, pair):
                    for k in range(KT):
                        for t in range(T):
                            if T == 4:
                                out = c.banks[2 * pair + k][:, t * P:(t + 1) * P]
                            else:
                                out = c.banks[2 * pair][:, k * TW + t * P:k * TW + (t + 1) * P]
                            last = pe.transpose(out, xg[par][:, t, k * P:(k + 1) * P], c.ident[:])
                    last.then_inc(s["x_turned"], 1)

                rows_count = 16 if shared else 16 * T

                def ab(e, par, m, left):
                    buf = chunk_par(par, m // 4)
                    if m % 4 == 0:
                        pe.wait_ge(s["w_lo"], 3 if shared else 4 * (e * CH + m // 4) + 3)
                    pe.wait_ge(s["pair_read"], use_ab(e, m, left))
                    for bank, part in zip(pair_of(par, m, left), (a_w, b_w)):
                        if shared and part is b_w and e * M + m <= Routing.BITS:
                            routing.count_bit(e * M + m)
                        for k in range(KT):
                            last = split_matmul(pe, bank[:, 0:TW],
                                                (part(w_hi[buf], k, m % 4), part(w_lo[buf], k, m % 4)),
                                                (x_hi[par][:, k], x_lo[par][:, k]), first=k == 0, last=k == KT - 1)
                    last.then_inc(s["ab_filled"], 1)

                def y(e, par, m):
                    buf = chunk_par(par, m // 4)
                    pe.wait_ge(s["h_lo"], e * M + m + 1)
                    if m % 4 == 0:
                        pe.wait_ge(s["w_lo"], 4 if shared else 4 * (e * CH + m // 4) + 4)
                    for t in range(T):
                        if m == 0:
                            pe.wait_ge(s["y_read"], T * e + t + 1)
                        at = slice(t * P, (t + 1) * P)
                        last = split_matmul(pe, c.banks[4 + (par % YB) * T + t][:, 0:D],
                                            (h_hi[m % 2][:, at], h_lo[m % 2][:, at]),
                                            (o_w(w_hi[buf], m % 4), o_w(w_lo[buf], m % 4)),
                                            first=m == 0, last=m == M - 1)
                    last.then_inc(s["y_done"], 1)

                if routing:
                    pe.wait_ge(routing.tables, routing.tables_total)
                    if not shared:
                        routing.tensor_end()
                pe.wait_ge(s["rows_in0"], rows_count)
                turn_rows(0, 0)
                pe.wait_ge(s["pair_read"], 2)
                ab(0, 0, 0, 1)
                ab(0, 0, 1, 1)

                def expert(e, par, k, left):
                    for m in range(2, M):
                        if m == M - 1 and left:
                            pe.wait_ge(s[f"rows_in{1 - par}"], rows_count * (k + 1 + par))
                            pe.wait_ge(s["pair_read"], e * U + M)
                            turn_rows(1 - par, turn_pair(par))
                        ab(e, par, m, left)
                        y(e, par, m - 2)
                    for m in range(2):
                        if left:
                            ab(e + 1, 1 - par, m, left - 1)
                        y(e, par, M - 2 + m)

                c.over_experts(pe, E, expert, shared)
                if shared:
                    routing.tensor_end()


class Ahead:

    def __init__(self, nc, ctx, weights):
        width = weights.shape[-1]
        self.weights = weights
        self.w_raw = [ctx.enter_context(nc.sbuf_tensor(f"ahead_raw{i}", [P, width], F32)) for i in range(2)]
        self.w_hi = ctx.enter_context(nc.sbuf_tensor("ahead_hi", [P, width], F32R))
        self.w_lo = ctx.enter_context(nc.sbuf_tensor("ahead_lo", [P, width], F32R))
        self.loaded = nc.alloc_semaphore(name="ahead_loaded")
        self.hi_ready = nc.alloc_semaphore(name="ahead_hi_ready")
        self.lo_ready = nc.alloc_semaphore(name="ahead_lo_ready")


class Shared:

    def rows(self, x, b):
        return x[bass.ds(b * S, S), :].rearrange("(t p) f -> p t f", p=P)

    def ctx_rows(self, b):
        return self.ctx_t[bass.ds(b, 1)].rearrange("o p k t -> p (o k) t")

    def tokens(self, x):
        return x.rearrange("(t p) f -> p t f", p=P)

    def row_group(self, x, n, tiles):
        return x[n * tiles * P:(n + 1) * tiles * P, :].rearrange("(t p) f -> p t f", p=P)

    def settle(self, eng):
        eng.sem_inc(self.passed, 1)

    def over_experts(self, eng, count, expert, unrolled):
        if unrolled:
            for e in range(count):
                expert(e, e % 2, e // 2, min(2, count - 1 - e))
            return
        with eng.Fori(0, count // 2 - 1) as i:
            expert(2 * i, 0, i, 2)
            expert(2 * i + 1, 1, i, 2)
        expert(count - 2, 0, count // 2 - 1, 1)
        expert(count - 1, 1, count // 2 - 1, 0)

    def by_position(self, x):
        return x.rearrange("(a t) (u d) -> (t u) a d", a=H * ST, d=HD)


def build(nc, ins, out):
    c = Shared()
    with ExitStack() as ctx:
        c.sems = ctx

        def sb(name, shape, dt=F32):
            return ctx.enter_context(nc.sbuf_tensor(name, shape, dt))

        def sem(name):
            return ctx.enter_context(nc.semaphore(name))

        def dram(name, shape, dt=F32):
            return nc.dram_tensor(name, shape, dt, kind="Internal").ap()

        c.banks = [ctx.enter_context(nc.psum_tensor(f"bank{i}", [P, 512], F32)) for i in range(8)]
        c.ident, c.ident_b = sb("ident", [P, P]), sb("ident_b", [P, P], BF16)
        c.mask_q, c.mask_k = sb("mask_q", [P, P], BF16), sb("mask_k", [P, P], BF16)
        c.minus_half = sb("minus_half", [P, 2])
        c.gates, c.tgate = sb("gates", [P, 4]), sb("tgate", [P, 4])
        c.logits = sb("logits", [P, NT, 16])
        c.passed = sem("passed")
        c.gates_loaded, c.gates_ready = sem("gates_loaded"), sem("gates_ready")
        c.const_set, c.ident_b_ready = sem("const_set"), sem("ident_b_ready")
        c.g_xattn, c.g_ffn = ins["g_xattn"], ins["g_ffn"]
        c.ctx_t = ins["ctx_t"]
        c.router_b = ins["L0_ffn_router_b"]
        c.qkv_dram = [dram(f"{n}_dram", [S, D]) for n in ("q", "k", "v")]
        c.ao_dram = dram("ao_dram", [S, D])
        c.idx_dram, c.wt_dram = dram("idx_dram", [SLOTS], I32), dram("wt_dram", [SLOTS])
        c.idx, c.wt = sb("idx", [P, SLOT_TILES], I32), sb("wt", [P, SLOT_TILES])
        c.zeros_set, c.spare_zeroed = sem("zeros_set"), sem("spare_zeroed")
        x0, xn0 = dram("x0", [N + SPARE, D]), dram("xn0", [N + SPARE, D])
        x1, xn1 = dram("x1", [N, D]), dram("xn1", [N, D])
        c.with_spare = [x0, xn0]

        c.zeros = sb("zeros", [P, SPARE // P * D])
        constants(nc, c)
        layer_0 = nc.snapshot_sems()
        attention(nc, c, 0, ins["x"], [ins[f"L0_xattn_{w}"] for w in ("Wq", "Wk", "Wv", "Wp")],
                  [ins[f"L0_xattn_{w}"] for w in ("bq", "bk", "bv", "bp")], None,
                  ins["L0_ffn_router_w"], c.logits[:, :, 0:8], 8, x0, xn0)
        experts(nc, c, "top2", 8, 4, 1, ins["L0_ffn"], xn0, x0, routed=(0, c.logits[:, :, 0:8], 8))
        nc.clear_and_free_semaphores(nc.allocated_since(layer_0))
        nc.all_engine_barrier()
        attention(nc, c, 1, x0, [ins[f"L1_xattn_W_{w}"] for w in "QKVO"],
                  [ins[f"L1_xattn_b_{w}"] for w in "QKVO"], ins["mask"],
                  ins["L1_ffn_gate_w"], c.logits[:, :, 0:16], 16, x1, xn1)
        with ExitStack() as both:
            ahead = Ahead(nc, both, ins["L1_ffn"])
            experts(nc, c, "shared", 8, 2, 1, ins["L1_shared"], xn1, out, x1, (1, c.logits[:, :, 0:16], 16), ahead)
            experts(nc, c, "choice", 16, 2, 2, ins["L1_ffn"], xn1, out, ahead=ahead)


def kernel(**inputs):
    import numpy as np
    import concourse.bacc as bacc
    from concourse.bass_utils import run_bass_kernel_spmd

    def by_row_tile(w):
        return w.reshape(-1, P, w.shape[-1]).transpose(1, 0, 2)

    def chunks(up, gate, down):
        e, _, hid = up.shape
        n = hid // 512
        parts = [w.reshape(e, KT, P, n, 512).transpose(0, 3, 2, 1, 4).reshape(e * n, P, -1) for w in (up, gate)]
        parts.append(down.reshape(e, n, 4, P, D).transpose(0, 1, 3, 2, 4).reshape(e * n, P, -1))
        return np.concatenate(parts, axis=2)

    a = {name: np.asarray(value) for name, value in inputs.items()}
    arrays = {
        "x": a["x"].reshape(N, D),
        "ctx_t": a["ctx_1024"].transpose(0, 2, 1).reshape(B, KT, P, S).transpose(0, 2, 1, 3),
        "mask": a["mask_BxS2_bk0"].reshape(B, ST, P).transpose(2, 0, 1),
        "g_xattn": a["g_xattn"][None], "g_ffn": a["g_ffn"][None],
        "L0_ffn_router_w": by_row_tile(a["L0_ffn_router_w"].T),
        "L0_ffn_router_b": a["L0_ffn_router_b"][None],
        "L1_ffn_gate_w": by_row_tile(a["L1_ffn_gate_w"].T),
        "L0_ffn": chunks(a["L0_ffn_W"], a["L0_ffn_V"], a["L0_ffn_W_out"]),
        "L1_ffn": chunks(a["L1_ffn_Wu"].transpose(0, 2, 1), a["L1_ffn_Wg"].transpose(0, 2, 1),
                         a["L1_ffn_Wd"].transpose(0, 2, 1)),
        "L1_shared": chunks(a["L1_ffn_Su"].T[None], a["L1_ffn_Sg"].T[None], a["L1_ffn_Sd"].T[None]),
    }
    for w in ("Wq", "Wk", "Wv", "Wp"):
        arrays[f"L0_xattn_{w}"] = by_row_tile(a[f"L0_xattn_{w}"].T)
        arrays[f"L0_xattn_b{w[1]}"] = a[f"L0_xattn_b{w[1]}"][None]
    for w in "QKVO":
        arrays[f"L1_xattn_W_{w}"] = by_row_tile(a[f"L1_xattn_W_{w}"])
        arrays[f"L1_xattn_b_{w}"] = a[f"L1_xattn_b_{w}"][None]
    arrays = {name: np.ascontiguousarray(value) for name, value in arrays.items()}

    nc = bacc.Bacc("TRN2", target_bir_lowering=False, num_devices=1)
    ins = {name: nc.dram_tensor(name, value.shape, mybir.dt.from_np(value.dtype), kind="ExternalInput").ap()
           for name, value in arrays.items()}
    out = nc.dram_tensor("out", [N, D], F32, kind="ExternalOutput").ap()
    build(nc, ins, out)
    result = run_bass_kernel_spmd(nc, [arrays], core_ids=[0])
    return result.results[0]["out"].reshape(B, S, D)
```
